# Optimizing a Trainium2 kernel written in Bass

```python
import numpy as np
import jax
import jax.numpy as jnp

def _softmax(x, axis=-1):
    return jax.nn.softmax(x, axis=axis)

def _gelu(x):
    return jax.nn.gelu(x, approximate=True)

def _silu(x):
    return jax.nn.silu(x)

def _sigmoid(x):
    return jax.nn.sigmoid(x)

def _layernorm(x, axis=-1, eps=1e-05):
    m = jnp.mean(x, axis=axis, keepdims=True)
    v = jnp.var(x, axis=axis, keepdims=True)
    return (x - m) / jnp.sqrt(v + eps)

def _scatter_add(tgt, idx, src, axis=0):
    return tgt.at[idx].add(src)

def _segment_sum(src, seg, n):
    return jax.ops.segment_sum(src, seg, n)
kernel_name = 'mk_gnn_preln_d4_gnn_r64_3474c1'

def setup_inputs(seed: int=0):
    np.random.seed(seed)
    _w = jnp.asarray

    def _rec_inputs():
        import jax
        import jax.numpy as jnp
        _gk = jax.random.key(seed)
        x = -0.000202 + 1 * jax.random.normal(jax.random.fold_in(_gk, 1), (50000, 128), jnp.float32)
        src = jax.random.randint(jax.random.fold_in(_gk, 2), (25000,), 0, 50000, jnp.int32)
        dst = jnp.minimum((50000 * jax.random.uniform(jax.random.fold_in(_gk, 3), (25000,)) ** 2.0).astype(jnp.int32), 49999)
        _o = jnp.argsort(dst, stable=True)
        src = src[_o]
        dst = dst[_o]
        edge_attr_50 = jax.random.uniform(jax.random.fold_in(_gk, 12), (25000, 50), jnp.float32, 0.0, 1)
        edge_weight = jax.random.uniform(jax.random.fold_in(_gk, 14), (25000,), jnp.float32, 0.0, 5.99999)
        return (x, src, dst, edge_attr_50, edge_weight)
    x, src, dst, edge_attr_50, edge_weight = _rec_inputs()

    def _L0_gnn_setup():
        import jax, jax.numpy as jnp
        import numpy as np
        N, E, EMB, HID, H = (50000, 12500, 128, 512, 8)
        D = EMB // H
        EPS = 1e-05

        def _linear_params(key, fan_in, fan_out):
            s = 1.0 / np.sqrt(fan_in)
            k1, k2 = jax.random.split(key)
            w = jax.random.uniform(k1, (fan_in, fan_out), minval=-s, maxval=s, dtype=jnp.float32)
            b = jax.random.uniform(k2, (fan_out,), minval=-s, maxval=s, dtype=jnp.float32)
            return (w, b)

        def _batchnorm(x, g, b):
            mu = x.mean(axis=0)
            var = ((x - mu) ** 2).mean(axis=0)
            return g * (x - mu) * jax.lax.rsqrt(var + EPS) + b

        def _forward(x, wq, bq, wk, bk, wv, bv, wo, bo, w1, b1, w2, b2, g1, be1, g2, be2, A, B):
            n = x.shape[0]
            q = (x @ wq + bq).reshape(n, H, D)
            k = (x @ wk + bk).reshape(n, H, D)
            v = (x @ wv + bv).reshape(n, H, D)
            score = jnp.einsum('ehd,egd->ehg', q[A], k[B])
            ssum = jax.ops.segment_sum(score, A, num_segments=n)
            cnt = jax.ops.segment_sum(jnp.ones((A.shape[0],), score.dtype), A, num_segments=n)
            score = ssum / jnp.maximum(cnt, 1.0)[:, None, None]
            score = jax.nn.softmax(score, axis=-1)
            out = jnp.einsum('ehg,egd->ehd', score, v).reshape(n, EMB)
            out = out @ wo + bo
            x = _batchnorm(out + x, g1, be1)
            h = jax.nn.gelu(x @ w1 + b1, approximate=False)
            h = h @ w2 + b2
            x = _batchnorm(h + x, g2, be2)
            return x
        key = jax.random.key(seed)
        ks = jax.random.split(key, 9)
        x = jax.random.normal(ks[0], (N, EMB), dtype=jnp.float32)
        edge_index = jax.random.randint(ks[1], (2, E), 0, N, dtype=jnp.int32)
        batch = jnp.zeros((N,), dtype=jnp.int32)
        wq, bq = _linear_params(ks[2], EMB, EMB)
        wk, bk = _linear_params(ks[3], EMB, EMB)
        wv, bv = _linear_params(ks[4], EMB, EMB)
        wo, bo = _linear_params(ks[5], EMB, EMB)
        w1, b1 = _linear_params(ks[6], EMB, HID)
        w2, b2 = _linear_params(ks[7], HID, EMB)
        g1 = jnp.ones((EMB,), jnp.float32)
        be1 = jnp.zeros((EMB,), jnp.float32)
        g2 = jnp.ones((EMB,), jnp.float32)
        be2 = jnp.zeros((EMB,), jnp.float32)
        return {'x': x, 'wq': wq, 'bq': bq, 'wk': wk, 'bk': bk, 'wv': wv, 'bv': bv, 'wo': wo, 'bo': bo, 'w1': w1, 'b1': b1, 'w2': w2, 'b2': b2, 'g1': g1, 'be1': be1, 'g2': g2, 'be2': be2, 'edge_index': edge_index, 'batch': batch, 'latent': 0}
    _L0_gnn_all = _L0_gnn_setup()
    _L0_gnn_in = {k: v for k, v in _L0_gnn_all.items() if k in ('wq', 'bq', 'wk', 'bk', 'wv', 'bv', 'wo', 'bo', 'w1', 'b1', 'w2', 'b2', 'g1', 'be1', 'g2', 'be2')}
    del _L0_gnn_all

    def _L1_gnn_setup():
        import jax, jax.numpy as jnp
        import numpy as np
        N, E, D = (100000, 500000, 128)
        key = jax.random.key(seed)
        ks = jax.random.split(key, 8)
        s = 1.0 / np.sqrt(D)
        return {'node_feat': jax.random.normal(ks[0], (N, D), dtype=jnp.float32), 'edge_index': jax.random.randint(ks[1], (2, E), 0, N, dtype=jnp.int64), 'W_edge': jax.random.normal(ks[2], (2 * D, D), dtype=jnp.float32) * s, 'b_edge': jnp.zeros((D,), dtype=jnp.float32), 'W1': jax.random.normal(ks[3], (D, D), dtype=jnp.float32) * s, 'b1': jnp.zeros((D,), dtype=jnp.float32), 'W2': jax.random.normal(ks[4], (D, D), dtype=jnp.float32) * s, 'b2': jnp.zeros((D,), dtype=jnp.float32), 'eps': jnp.zeros((1,), dtype=jnp.float32)}
    _L1_gnn_all = _L1_gnn_setup()
    _L1_gnn_in = {k: v for k, v in _L1_gnn_all.items() if k in ('W_edge', 'b_edge', 'W1', 'b1', 'W2', 'b2', 'eps')}
    del _L1_gnn_all

    def _L2_gnn_setup():
        import jax, jax.numpy as jnp
        import numpy as np
        EPS = 1e-07
        N_NODES, N_EDGES, D = (10000, 2500, 128)

        def mobius_add(x, y):
            x2 = jnp.sum(x * x, axis=-1, keepdims=True)
            y2 = jnp.sum(y * y, axis=-1, keepdims=True)
            xy = jnp.sum(x * y, axis=-1, keepdims=True)
            num = (1.0 + 2.0 * xy + y2) * x + (1.0 - x2) * y
            den = 1.0 + 2.0 * xy + x2 * y2
            return num / jnp.maximum(den, EPS)

        def mobius_scalar_mul(r, x):
            nrm = jnp.sqrt(jnp.sum(x * x, axis=-1, keepdims=True))
            nrm_c = jnp.clip(nrm, EPS, 1.0 - EPS)
            scaled = jnp.tanh(r * jnp.arctanh(nrm_c)) * (x / nrm_c)
            return jnp.where(nrm > EPS, scaled, jnp.zeros_like(x))
        key = jax.random.key(seed)
        kx, ke = jax.random.split(key)
        raw = jax.random.normal(kx, (N_NODES, D), dtype=jnp.float32)
        x = 0.4 * raw / (1.0 + jnp.linalg.norm(raw, axis=-1, keepdims=True))
        edge_index = jax.random.randint(ke, (2, N_EDGES), 0, N_NODES, dtype=jnp.int64)
        return {'x': x, 'edge_index': edge_index}
    _L2_gnn_all = _L2_gnn_setup()
    _L2_gnn_in = {k: v for k, v in _L2_gnn_all.items() if k in ()}
    del _L2_gnn_all

    def _L3_gnn_setup():
        import jax, jax.numpy as jnp
        import numpy as np
        N_NODES = 1024
        N_EDGES = 16384
        HIDDEN = 128
        N_GAUSS = 50
        CUTOFF = 6.0

        def _gaussian_smearing(dist):
            offset = jnp.linspace(0.0, CUTOFF, N_GAUSS)
            coeff = -0.5 / (offset[1] - offset[0]) ** 2
            d = dist[:, None] - offset[None, :]
            return jnp.exp(coeff * d * d)

        def _ssp(v):
            return jax.nn.softplus(v) - jnp.log(2.0).astype(v.dtype)
        key = jax.random.key(seed)
        ks = jax.random.split(key, 12)
        x = jax.random.normal(ks[0], (N_NODES, HIDDEN), dtype=jnp.float32)
        src = jax.random.randint(ks[1], (N_EDGES,), 0, N_NODES, dtype=jnp.int32)
        dst = jax.random.randint(ks[2], (N_EDGES,), 0, N_NODES, dtype=jnp.int32)
        edge_index = jnp.stack([src, dst])
        edge_weight = jax.random.uniform(ks[3], (N_EDGES,), minval=1.0, maxval=CUTOFF, dtype=jnp.float32)
        edge_attr = _gaussian_smearing(edge_weight)

        def w(k, fan_in, fan_out):
            return jax.random.normal(k, (fan_in, fan_out), dtype=jnp.float32) / np.sqrt(fan_in)
        return {'x': x, 'edge_index': edge_index, 'edge_weight': edge_weight, 'edge_attr': edge_attr, 'mlp_w1': w(ks[4], N_GAUSS, HIDDEN), 'mlp_b1': jnp.zeros((HIDDEN,), jnp.float32), 'mlp_w2': w(ks[5], HIDDEN, HIDDEN), 'mlp_b2': jnp.zeros((HIDDEN,), jnp.float32), 'lin1_w': w(ks[6], HIDDEN, HIDDEN), 'lin2_w': w(ks[7], HIDDEN, HIDDEN), 'lin2_b': jnp.zeros((HIDDEN,), jnp.float32), 'lin_w': w(ks[8], HIDDEN, HIDDEN), 'lin_b': jnp.zeros((HIDDEN,), jnp.float32)}
    _L3_gnn_all = _L3_gnn_setup()
    _L3_gnn_in = {k: v for k, v in _L3_gnn_all.items() if k in ('mlp_w1', 'mlp_b1', 'mlp_w2', 'mlp_b2', 'lin1_w', 'lin2_w', 'lin2_b', 'lin_w', 'lin_b')}
    del _L3_gnn_all
    return {'x': x, 'src': src, 'dst': dst, 'edge_attr_50': edge_attr_50, 'edge_weight': edge_weight, 'L0_gnn_wq': _L0_gnn_in['wq'], 'L0_gnn_bq': _L0_gnn_in['bq'], 'L0_gnn_wk': _L0_gnn_in['wk'], 'L0_gnn_bk': _L0_gnn_in['bk'], 'L0_gnn_wv': _L0_gnn_in['wv'], 'L0_gnn_bv': _L0_gnn_in['bv'], 'L0_gnn_wo': _L0_gnn_in['wo'], 'L0_gnn_bo': _L0_gnn_in['bo'], 'L0_gnn_w1': _L0_gnn_in['w1'], 'L0_gnn_b1': _L0_gnn_in['b1'], 'L0_gnn_w2': _L0_gnn_in['w2'], 'L0_gnn_b2': _L0_gnn_in['b2'], 'L0_gnn_g1': _L0_gnn_in['g1'], 'L0_gnn_be1': _L0_gnn_in['be1'], 'L0_gnn_g2': _L0_gnn_in['g2'], 'L0_gnn_be2': _L0_gnn_in['be2'], 'L1_gnn_W_edge': _L1_gnn_in['W_edge'], 'L1_gnn_b_edge': _L1_gnn_in['b_edge'], 'L1_gnn_W1': _L1_gnn_in['W1'], 'L1_gnn_b1': _L1_gnn_in['b1'], 'L1_gnn_W2': _L1_gnn_in['W2'], 'L1_gnn_b2': _L1_gnn_in['b2'], 'L1_gnn_eps': _L1_gnn_in['eps'], 'L3_gnn_mlp_w1': _L3_gnn_in['mlp_w1'], 'L3_gnn_mlp_b1': _L3_gnn_in['mlp_b1'], 'L3_gnn_mlp_w2': _L3_gnn_in['mlp_w2'], 'L3_gnn_mlp_b2': _L3_gnn_in['mlp_b2'], 'L3_gnn_lin1_w': _L3_gnn_in['lin1_w'], 'L3_gnn_lin2_w': _L3_gnn_in['lin2_w'], 'L3_gnn_lin2_b': _L3_gnn_in['lin2_b'], 'L3_gnn_lin_w': _L3_gnn_in['lin_w'], 'L3_gnn_lin_b': _L3_gnn_in['lin_b']}

def reference(x, src, dst, edge_attr_50, edge_weight, L0_gnn_wq, L0_gnn_bq, L0_gnn_wk, L0_gnn_bk, L0_gnn_wv, L0_gnn_bv, L0_gnn_wo, L0_gnn_bo, L0_gnn_w1, L0_gnn_b1, L0_gnn_w2, L0_gnn_b2, L0_gnn_g1, L0_gnn_be1, L0_gnn_g2, L0_gnn_be2, L1_gnn_W_edge, L1_gnn_b_edge, L1_gnn_W1, L1_gnn_b1, L1_gnn_W2, L1_gnn_b2, L1_gnn_eps, L3_gnn_mlp_w1, L3_gnn_mlp_b1, L3_gnn_mlp_w2, L3_gnn_mlp_b2, L3_gnn_lin1_w, L3_gnn_lin2_w, L3_gnn_lin2_b, L3_gnn_lin_w, L3_gnn_lin_b):
    import jax
    import jax.numpy as jnp

    def _L0_gnn_ref(x, wq, bq, wk, bk, wv, bv, wo, bo, w1, b1, w2, b2, g1, be1, g2, be2, edge_index, batch, latent):
        import jax, jax.numpy as jnp
        import numpy as np
        N, E, EMB, HID, H = (50000, 12500, 128, 512, 8)
        D = EMB // H
        EPS = 1e-05

        def _linear_params(key, fan_in, fan_out):
            s = 1.0 / np.sqrt(fan_in)
            k1, k2 = jax.random.split(key)
            w = jax.random.uniform(k1, (fan_in, fan_out), minval=-s, maxval=s, dtype=jnp.float32)
            b = jax.random.uniform(k2, (fan_out,), minval=-s, maxval=s, dtype=jnp.float32)
            return (w, b)

        def _batchnorm(x, g, b):
            mu = x.mean(axis=0)
            var = ((x - mu) ** 2).mean(axis=0)
            return g * (x - mu) * jax.lax.rsqrt(var + EPS) + b

        def _forward(x, wq, bq, wk, bk, wv, bv, wo, bo, w1, b1, w2, b2, g1, be1, g2, be2, A, B):
            n = x.shape[0]
            q = (x @ wq + bq).reshape(n, H, D)
            k = (x @ wk + bk).reshape(n, H, D)
            v = (x @ wv + bv).reshape(n, H, D)
            score = jnp.einsum('ehd,egd->ehg', q[A], k[B])
            ssum = jax.ops.segment_sum(score, A, num_segments=n)
            cnt = jax.ops.segment_sum(jnp.ones((A.shape[0],), score.dtype), A, num_segments=n)
            score = ssum / jnp.maximum(cnt, 1.0)[:, None, None]
            score = jax.nn.softmax(score, axis=-1)
            out = jnp.einsum('ehg,egd->ehd', score, v).reshape(n, EMB)
            out = out @ wo + bo
            x = _batchnorm(out + x, g1, be1)
            h = jax.nn.gelu(x @ w1 + b1, approximate=False)
            h = h @ w2 + b2
            x = _batchnorm(h + x, g2, be2)
            return x
        A, B = (edge_index[0], edge_index[1])
        return _forward(x, wq, bq, wk, bk, wv, bv, wo, bo, w1, b1, w2, b2, g1, be1, g2, be2, A, B)

    def _L1_gnn_ref(node_feat, edge_index, W_edge, b_edge, W1, b1, W2, b2, eps):
        import jax, jax.numpy as jnp
        import numpy as np
        N, E, D = (100000, 500000, 128)
        n_nodes = node_feat.shape[0]
        src, dst = (edge_index[0], edge_index[1])
        h_src = node_feat[src]
        h_dst = node_feat[dst]
        edge_emb = jnp.concatenate([h_src, h_dst], axis=1)
        m = jax.nn.relu(edge_emb @ W_edge + b_edge)
        neigh = jax.ops.segment_sum(m, dst, num_segments=n_nodes)
        rst = (1.0 + eps[0]) * node_feat + neigh
        out = jax.nn.relu(rst @ W1 + b1) @ W2 + b2
        return out

    def _L2_gnn_ref(x, edge_index):
        import jax, jax.numpy as jnp
        import numpy as np
        EPS = 1e-07
        N_NODES, N_EDGES, D = (10000, 2500, 128)

        def mobius_add(x, y):
            x2 = jnp.sum(x * x, axis=-1, keepdims=True)
            y2 = jnp.sum(y * y, axis=-1, keepdims=True)
            xy = jnp.sum(x * y, axis=-1, keepdims=True)
            num = (1.0 + 2.0 * xy + y2) * x + (1.0 - x2) * y
            den = 1.0 + 2.0 * xy + x2 * y2
            return num / jnp.maximum(den, EPS)

        def mobius_scalar_mul(r, x):
            nrm = jnp.sqrt(jnp.sum(x * x, axis=-1, keepdims=True))
            nrm_c = jnp.clip(nrm, EPS, 1.0 - EPS)
            scaled = jnp.tanh(r * jnp.arctanh(nrm_c)) * (x / nrm_c)
            return jnp.where(nrm > EPS, scaled, jnp.zeros_like(x))
        src, dst = (edge_index[0], edge_index[1])
        n, d = x.shape
        messages = mobius_add(x[src], -x[dst])

        def body(out, em):
            m, idx = em
            return (out.at[idx].set(mobius_add(out[idx], m)), None)
        out0 = jnp.zeros((n, d), dtype=x.dtype)
        total, _ = jax.lax.scan(body, out0, (messages, dst))
        count = jnp.zeros((n,), dtype=x.dtype).at[dst].add(1.0)
        scale = 1.0 / jnp.maximum(count, 1.0)
        aggr = mobius_scalar_mul(scale[:, None], total)
        return mobius_add(x, aggr)

    def _L3_gnn_ref(x, edge_index, edge_weight, edge_attr, mlp_w1, mlp_b1, mlp_w2, mlp_b2, lin1_w, lin2_w, lin2_b, lin_w, lin_b):
        import jax, jax.numpy as jnp
        import numpy as np
        N_NODES = 1024
        N_EDGES = 16384
        HIDDEN = 128
        N_GAUSS = 50
        CUTOFF = 6.0

        def _gaussian_smearing(dist):
            offset = jnp.linspace(0.0, CUTOFF, N_GAUSS)
            coeff = -0.5 / (offset[1] - offset[0]) ** 2
            d = dist[:, None] - offset[None, :]
            return jnp.exp(coeff * d * d)

        def _ssp(v):
            return jax.nn.softplus(v) - jnp.log(2.0).astype(v.dtype)
        n_nodes = x.shape[0]
        C = 0.5 * (jnp.cos(edge_weight * (jnp.pi / CUTOFF)) + 1.0)
        W = _ssp(edge_attr @ mlp_w1 + mlp_b1) @ mlp_w2 + mlp_b2
        W = W * C[:, None]
        h = x @ lin1_w
        src, dst = (edge_index[0], edge_index[1])
        msg = h[src] * W
        agg = jax.ops.segment_sum(msg, dst, num_segments=n_nodes)
        out = agg @ lin2_w + lin2_b
        out = _ssp(out)
        return out @ lin_w + lin_b
    edge_index = jnp.stack([src, dst])
    batch0 = jnp.zeros((50000,), jnp.int32)
    h = jnp.maximum(_layernorm(x, axis=-1), 0.0)
    x = x + _L0_gnn_ref(h, L0_gnn_wq, L0_gnn_bq, L0_gnn_wk, L0_gnn_bk, L0_gnn_wv, L0_gnn_bv, L0_gnn_wo, L0_gnn_bo, L0_gnn_w1, L0_gnn_b1, L0_gnn_w2, L0_gnn_b2, L0_gnn_g1, L0_gnn_be1, L0_gnn_g2, L0_gnn_be2, edge_index, batch0, 0)
    h = jnp.maximum(_layernorm(x, axis=-1), 0.0)
    x = x + _L1_gnn_ref(h, edge_index, L1_gnn_W_edge, L1_gnn_b_edge, L1_gnn_W1, L1_gnn_b1, L1_gnn_W2, L1_gnn_b2, L1_gnn_eps)
    h = jnp.maximum(_layernorm(x, axis=-1), 0.0)
    x = x + _L2_gnn_ref(h, edge_index)
    h = jnp.maximum(_layernorm(x, axis=-1), 0.0)
    x = x + _L3_gnn_ref(h, edge_index, edge_weight, edge_attr_50, L3_gnn_mlp_w1, L3_gnn_mlp_b1, L3_gnn_mlp_w2, L3_gnn_mlp_b2, L3_gnn_lin1_w, L3_gnn_lin2_w, L3_gnn_lin2_b, L3_gnn_lin_w, L3_gnn_lin_b)
    return x

_drawn_inputs = setup_inputs


def setup_inputs(seed=0):
    import zlib

    import numpy as np

    out = dict(_drawn_inputs(seed))
    spreads = {'L0_gnn_g1': (1.0, 0.571),
     'L0_gnn_be1': (0.0, 0.8),
     'L0_gnn_g2': (1.0, 0.2),
     'L0_gnn_be2': (0.0, 0.1),
     'L1_gnn_b_edge': (0.0, 0.411),
     'L1_gnn_b1': (0.0, 0.1),
     'L1_gnn_b2': (0.0, 0.1),
     'L3_gnn_mlp_b1': (0.0, 0.8),
     'L3_gnn_mlp_b2': (0.0, 0.8),
     'L3_gnn_lin2_b': (0.0, 0.452),
     'L3_gnn_lin_b': (0.0, 0.1)}
    factors = {'edge_attr_50': 5.819,
     'edge_weight': 5.166,
     'L0_gnn_bq': 8.0,
     'L0_gnn_bk': 8.0,
     'L0_gnn_bv': 8.0,
     'L0_gnn_bo': 8.0,
     'L0_gnn_b1': 8.0,
     'L0_gnn_b2': 8.0,
     'L3_gnn_lin2_w': 2.707}
    for name, (base, spread) in spreads.items():
        noise = np.random.default_rng([zlib.crc32(name.encode()), seed]).standard_normal(out[name].shape)
        drawn = base * np.exp(spread * noise) if base else spread * noise
        out[name] = jnp.asarray(drawn.astype(out[name].dtype))
    for name, factor in factors.items():
        out[name] = (out[name] * factor).astype(out[name].dtype)
    return out
```

```python
import math
from contextlib import ExitStack


import concourse.bass as bass
import concourse.mybir as mybir

P = 128
D = 128
J = 4
CH = P * J
HID = 512
HEADS = 8
DH = D // HEADS
NG = 50
LO_BITS = 9
LO = 1 << LO_BITS
SKIP = 1 << 20
LN_EPS = 1e-5
HYP_EPS = 1e-7
CUTOFF = 6.0

F32 = mybir.dt.float32
F16 = mybir.dt.float16
BF16 = mybir.dt.bfloat16
I32 = mybir.dt.int32
U32 = mybir.dt.uint32
ALU = mybir.AluOpType
ACT = mybir.ActivationFunctionType
AX = mybir.AxisListType

REC_KEY, REC_OTHER, REC_ID, REC_WEIGHT, REC = 0, 1, 2, 3, 4


class Shapes:

    def __init__(self, n_nodes, n_edges):
        self.N, self.E = n_nodes, n_edges
        self.chunks = -(-n_nodes // CH)
        self.chunks += self.chunks % 2
        self.NP = self.chunks * CH
        self.full = (n_nodes // CH)
        self.tail = n_nodes - (self.chunks - 1) * CH
        assert 0 < self.tail < CH and self.tail % J == 0
        self.tp = self.tail // J
        self.tiles = -(-n_edges // P)
        self.tiles += self.tiles % 2
        self.echunks = self.tiles * P // CH + 1
        self.echunks += self.echunks % 2
        self.T = self.echunks * J
        self.EP = self.T * P
        assert self.EP > self.tiles * P and n_nodes + 1 <= P * LO


def after(eng, sem, value):
    if isinstance(value, int) and value <= 0:
        return
    eng.wait_ge(sem, value)


def each(eng, n, body, ring=2, peel=1):
    assert n % ring == 0
    front = min(peel * ring, n)
    back = max(n - ring, front)
    for c in range(front):
        body(c, c % ring)
    if back > front:
        with eng.Fori(front // ring, back // ring) as i:
            for u in range(ring):
                body(i * ring + u, u)
    for c in range(back, n):
        body(c, c % ring)


def each_phases(eng, n, phases, ring=2):
    lags = len(phases)
    peel = -(-(lags + ring - 1) // ring)

    def body(c, u):
        for i, f in enumerate(phases):
            if f is not None and not (isinstance(c, int) and c < i):
                f(c - i, (u - i) % ring)
    each(eng, n, body, ring, peel)
    for c in range(n, n + lags - 1):
        for i, f in enumerate(phases):
            if f is not None and c - i < n:
                f(c - i, (c - i) % ring)




class Chain:

    def __init__(self, eng, sem, per):
        self.eng, self.sem, self.per = eng, sem, per
        self.base, self.n = 0, 0

    def step(self, c):
        self.base, self.n = c * self.per, 0

    def link(self, ins):
        ins.then_inc(self.sem, 1)
        self.n += 1
        assert self.n <= self.per
        self.eng.wait_ge(self.sem, self.base + self.n)


class Stage:

    def __init__(self, nc, name):
        self.nc, self.name, self.stack, self.sems = nc, name, ExitStack(), []

    def __enter__(self):
        return self

    def __exit__(self, *e):
        self.stack.close()
        if e[0] is None:
            self.nc.clear_and_free_semaphores([s.num for s in self.sems])
            self.nc.all_engine_barrier()

    def sb(self, name, shape, dt=F32):
        return self.stack.enter_context(self.nc.sbuf_tensor(f"{self.name}_{name}", shape, dt))

    def ps(self, name, shape, dt=F32):
        return self.stack.enter_context(self.nc.psum_tensor(f"{self.name}_{name}", shape, dt))

    def sem(self, name):
        s = self.nc.alloc_semaphore(f"{self.name}_{name}")
        self.sems.append(s)
        return s

    def run(self):
        return self.nc.Block()


def rows(table, c):
    return table[bass.ds(c * CH, CH), :].rearrange("(p j) d -> p j d", j=J)


def make_constants(nc, k):
    with Stage(nc, "consts") as st:
        made = st.sem("made")
        seen = st.sem("seen")
        with st.run() as block:

            @block.gpsimd
            def _(pool):
                n = 0
                for t, v in ((k.ident, 0.0), (k.lower, 1.0), (k.strict, 1.0), (k.shift, 0.0),
                             (k.unshift, 0.0), (k.ones, 1.0), (k.zero_col, 0.0), (k.e_first, 0.0),
                             (k.eps_col, LN_EPS), (k.half_col, 0.5)):
                    pool.memset(t[:], v).then_inc(made, 1)
                    n += 1
                pool.wait_ge(made, n)
                pool.affine_select(out=k.ident[:], in_=k.ident[:], compare_op=ALU.not_equal, fill=1.0,
                                   base=0, pattern=[[-1, P]], channel_multiplier=1).then_inc(made, 1)
                pool.affine_select(out=k.lower[:], in_=k.lower[:], compare_op=ALU.is_gt, fill=0.0,
                                   base=0, pattern=[[-1, P]], channel_multiplier=1).then_inc(made, 1)
                pool.affine_select(out=k.strict[:], in_=k.strict[:], compare_op=ALU.is_gt, fill=0.0,
                                   base=0, pattern=[[1, P]], channel_multiplier=-1).then_inc(made, 1)
                pool.affine_select(out=k.shift[:], in_=k.shift[:], compare_op=ALU.not_equal, fill=1.0,
                                   base=1, pattern=[[-1, P]], channel_multiplier=1).then_inc(made, 1)
                pool.affine_select(out=k.unshift[:], in_=k.unshift[:], compare_op=ALU.not_equal, fill=1.0,
                                   base=-1, pattern=[[-1, P]], channel_multiplier=1).then_inc(made, 1)
                pool.affine_select(out=k.e_first[:], in_=k.e_first[:], compare_op=ALU.not_equal, fill=1.0,
                                   base=0, pattern=[[0, 1]], channel_multiplier=1).then_inc(made, 1)
                n += 6
                pool.wait_ge(made, n)

            @block.vector
            def _(dve):
                dve.wait_ge(made, 16)
                nc.vector.tensor_copy(k.ident16[:], k.ident[:]).then_inc(seen, 1)
                dve.wait_ge(seen, 1)


def sort_edges(nc, k, s, key, other, weight, rec):
    full = s.E // P
    rem = s.E - full * P
    halves = [(0, min(full, P)), (P, max(full - P, 0))]
    with Stage(nc, f"sort_{key.tensor.name}") as st:
        raw = st.sb("raw", [P, 4, 2, P], I32)
        asf = st.sb("asf", [P, 5, 2, P])
        lanes = st.sb("lanes", [P, 5, 2 * P])
        recs = st.sb("recs", [P, 2 * P, REC])
        iota_i = st.sb("iota_i", [P, LO], I32)
        iota_h = st.sb("iota_h", [P, LO], F16)
        ids = st.sb("ids", [P, 2 * P], I32)
        pad = st.sb("pad", [P, (s.EP // P - s.tiles) * REC])
        hot_hi = st.sb("hot_hi", [P, 2, P], BF16)
        hot_lo = st.sb("hot_lo", [P, 2, LO], BF16)
        zeros = st.sb("zeros", [P, LO], BF16)
        scan = st.sb("scan", [P, LO])
        onesf = st.sb("onesf", [P, LO])
        rowtot = st.sb("rowtot", [P, 1])
        table = st.sb("table", [P, 2, LO])
        hotT = st.sb("hotT", [P, 2, P])
        diag = st.sb("diag", [P, 2, P])
        junk = st.sb("junk", [P, LO])
        junk2 = st.sb("junk2", [P, P])
        rank = st.sb("rank", [P, 2])
        base = st.sb("base", [P, 2])
        place = st.sb("place", [P, 2], U32)
        outrec = st.sb("outrec", [P, 2, REC])
        psT = [st.ps(f"psT{i}", [P, 2 * P]) for i in range(2)]
        count = st.ps("count", [P, LO])
        look = st.ps("look", [P, LO])
        psH = st.ps("psH", [P, P], BF16)
        psK = st.ps("psK", [P, P])
        psR = st.ps("psR", [P, 4])

        loaded, cleared, chain = st.sem("loaded"), st.sem("cleared"), st.sem("chain")
        split, turned, taken = st.sem("split"), st.sem("turned"), st.sem("taken")
        iotas, hot, counted = st.sem("iotas"), st.sem("hot"), st.sem("counted")
        totals, offsets, started = st.sem("totals"), st.sem("offsets"), st.sem("started")
        seeded = st.sem("seeded")
        t_hot, t_updated, t_hotT, t_copied, t_hotT_sb = (st.sem("t_hot"), st.sem("t_updated"), st.sem("t_hotT"),
                                                         st.sem("t_copied"), st.sem("t_hotT_sb"))
        t_diag, t_keys, t_rank, t_look, t_place = (st.sem("t_diag"), st.sem("t_keys"), st.sem("t_rank"),
                                                   st.sem("t_look"), st.sem("t_place"))
        t_rec, padded, pad_sent, tick = st.sem("t_rec"), st.sem("padded"), st.sem("pad_sent"), st.sem("tick")
        t_sent = [st.sem(f"t_sent{i}") for i in range(2)]
        n_loads = 3 * ((1 if halves[0][1] else 0) + (1 if halves[1][1] else 0) + (1 if rem else 0))
        rem_half, rem_row = full // P, full % P
        first_pad = s.tiles * P

        with st.run() as block:

            @block.sync
            def _(sp):
                sp.wait_ge(cleared, 4)
                for a, src in ((0, key), (1, other)):
                    for h, (t0, nt) in enumerate(halves):
                        if nt:
                            sp.dma_start(raw[0:nt, a, h, :], src[t0 * P:(t0 + nt) * P].rearrange("(t e) -> t e", e=P)).then_inc(loaded, 16)
                    if rem:
                        sp.dma_start(raw[rem_row:rem_row + 1, a, rem_half, 0:rem],
                                     src[full * P:s.E].rearrange("(t e) -> t e", t=1)).then_inc(loaded, 16)
                for h, (t0, nt) in enumerate(halves):
                    if nt:
                        sp.dma_start(asf[0:nt, 4, h, :], weight[t0 * P:(t0 + nt) * P].rearrange("(t e) -> t e", e=P)).then_inc(loaded, 16)
                if rem:
                    sp.dma_start(asf[rem_row:rem_row + 1, 4, rem_half, 0:rem],
                                 weight[full * P:s.E].rearrange("(t e) -> t e", t=1)).then_inc(loaded, 16)
                sp.wait_ge(padded, 2)
                sp.dma_start(rec[first_pad:s.EP, :].rearrange("(p t) r -> p (t r)", p=P), pad[:]).then_inc(pad_sent, 16)
                sp.wait_ge(pad_sent, 16)

            @block.gpsimd
            def _(pool):
                pool.memset(raw[:, 0], s.N).then_inc(cleared, 1)
                pool.memset(raw[:, 1], 0).then_inc(cleared, 1)
                pool.memset(asf[:, 4], 0.0).then_inc(cleared, 1)
                pool.memset(zeros[:], 0.0).then_inc(cleared, 1)
                pool.memset(onesf[:], 1.0).then_inc(iotas, 1)
                pool.iota(iota_i[:], [[1, LO]], base=0, channel_multiplier=0).then_inc(iotas, 1)
                pool.iota(ids[:], [[P, 2 * P]], base=0, channel_multiplier=1).then_inc(iotas, 1)
                pool.memset(pad[:], 0.0).then_inc(padded, 1)
                pool.wait_ge(padded, 1)
                pool.memset(pad[:].rearrange("p (t r) -> p t r", r=REC)[:, :, REC_KEY], float(s.N)).then_inc(padded, 1)

                bound = pool.to_reg(s.EP - 1)

                def send(t, u):
                    pool.wait_ge(t_place, t + 1)
                    pool.wait_ge(t_rec, t + 1)
                    pool.sem_inc(tick, 1)
                    pool.indirect_dma_start(out=rec, out_offset=bass.IndirectOffsetOnAxis(ap=place[:, u:u + 1], axis=0),
                                            in_=outrec[:, u, :], in_offset=None, bounds_check=bound,
                                            oob_is_err=False).then_inc(t_sent[u], 16)
                each(pool, s.tiles, send)
                for u in range(2):
                    pool.wait_ge(t_sent[u], 16 * (s.tiles // 2))

            @block.vector
            def _(dve):
                ch = Chain(dve, chain, 8)
                dve.wait_ge(loaded, 16 * n_loads)
                dve.wait_ge(iotas, 3)
                nc.vector.tensor_scalar(raw[:, 2], raw[:, 0], LO_BITS, None, ALU.logical_shift_right).then_inc(chain, 1)
                nc.vector.tensor_scalar(raw[:, 3], raw[:, 0], LO - 1, None, ALU.bitwise_and).then_inc(chain, 1)
                nc.vector.tensor_copy(iota_h[:], iota_i[:]).then_inc(chain, 1)
                dve.wait_ge(chain, 3)
                nc.vector.tensor_copy(asf[:, 0:4], raw[:]).then_inc(split, 1)
                nc.vector.tensor_copy(recs[:, :, REC_ID], ids[:]).then_inc(chain, 1)
                for a in range(5):
                    dve.wait_ge(turned, a + 1)
                    nc.vector.tensor_copy(lanes[:, a, :], psT[a % 2][:]).then_inc(taken, 1)
                dve.wait_ge(taken, 5)
                nc.vector.tensor_copy(recs[:, :, REC_KEY], lanes[:, 0, :]).then_inc(chain, 1)
                nc.vector.tensor_copy(recs[:, :, REC_OTHER], lanes[:, 1, :]).then_inc(chain, 1)
                nc.vector.tensor_copy(recs[:, :, REC_WEIGHT], lanes[:, 4, :]).then_inc(chain, 1)
                dve.wait_ge(chain, 7)

                def one_hots(t, u):
                    nc.vector.tensor_scalar(hot_hi[:, u, :], iota_h[:, 0:P], lanes[:, 2, bass.ds(t, 1)], None, ALU.is_equal)
                    return nc.vector.tensor_scalar(hot_lo[:, u, :], iota_h[:], lanes[:, 3, bass.ds(t, 1)], None, ALU.is_equal)

                def count_step(t, u):
                    after(dve, counted, t - 1)
                    one_hots(t, u).then_inc(hot, 1)
                each(dve, s.tiles, count_step)
                dve.wait_ge(counted, s.tiles)
                nc.vector.tensor_tensor_scan(scan[:], onesf[:], count[:], 0.0, ALU.mult, ALU.add).then_inc(chain, 1)
                dve.wait_ge(chain, 8)
                nc.vector.tensor_copy(rowtot[:], scan[:, LO - 1:LO]).then_inc(totals, 1)
                nc.vector.tensor_tensor(junk[:], scan[:], count[:], ALU.subtract).then_inc(chain, 1)
                dve.wait_ge(offsets, 1)
                dve.wait_ge(chain, 9)
                nc.vector.tensor_scalar(table[:, 1, :], junk[:], psR[:, 0:1], None, ALU.add).then_inc(started, 1)

                def place_step(t, u):
                    after(dve, t_updated, t - 1)
                    one_hots(t, u).then_inc(t_hot, 1)
                    after(dve, t_keys, t - 1)
                    nc.vector.tensor_scalar(diag[:, u, :], k.ident[:], lanes[:, 0, bass.ds(t, 1)], None, ALU.mult).then_inc(t_diag, 1)
                    dve.wait_ge(t_keys, t + 1)
                    nc.vector.scalar_tensor_tensor(junk2[:], psK[:], lanes[:, 0, bass.ds(t, 1)], k.lower[:],
                                                   ALU.is_equal, ALU.mult, accum_out=rank[:, u:u + 1]).then_inc(t_rank, 1)
                    dve.wait_ge(t_look, t + 1)
                    nc.vector.scalar_tensor_tensor(junk[:], look[:], 1.0, hot_lo[:, u, :],
                                                   ALU.mult, ALU.mult, accum_out=base[:, u:u + 1]).then_inc(t_rank, 1)
                    dve.wait_ge(t_rank, 2 * t + 2)
                    if not isinstance(t, int) or t >= 2:
                        dve.wait_ge(t_sent[u], 16 * ((t - u) // 2) if isinstance(t, int) else (t - u) * 8)
                    nc.vector.tensor_tensor(place[:, u:u + 1], rank[:, u:u + 1], base[:, u:u + 1], ALU.add).then_inc(t_place, 1)
                    nc.vector.tensor_copy(outrec[:, u, :], recs[:].rearrange("p t r -> p (t r)")[:, bass.ds(t * REC, REC)]).then_inc(t_rec, 1)
                each(dve, s.tiles, place_step)

            @block.tensor
            def _(pe):
                pe.wait_ge(split, 1)
                for a in range(5):
                    after(pe, taken, a - 1)
                    nc.tensor.transpose(psT[a % 2][:, 0:P], asf[:, a, 0, :], k.ident[:])
                    nc.tensor.transpose(psT[a % 2][:, P:2 * P], asf[:, a, 1, :], k.ident[:]).then_inc(turned, 1)
                pe.wait_ge(cleared, 4)
                nc.tensor.matmul(count[:], zeros[:, 0:P], zeros[:], start=True, stop=False, skip_group_check=True)

                def count_step(t, u):
                    pe.wait_ge(hot, t + 1)
                    nc.tensor.matmul(count[:], hot_hi[:, u, :], hot_lo[:, u, :], start=False, stop=False,
                                     skip_group_check=True).then_inc(counted, 1)
                each(pe, s.tiles, count_step)
                pe.wait_ge(totals, 1)
                nc.tensor.matmul(psR[:, 0:1], k.strict[:], rowtot[:], start=True, stop=True).then_inc(offsets, 1)
                pe.wait_ge(started, 1)
                nc.tensor.matmul(count[:], k.ident[:], table[:, 1, :], start=True, stop=False,
                                 skip_group_check=True).then_inc(seeded, 1)

                def place_step(t, u):
                    pe.wait_ge(t_hot, t + 1)
                    after(pe, t_hotT_sb, t)
                    nc.tensor.transpose(psH[:], hot_hi[:, u, :], k.ident16[:]).then_inc(t_hotT, 1)
                    pe.wait_ge(t_diag, t + 1)
                    after(pe, t_rank, 2 * t - 1)
                    nc.tensor.matmul(psK[:], k.ones[:], diag[:, u, :], start=True, stop=True).then_inc(t_keys, 1)
                    pe.wait_ge(t_copied, t + 1)
                    pe.wait_ge(t_hotT_sb, t + 1)
                    after(pe, t_rank, 2 * t)
                    nc.tensor.matmul(look[:], hotT[:, u, :], table[:, u, :], start=True, stop=True).then_inc(t_look, 1)
                    nc.tensor.matmul(count[:], hot_hi[:, u, :], hot_lo[:, u, :], start=False, stop=False,
                                     skip_group_check=True).then_inc(t_updated, 1)
                each(pe, s.tiles, place_step)

            @block.scalar
            def _(act):
                act.wait_ge(seeded, 1)

                def place_step(t, u):
                    after(act, t_updated, t)
                    after(act, t_look, t - 1)
                    nc.scalar.copy(table[:, u, :], count[:]).then_inc(t_copied, 1)
                    act.wait_ge(t_hotT, t + 1)
                    nc.scalar.copy(hotT[:, u, :], psH[:]).then_inc(t_hotT_sb, 1)
                each(act, s.tiles, place_step)


def edge_plan(nc, k, s, rec, plan):
    T = s.T
    with Stage(nc, f"plan_{plan.name}") as st:
        r = st.sb("r", [P, T, REC])
        keyf = st.sb("keyf", [P, T + 2])
        tmp = st.sb("tmp", [P, T])
        real = st.sb("real", [P, T])
        lastf = st.sb("lastf", [P, T])
        ones = st.sb("ones", [P, T])
        diag = st.sb("diag", [P, P])
        cc = st.sb("cc", [P, 1])
        psE = st.ps("psE", [P, 8])
        psB = st.ps("psB", [P, P])
        loaded, chain = st.sem("loaded"), st.sem("chain")
        keys, ends, first, firsts = st.sem("keys"), st.sem("ends"), st.sem("first"), st.sem("firsts")
        counts, carried = st.sem("counts"), st.sem("carried")
        ones_made = st.sem("ones_made")
        with st.run() as block:

            @block.sync
            def _(sp):
                sp.dma_start(r[:], rec[:, :].rearrange("(p t) r -> p t r", p=P)).then_inc(loaded, 16)
                sp.wait_ge(loaded, 16)

            @block.gpsimd
            def _(pool):
                pool.memset(ones[:], 1.0).then_inc(ones_made, 1)

            @block.vector
            def _(dve):
                ch = Chain(dve, chain, 99)
                key = keyf[:, 1:T + 1]
                dve.wait_ge(loaded, 16)
                nc.vector.tensor_copy(key, r[:, :, REC_KEY]).then_inc(keys, 1)
                nc.vector.tensor_copy(plan.other[:], r[:, :, REC_OTHER])
                nc.vector.tensor_copy(plan.edge[:], r[:, :, REC_ID])
                nc.vector.tensor_copy(plan.weight[:], r[:, :, REC_WEIGHT])
                dve.wait_ge(keys, 1)
                nc.vector.tensor_scalar(diag[:], k.ident[:], keyf[:, 1:2], None, ALU.mult).then_inc(first, 1)
                dve.wait_ge(ends, 1)
                nc.vector.tensor_tensor(keyf[:, 0:1], psE[:, 0:1], k.e_first[:], ALU.subtract)
                ch.link(nc.vector.tensor_copy(keyf[:, T + 1:T + 2], psE[:, 1:2]))
                nc.vector.tensor_tensor(plan.same[:], key, keyf[:, 0:T], ALU.is_equal)
                nc.vector.tensor_tensor(lastf[:], key, keyf[:, 2:T + 2], ALU.not_equal)
                nc.vector.tensor_scalar(real[:], key, float(s.N), None, ALU.is_lt)
                nc.vector.tensor_scalar(plan.first[:], key, keyf[:, 1:2], None, ALU.is_equal)
                ch.link(nc.vector.tensor_tensor(tmp[:], key, key, ALU.bypass))
                ch.link(nc.vector.tensor_tensor(lastf[:], lastf[:], real[:], ALU.mult))
                nc.vector.tensor_copy(plan.cont[:], plan.same[:, 0:1])
                ch.link(nc.vector.tensor_tensor(tmp[:], key, real[:], ALU.mult))
                ch.link(nc.vector.tensor_copy(plan.key[:], tmp[:]))
                ch.link(nc.vector.tensor_scalar(tmp[:], lastf[:], -float(SKIP), float(SKIP), ALU.mult, ALU.add))
                ch.link(nc.vector.tensor_tensor(lastf[:], lastf[:], key, ALU.mult))
                ch.link(nc.vector.tensor_tensor(plan.last[:], tmp[:], lastf[:], ALU.add))
                ch.link(nc.vector.memset(plan.same[:, 0:1], 1.0))
                dve.wait_ge(firsts, 1)
                ch.link(nc.vector.scalar_tensor_tensor(plan.carry[:], psB[:], keyf[:, T:T + 1], k.strict[:],
                                                       ALU.is_equal, ALU.mult))
                dve.wait_ge(ones_made, 1)
                ch.link(nc.vector.tensor_tensor_scan(plan.count[:], plan.same[:], ones[:], 0.0, ALU.mult, ALU.add))
                nc.vector.tensor_copy(tmp[:, 0:1], plan.count[:, T - 1:T]).then_inc(counts, 1)
                dve.wait_ge(carried, 1)
                ch.link(nc.vector.tensor_copy(cc[:], psE[:, 2:3]))
                ch.link(nc.vector.scalar_tensor_tensor(plan.count[:], plan.first[:], cc[:], plan.count[:],
                                                       ALU.mult, ALU.add))
                ch.link(nc.vector.reciprocal(plan.inv[:], plan.count[:]))
                ch.link(nc.vector.tensor_tensor(plan.through[:], keyf[:, 1:2], keyf[:, T:T + 1], ALU.is_equal))
                ch.link(nc.vector.tensor_tensor(plan.through[:], plan.through[:], plan.cont[:], ALU.mult))
                ch.link(nc.vector.tensor_tensor(plan.through[:], plan.through[:], real[:, 0:1], ALU.mult))

            @block.tensor
            def _(pe):
                pe.wait_ge(keys, 1)
                nc.tensor.matmul(psE[:, 0:1], k.shift[:], keyf[:, T:T + 1], start=True, stop=True)
                nc.tensor.matmul(psE[:, 1:2], k.unshift[:], keyf[:, 1:2], start=True, stop=True).then_inc(ends, 1)
                pe.wait_ge(first, 1)
                nc.tensor.matmul(psB[:], k.ones[:], diag[:], start=True, stop=True).then_inc(firsts, 1)
                pe.wait_ge(counts, 1)
                nc.tensor.matmul(psE[:, 2:3], plan.carry[:], tmp[:, 0:1], start=True, stop=True).then_inc(carried, 1)


class Constants:
    def __init__(self, stack, nc):
        def sb(name, shape, dt=F32):
            return stack.enter_context(nc.sbuf_tensor(name, shape, dt))
        self.ident, self.ident16 = sb("ident", [P, P]), sb("ident16", [P, P], BF16)
        self.ones = sb("ones", [P, P])
        self.lower, self.strict = sb("lower", [P, P]), sb("strict", [P, P])
        self.shift, self.unshift = sb("shift", [P, P]), sb("unshift", [P, P])
        self.zero_col, self.e_first = sb("zero_col", [P, 1]), sb("e_first", [P, 1])
        self.eps_col, self.half_col = sb("eps_col", [P, 1]), sb("half_col", [P, 1])


class Plan:

    def __init__(self, stack, nc, s, name):
        def sb(n, shape, dt=F32):
            return stack.enter_context(nc.sbuf_tensor(f"{name}_{n}", shape, dt))
        T = s.T
        self.name = name
        self.key, self.other, self.edge = sb("key", [P, T], U32), sb("other", [P, T], U32), sb("edge", [P, T], U32)
        self.last = sb("last", [P, T], U32)
        self.weight = sb("weight", [P, T])
        self.same = sb("same", [P, T])
        self.first = sb("first", [P, T])
        self.count, self.inv = sb("count", [P, T]), sb("inv", [P, T])
        self.carry = sb("carry", [P, P])
        self.cont, self.through = sb("cont", [P, 1]), sb("through", [P, 1])


def each_lagged(eng, n, now, lag):
    each_phases(eng, n, [now, lag])


def sent(eng, sems, c, u, per=1):
    ring = len(sems)
    if isinstance(c, int):
        after(eng, sems[u], 16 * per * ((c - u) // ring))
    else:
        eng.wait_ge(sems[u], (c - u) * (16 * per // ring))


def landed(eng, sems, c, u, per=1):
    eng.wait_ge(sems[u], (c - u) * (16 * per // len(sems)) + 16 * per)


def all_landed(eng, sems, n, per=1):
    for sem in sems:
        eng.wait_ge(sem, (n // len(sems)) * 16 * per)


class Norm:

    def __init__(self, nc, st, k):
        self.nc, self.k = nc, k
        self.stats = st.sb("ln_stats", [P, 2, J, 6])
        self.mv = st.sb("ln_mv", [P, 2, J, 2])
        self.std = st.sb("ln_std", [P, 2, J])
        self.scale = st.sb("ln_scale", [P, 2, J])
        self.bias = st.sb("ln_bias", [P, 2, J])
        self.halves, self.moments, self.roots, self.coefs = (st.sem("ln_halves"), st.sem("ln_moments"),
                                                             st.sem("ln_roots"), st.sem("ln_coefs"))
        self.scaled, self.tick = st.sem("ln_scaled"), st.sem("ln_tick")

    def dve_moments(self, dve, x, c, u):
        for j in range(J):
            last = self.nc.vector.bn_stats(self.stats[:, u, j, :], x[:, j, :])
        last.then_inc(self.halves, 1)
        dve.wait_ge(self.halves, c + 1)
        after(dve, self.coefs, c - 1)
        dve.sem_inc(self.tick, 1)
        for j in range(J):
            last = self.nc.vector.bn_aggr(self.mv[:, u, j, :], self.stats[:, u, j, :])
        last.then_inc(self.moments, 1)

    def act_root(self, act, c, u):
        act.wait_ge(self.moments, c + 1)
        after(act, self.scaled, c - 1)
        self.nc.scalar.activation(self.std[:, u, :], self.mv[:, u, :, 1], ACT.Sqrt,
                                  bias=self.k.eps_col[:]).then_inc(self.roots, 1)

    def dve_coefs(self, dve, c, u, used):
        dve.wait_ge(self.roots, c + 1)
        used()
        self.nc.vector.reciprocal(self.scale[:, u, :], self.std[:, u, :]).then_inc(self.scaled, 1)
        dve.wait_ge(self.scaled, c + 1)
        self.nc.vector.scalar_tensor_tensor(self.bias[:, u, :], self.mv[:, u, :, 0], -1.0, self.scale[:, u, :],
                                            ALU.mult, ALU.mult).then_inc(self.coefs, 1)

    def act_apply(self, act, h, x, c, u):
        act.wait_ge(self.coefs, c + 1)
        for j in range(J):
            last = self.nc.scalar.activation(h[:, j, :], x[:, j, :], ACT.Relu, bias=self.bias[:, u, j:j + 1],
                                             scale=self.scale[:, u, j:j + 1])
        return last


def rows_product(nc, out, lhsT, w, bias, k):
    for j in range(J):
        nc.tensor.matmul(out[:, j * D:(j + 1) * D], lhsT[:, j * P:(j + 1) * P], w[:], start=j == 0, stop=False,
                         skip_group_check=True)
    return nc.tensor.matmul(out[:], k.ones[0:1, :], bias, start=False, stop=True, skip_group_check=True)


def load_x(nc, sp, s, x, dst, c, sem):
    if isinstance(c, int) and c == s.chunks - 1:
        r0 = c * CH
        sp.dma_start(dst[0:s.tp], x[r0:s.N, :].rearrange("(p j) d -> p j d", j=J)).then_inc(sem, 16)
        sp.dma_start(dst[s.tp:P], x[0:(P - s.tp) * J, :].rearrange("(p j) d -> p j d", j=J)).then_inc(sem, 16)
    else:
        sp.dma_start(dst, rows(x, c)).then_inc(sem, 16)


def first_norm(nc, k, s, x, wv, bv, wo, bo, H, Y):
    with Stage(nc, "norm0") as st:
        norm = Norm(nc, st, k)
        xin = st.sb("xin", [P, 2, J, D])
        h = st.sb("h", [P, 2, J, D])
        hT = st.sb("hT", [P, 2, CH])
        y = st.sb("y", [P, 2, J, D])
        wv_sb, wo_sb, mean = st.sb("wv", [P, D]), st.sb("wo", [P, D]), st.sb("mean", [P, D])
        wvT, wmean, wc = st.sb("wvT", [P, D]), st.sb("wmean", [P, D]), st.sb("wc", [P, D])
        bv_sb, bo_sb = st.sb("bv", [P, 1]), st.sb("bo", [1, D])
        bias = st.sb("bias", [1, J, D])
        headi = st.sb("headi", [P, D], I32)
        psT = [st.ps(f"psT{i}", [P, CH]) for i in range(2)]
        psY = [st.ps(f"psY{i}", [P, CH]) for i in range(2)]
        psW = st.ps("psW", [P, 4, P])
        weights, prep, mixed, used = st.sem("weights"), st.sem("prep"), st.sem("mixed"), st.sem("used")
        xl = [st.sem(f"xl{i}") for i in range(2)]
        hs = [st.sem(f"hs{i}") for i in range(2)]
        ys = [st.sem(f"ys{i}") for i in range(2)]
        h_done, hT_ps, hT_sb, y_ps, y_sb = (st.sem("h_done"), st.sem("hT_ps"), st.sem("hT_sb"),
                                            st.sem("y_ps"), st.sem("y_sb"))
        n = s.chunks
        with st.run() as block:

            @block.sync
            def _(sp):
                for dst, src in ((wv_sb, wv[:, :]), (wo_sb, wo[:, :]), (bv_sb, column(bv)), (bo_sb, row(bo))):
                    sp.dma_start(dst[:], src).then_inc(weights, 16)

                def load(c, u):
                    after(sp, h_done, c - 1)
                    load_x(nc, sp, s, x, xin[:, u], c, xl[u])

                def store(c, u):
                    sp.wait_ge(h_done, c + 1)
                    sp.dma_start(rows(H, c), h[:, u]).then_inc(hs[u], 16)
                    sp.wait_ge(y_sb, c + 1)
                    sp.dma_start(rows(Y, c), y[:, u]).then_inc(ys[u], 16)
                each_lagged(sp, n, load, store)
                all_landed(sp, hs, n)
                all_landed(sp, ys, n)

            @block.gpsimd
            def _(pool):
                pool.iota(headi[:], [[-1, D]], base=D, channel_multiplier=1).then_inc(prep, 1)

            @block.vector
            def _(dve):
                dve.wait_ge(prep, 1)
                nc.vector.tensor_scalar(headi[:], headi[:], DH - 1, None, ALU.bitwise_and).then_inc(prep, 1)
                dve.wait_ge(prep, 2)
                nc.vector.tensor_copy(mean[:], headi[:]).then_inc(prep, 1)
                dve.wait_ge(prep, 3)
                nc.vector.tensor_scalar(mean[:], mean[:], 0.0, 1.0 / HEADS, ALU.is_equal, ALU.mult).then_inc(prep, 1)
                dve.wait_ge(mixed, 2)
                nc.vector.tensor_copy(wvT[:], psW[:, 0, :])
                nc.vector.tensor_copy(wmean[:], psW[:, 1, :]).then_inc(used, 1)
                dve.wait_ge(mixed, 4)
                nc.vector.tensor_tensor(wc[:], psW[:, 2, :], k.ident[:], ALU.add)
                for j in range(J):
                    last = nc.vector.tensor_tensor(bias[0:1, j, :], psW[0:1, 3, :], bo_sb[:], ALU.add)
                last.then_inc(used, 1)

                def stats(c, u):
                    if isinstance(c, int) and c == n - 1:
                        dve.wait_ge(xl[u], 16 * (n // 2 + 1))
                    else:
                        landed(dve, xl, c, u)
                    norm.dve_moments(dve, xin[:, u], c, u)
                    norm.dve_coefs(dve, c, u, lambda: after(dve, h_done, c - 1))

                def take(c, u):
                    dve.wait_ge(hT_ps, c + 1)
                    after(dve, y_ps, c - 1)
                    nc.vector.tensor_copy(hT[:, u, :], psT[u][:]).then_inc(hT_sb, 1)
                each_lagged(dve, n, stats, take)

            @block.scalar
            def _(act):
                def normed(c, u):
                    norm.act_root(act, c, u)
                    sent(act, hs, c, u)
                    after(act, hT_ps, c - 1)
                    norm.act_apply(act, h[:, u], xin[:, u], c, u).then_inc(h_done, 1)

                def take(c, u):
                    act.wait_ge(y_ps, c + 1)
                    sent(act, ys, c, u)
                    nc.scalar.copy(y[:, u].rearrange("p j d -> p (j d)"), psY[u][:]).then_inc(y_sb, 1)
                each_lagged(act, n, normed, take)

            @block.tensor
            def _(pe):
                pe.wait_ge(weights, 16 * 4)
                pe.wait_ge(prep, 4)
                nc.tensor.transpose(psW[:, 0, :], wv_sb[:], k.ident[:]).then_inc(mixed, 1)
                nc.tensor.matmul(psW[:, 1, :], mean[:], wo_sb[:], start=True, stop=True).then_inc(mixed, 1)
                pe.wait_ge(used, 1)
                nc.tensor.matmul(psW[:, 2, :], wvT[:], wmean[:], start=True, stop=True).then_inc(mixed, 1)
                nc.tensor.matmul(psW[0:1, 3, :], bv_sb[:], wmean[:], start=True, stop=True).then_inc(mixed, 1)
                pe.wait_ge(used, 2)

                def turn(c, u):
                    pe.wait_ge(h_done, c + 1)
                    after(pe, hT_sb, c - 1)
                    for j in range(J):
                        last = nc.tensor.transpose(psT[u][:, j * P:(j + 1) * P], h[:, u, j, :], k.ident[:])
                    last.then_inc(hT_ps, 1)

                def mix(c, u):
                    pe.wait_ge(hT_sb, c + 1)
                    after(pe, y_sb, c - 1)
                    rows_product(nc, psY[u], hT[:, u], wc, bias[:].rearrange("a j d -> a (j d)"), k).then_inc(y_ps, 1)
                each_lagged(pe, n, turn, mix)


def column(v):
    return v.rearrange("(p a) -> p a", a=1)


def row(v):
    return v.rearrange("(a p) -> a p", a=1)


def sum_neighbours(nc, k, s, plan, H, edges, carry):
    with Stage(nc, "sum0") as st:
        got_rows = st.sb("rows", [P, 2, J, D])
        idx = st.sb("idx", [P, 2, J], U32)
        psC = st.ps("psC", [P, D])
        idx_ready, chain, tick = st.sem("idx_ready"), st.sem("chain"), st.sem("tick")
        zeroed, carried, taken = st.sem("zeroed"), st.sem("carried"), st.sem("taken")
        got = [st.sem(f"got{i}") for i in range(2)]
        n = s.echunks
        with st.run() as block:

            @block.gpsimd
            def _(pool):
                bound = pool.to_reg(s.NP - 1)

                def gather(c, u):
                    pool.wait_ge(idx_ready, c + 1)
                    after(pool, chain, (c - 1) * J)
                    pool.sem_inc(tick, 1)
                    for q in range(J):
                        pool.indirect_dma_start(out=got_rows[:, u, q, :], out_offset=None, in_=H,
                                                in_offset=bass.IndirectOffsetOnAxis(ap=idx[:, u, q:q + 1], axis=0),
                                                bounds_check=bound, oob_is_err=False).then_inc(got[u], 16)
                each(pool, n, gather)

            @block.scalar
            def _(act):
                def index(c, u):
                    sent(act, got, c, u, J)
                    nc.scalar.copy(idx[:, u, :], plan.other[:, bass.ds(c * J, J)]).then_inc(idx_ready, 1)
                each(act, n, index)

            @block.vector
            def _(dve):
                ch = Chain(dve, chain, J)
                nc.vector.memset(edges[:, 0:D], 0.0).then_inc(zeroed, 1)
                dve.wait_ge(zeroed, 1)

                def add(c, u):
                    landed(dve, got, c, u, J)
                    ch.step(c)
                    for q in range(J):
                        ch.link(nc.vector.scalar_tensor_tensor(
                            edges[:, bass.ds((c * J + q + 1) * D, D)], edges[:, bass.ds((c * J + q) * D, D)],
                            plan.same[:, bass.ds(c * J + q, 1)], got_rows[:, u, q, :], ALU.mult, ALU.add))
                each(dve, n, add)
                dve.wait_ge(carried, 1)
                nc.vector.tensor_copy(carry[:], psC[:]).then_inc(taken, 1)
                dve.wait_ge(taken, 1)

            @block.tensor
            def _(pe):
                pe.wait_ge(chain, n * J)
                nc.tensor.matmul(psC[:], plan.carry[:], edges[:, s.T * D:], start=True, stop=True).then_inc(carried, 1)


def attend(nc, k, s, plan, L0, H, Y, edges, carry):
    R = 4
    with Stage(nc, "attend") as st:
        hs = st.sb("hs", [P, R, D])
        y = st.sb("y", [P, R, D])
        gidx, sidx = st.sb("gidx", [P, R], U32), st.sb("sidx", [P, R], U32)
        kin, kmean = st.sb("kin", [P, R, D]), st.sb("kmean", [P, R, D])
        turned = st.sb("turned", [P, 2, 2 * D])
        qvk = st.sb("qvk", [P, R, 3 * D])
        prod = st.sb("prod", [P, 1024])
        score, shifted, expd, prob = (st.sb("score", [P, 2, 64]), st.sb("shifted", [P, 2, 64]),
                                      st.sb("expd", [P, R, 64]), st.sb("prob", [P, 2, 64]))
        top, total, inv = st.sb("top", [P, 2, HEADS]), st.sb("total", [P, 2, HEADS]), st.sb("inv", [P, 2, HEADS])
        prod2 = st.sb("prod2", [P, 1024])
        mixed, mixedT = st.sb("mixed", [P, R, D]), st.sb("mixedT", [P, 2, D])
        wqv, wk, wo = st.sb("wqv", [P, 2 * D]), st.sb("wk", [P, D]), st.sb("wo", [P, D])
        bias, bo = st.sb("bias", [1, 3 * D]), st.sb("bo", [1, D])
        psT = [st.ps(f"psT{i}", [P, 2 * D]) for i in range(2)]
        psQ = [st.ps(f"psQ{i}", [P, 3 * D]) for i in range(2)]
        psM = st.ps("psM", [P, D])
        psO = [st.ps(f"psO{i}", [P, D]) for i in range(2)]
        weights, tick = st.sem("weights"), st.sem("tick")
        got = [st.sem(f"got{i}") for i in range(R)]
        put = [st.sem(f"put{i}") for i in range(R)]
        (gidx_ready, sidx_ready, kin_done, kmean_done, T_ps, T_sb, q_ps, q_sb) = (
            st.sem(x) for x in ("gidx_ready", "sidx_ready", "kin_done", "kmean_done", "T_ps", "T_sb", "q_ps", "q_sb"))
        chain, score_done, exp_done, mix_done, m_ps, m_sb, o_ps, y_done = (
            st.sem(x) for x in ("chain", "score_done", "exp_done", "mix_done", "m_ps", "m_sb", "o_ps", "y_done"))
        chain2 = st.sem("chain2")
        n = s.T
        with st.run() as block:

            @block.sync
            def _(sp):
                for dst, src in ((wqv[:, 0:D], L0["wq"][:, :]), (wqv[:, D:2 * D], L0["wv"][:, :]), (wk[:], L0["wk"][:, :]),
                                 (wo[:], L0["wo"][:, :]), (bias[:, 0:D], row(L0["bq"])), (bias[:, D:2 * D], row(L0["bv"])),
                                 (bias[:, 2 * D:3 * D], row(L0["bk"])), (bo[:], row(L0["bo"]))):
                    sp.dma_start(dst, src).then_inc(weights, 16)

            @block.gpsimd
            def _(pool):
                bound = pool.to_reg(s.N - 1)

                def gather(t, u):
                    pool.wait_ge(gidx_ready, t + 1)
                    after(pool, y_done, t - R + 1)
                    pool.sem_inc(tick, 1)
                    pool.indirect_dma_start(out=hs[:, u, :], out_offset=None, in_=H,
                                            in_offset=bass.IndirectOffsetOnAxis(ap=gidx[:, u:u + 1], axis=0),
                                            bounds_check=bound, oob_is_err=False).then_inc(got[u], 16)

                def scatter(t, u):
                    pool.wait_ge(y_done, t + 1)
                    pool.wait_ge(sidx_ready, t + 1)
                    pool.sem_inc(tick, 1)
                    pool.indirect_dma_start(out=Y, out_offset=bass.IndirectOffsetOnAxis(ap=sidx[:, u:u + 1], axis=0),
                                            in_=y[:, u, :], in_offset=None, bounds_check=bound,
                                            oob_is_err=False).then_inc(put[u], 16)
                each_phases(pool, n, [gather, None, None, None, scatter], R)
                all_landed(pool, put, n)

            @block.vector
            def _(dve):
                ch, ch2 = Chain(dve, chain, 3), Chain(dve, chain2, 4)

                def keys(t, u):
                    after(dve, kmean_done, t - R + 1)
                    nc.vector.scalar_tensor_tensor(kin[:, u, :], carry[:], plan.first[:, bass.ds(t, 1)],
                                                   edges[:, bass.ds((t + 1) * D, D)], ALU.mult, ALU.add).then_inc(kin_done, 1)

                def scores(t, u):
                    dve.wait_ge(q_sb, t + 1)
                    v = u % 2
                    q4 = qvk[:, u, 0:D].rearrange("p (h a d) -> p h a d", h=HEADS, a=1).broadcast_to([P, HEADS, HEADS, DH])
                    k4 = qvk[:, u, 2 * D:3 * D].rearrange("p (a g d) -> p a g d", a=1, g=HEADS).broadcast_to([P, HEADS, HEADS, DH])
                    ch.step(t)
                    ch.link(nc.vector.tensor_tensor(prod[:].rearrange("p (h g d) -> p h g d", h=HEADS, g=HEADS), q4, k4, ALU.mult))
                    ch.link(nc.vector.tensor_reduce(score[:, v, :], prod[:].rearrange("p (a d) -> p a d", d=DH), AX.X, ALU.add))
                    s3 = score[:, v, :].rearrange("p (h g) -> p h g", h=HEADS)
                    ch.link(nc.vector.tensor_reduce(top[:, v, :], s3, AX.X, ALU.max))
                    after(dve, exp_done, t - 1)
                    nc.vector.tensor_tensor(shifted[:, v, :].rearrange("p (h g) -> p h g", h=HEADS), s3,
                                            top[:, v, :].rearrange("p (h a) -> p h a", a=1).broadcast_to([P, HEADS, HEADS]),
                                            ALU.subtract).then_inc(score_done, 1)

                def mix(t, u):
                    dve.wait_ge(exp_done, t + 1)
                    v = u % 2
                    e3 = expd[:, u, :].rearrange("p (h g) -> p h g", h=HEADS)
                    ch2.step(t)
                    ch2.link(nc.vector.tensor_reduce(total[:, v, :], e3, AX.X, ALU.add))
                    ch2.link(nc.vector.reciprocal(inv[:, v, :], total[:, v, :]))
                    ch2.link(nc.vector.tensor_tensor(prob[:, v, :].rearrange("p (h g) -> p h g", h=HEADS), e3,
                                                     inv[:, v, :].rearrange("p (h a) -> p h a", a=1).broadcast_to([P, HEADS, HEADS]), ALU.mult))
                    p4 = prob[:, v, :].rearrange("p (h a g) -> p h a g", h=HEADS, a=1).broadcast_to([P, HEADS, DH, HEADS])
                    v4 = qvk[:, u, D:2 * D].rearrange("p (a g d) -> p a d g", a=1, g=HEADS).broadcast_to([P, HEADS, DH, HEADS])
                    ch2.link(nc.vector.tensor_tensor(prod2[:].rearrange("p (h d g) -> p h d g", h=HEADS, d=DH), p4, v4, ALU.mult))
                    after(dve, m_ps, t - R + 1)
                    nc.vector.tensor_reduce(mixed[:, u, :], prod2[:].rearrange("p (a g) -> p a g", g=HEADS), AX.X, ALU.add).then_inc(mix_done, 1)

                def result(t, u):
                    dve.wait_ge(o_ps, t + 1)
                    sent(dve, put, t, u)
                    nc.vector.tensor_tensor(y[:, u, :], psO[u % 2][:], hs[:, u, :], ALU.add).then_inc(y_done, 1)
                each_phases(dve, n, [None, keys, scores, mix, result], R)

            @block.scalar
            def _(act):
                def index(t, u):
                    sent(act, got, t, u)
                    nc.scalar.copy(gidx[:, u:u + 1], plan.key[:, bass.ds(t, 1)]).then_inc(gidx_ready, 1)

                def project(t, u):
                    act.wait_ge(kin_done, t + 1)
                    after(act, T_ps, t - R + 1)
                    nc.scalar.mul(kmean[:, u, :], kin[:, u, :], plan.inv[:, bass.ds(t, 1)]).then_inc(kmean_done, 1)
                    act.wait_ge(T_ps, t + 1)
                    after(act, q_ps, t - 1)
                    nc.scalar.copy(turned[:, u % 2, :], psT[u % 2][:]).then_inc(T_sb, 1)
                    act.wait_ge(q_ps, t + 1)
                    after(act, mix_done, t - R + 1)
                    nc.scalar.copy(qvk[:, u, :], psQ[u % 2][:]).then_inc(q_sb, 1)

                def exps(t, u):
                    act.wait_ge(score_done, t + 1)
                    after(act, mix_done, t - R + 1)
                    nc.scalar.activation(expd[:, u, :], shifted[:, u % 2, :], ACT.Exp).then_inc(exp_done, 1)

                def turn(t, u):
                    act.wait_ge(m_ps, t + 1)
                    after(act, o_ps, t - 1)
                    nc.scalar.copy(mixedT[:, u % 2, :], psM[:]).then_inc(m_sb, 1)
                    sent(act, put, t, u)
                    nc.scalar.copy(sidx[:, u:u + 1], plan.last[:, bass.ds(t, 1)]).then_inc(sidx_ready, 1)
                each_phases(act, n, [index, project, exps, turn], R)

            @block.tensor
            def _(pe):
                pe.wait_ge(weights, 16 * 8)

                def project(t, u):
                    v = u % 2
                    pe.wait_ge(kmean_done, t + 1)
                    landed(pe, got, t, u)
                    after(pe, T_sb, t - 1)
                    nc.tensor.transpose(psT[v][:, 0:D], kmean[:, u, :], k.ident[:])
                    nc.tensor.transpose(psT[v][:, D:2 * D], hs[:, u, :], k.ident[:]).then_inc(T_ps, 1)
                    pe.wait_ge(T_sb, t + 1)
                    after(pe, q_sb, t - 1)
                    nc.tensor.matmul(psQ[v][:, 0:2 * D], turned[:, v, D:2 * D], wqv[:], start=True, stop=False, skip_group_check=True)
                    nc.tensor.matmul(psQ[v][:, 2 * D:3 * D], turned[:, v, 0:D], wk[:], start=False, stop=False, skip_group_check=True)
                    nc.tensor.matmul(psQ[v][:], k.ones[0:1, :], bias[:], start=False, stop=True, skip_group_check=True).then_inc(q_ps, 1)

                def out(t, u):
                    v = u % 2
                    pe.wait_ge(mix_done, t + 1)
                    after(pe, m_sb, t)
                    nc.tensor.transpose(psM[:], mixed[:, u, :], k.ident[:]).then_inc(m_ps, 1)
                    pe.wait_ge(m_sb, t + 1)
                    after(pe, y_done, t - 1)
                    nc.tensor.matmul(psO[v][:], mixedT[:, v, :], wo[:], start=True, stop=False)
                    nc.tensor.matmul(psO[v][:], k.ones[0:1, :], bo[:], start=False, stop=True).then_inc(o_ps, 1)
                each_phases(pe, n, [None, project, None, out], R)


def batch_coefs(nc, dve, act_ready, ch, k, gain, shift, mean, var, std, scale, offset):
    dve.wait_ge(act_ready, 1)
    ch.link(nc.vector.reciprocal(scale[:], std[:]))
    ch.link(nc.vector.tensor_tensor(scale[:], scale[:], gain[:], ALU.mult))
    ch.link(nc.vector.tensor_tensor(offset[:], mean, scale[:], ALU.mult))
    ch.link(nc.vector.tensor_tensor(offset[:], shift[:], offset[:], ALU.subtract))


def node_moments(nc, k, s, Y, g1, be1, scale, offset):
    with Stage(nc, "moments") as st:
        y = st.sb("y", [P, 2, J, D])
        sq = st.sb("sq", [P, 2, J, D])
        acc = st.sb("acc", [P, J, D])
        acc2 = st.sb("acc2", [P, J, D])
        gain, shift = st.sb("gain", [P, 1]), st.sb("shift", [P, 1])
        mean, second, var, std = (st.sb(x, [P, 1]) for x in ("mean", "second", "var", "std"))
        psS = st.ps("psS", [P, 2])
        weights, zeroed, zeroed2 = st.sem("weights"), st.sem("zeroed"), st.sem("zeroed2")
        yl = [st.sem(f"yl{i}") for i in range(2)]
        added, squared, added2, folded, chain, root, var_done = (
            st.sem(x) for x in ("added", "squared", "added2", "folded", "chain", "root", "var_done"))
        n = s.chunks
        with st.run() as block:

            def live(buf, c, u):
                last = isinstance(c, int) and c == n - 1
                return buf[0:s.tp if last else P, u] if u is not None else buf[0:s.tp if last else P]

            @block.sync
            def _(sp):
                sp.dma_start(gain[:], column(g1)).then_inc(weights, 16)
                sp.dma_start(shift[:], column(be1)).then_inc(weights, 16)

                def load(c, u):
                    after(sp, added, c - 1)
                    after(sp, squared, c - 1)
                    sp.dma_start(y[:, u], rows(Y, c)).then_inc(yl[u], 16)
                each(sp, n, load)

            @block.vector
            def _(dve):
                nc.vector.memset(acc[:], 0.0).then_inc(zeroed, 1)
                dve.wait_ge(zeroed, 1)

                def add(c, u):
                    landed(dve, yl, c, u)
                    nc.vector.tensor_tensor(live(acc, c, None), live(acc, c, None), live(y, c, u), ALU.add).then_inc(added, 1)
                    dve.wait_ge(added, c + 1)
                each(dve, n, add)
                ch = Chain(dve, chain, 99)
                dve.wait_ge(folded, 1)
                ch.link(nc.vector.tensor_scalar(mean[:], psS[:, 0:1], 1.0 / s.N, None, ALU.mult))
                ch.link(nc.vector.tensor_scalar(second[:], psS[:, 1:2], 1.0 / s.N, None, ALU.mult))
                ch.link(nc.vector.tensor_tensor(var[:], mean[:], mean[:], ALU.mult))
                nc.vector.tensor_tensor(var[:], second[:], var[:], ALU.subtract).then_inc(var_done, 1)
                dve.wait_ge(weights, 32)
                batch_coefs(nc, dve, root, ch, k, gain, shift, mean[:], var, std, scale, offset)

            @block.scalar
            def _(act):
                def square(c, u):
                    landed(act, yl, c, u)
                    after(act, added2, c - 1)
                    nc.scalar.activation(sq[:, u], y[:, u], ACT.Square).then_inc(squared, 1)
                each(act, n, square)
                act.wait_ge(var_done, 1)
                nc.scalar.activation(std[:], var[:], ACT.Sqrt, bias=k.eps_col[:]).then_inc(root, 1)

            @block.gpsimd
            def _(pool):
                pool.memset(acc2[:], 0.0).then_inc(zeroed2, 1)
                pool.wait_ge(zeroed2, 1)

                def add(c, u):
                    pool.wait_ge(squared, c + 1)
                    nc.gpsimd.tensor_tensor(live(acc2, c, None), live(acc2, c, None), live(sq, c, u), ALU.add).then_inc(added2, 1)
                    pool.wait_ge(added2, c + 1)
                each(pool, n, add)

            @block.tensor
            def _(pe):
                for a, (src, done) in enumerate(((acc, added), (acc2, added2))):
                    pe.wait_ge(done, n)
                    for j in range(J):
                        last = nc.tensor.matmul(psS[:, a:a + 1], src[:, j, :], k.ones[:, 0:1], start=j == 0, stop=j == J - 1)
                last.then_inc(folded, 1)


def node_mlp(nc, k, s, L0, Y, U, scale, offset, scale2, offset2):
    M = HID // P
    with Stage(nc, "mlp") as st:
        y = st.sb("y", [P, 2, J, D])
        t = st.sb("t", [P, 2, CH])
        g = st.sb("g", [P, 2, M, CH])
        u_sb = st.sb("u", [P, 2, CH])
        w1, w2 = st.sb("w1", [P, HID]), st.sb("w2", [P, M, D])
        b1, b2 = st.sb("b1", [P, M]), st.sb("b2", [P, 1])
        gain, shift, std = st.sb("gain", [P, 1]), st.sb("shift", [P, 1]), st.sb("std", [P, 1])
        stats, mv = st.sb("stats", [P, s.chunks, 6]), st.sb("mv", [P, 2])
        psT = [st.ps("psT0", [P, CH])]
        psG = [st.ps(f"psG{i}", [P, CH]) for i in range(M)]
        psU = [st.ps(f"psU{i}", [P, CH]) for i in range(2)]
        weights = st.sem("weights")
        yl = [st.sem(f"yl{i}") for i in range(2)]
        us = [st.sem(f"us{i}") for i in range(2)]
        T_ps, T_sb, G_ps, G_sb, U_ps, U_sb, stat, moments, root, chain = (
            st.sem(x) for x in ("T_ps", "T_sb", "G_ps", "G_sb", "U_ps", "U_sb", "stat", "moments", "root", "chain"))
        n = s.chunks
        with st.run() as block:

            @block.sync
            def _(sp):
                with nc.allow_non_contiguous_dma("biases as columns"):
                    for dst, src in ((w1[:], L0["w1"][:, :]), (w2[:], L0["w2"].rearrange("(m p) d -> p m d", p=P)),
                                     (b1[:], L0["b1"].rearrange("(m p) -> p m", p=P)), (b2[:], column(L0["b2"])),
                                     (gain[:], column(L0["g2"])), (shift[:], column(L0["be2"]))):
                        sp.dma_start(dst, src).then_inc(weights, 16)

                def load(c, u):
                    after(sp, T_ps, c - 1)
                    sp.dma_start(y[:, u], rows(Y, c)).then_inc(yl[u], 16)

                def store(c, u):
                    sp.wait_ge(U_sb, c + 1)
                    sp.dma_start(U[bass.ds(c * P, P), :], u_sb[:, u, :]).then_inc(us[u], 16)
                each_phases(sp, n, [load, None, store])
                all_landed(sp, us, n)

            @block.tensor
            def _(pe):
                pe.wait_ge(weights, 16 * 6)

                def turn(c, u):
                    landed(pe, yl, c, u)
                    after(pe, T_sb, c)
                    for j in range(J):
                        last = nc.tensor.transpose(psT[0][:, j * P:(j + 1) * P], y[:, u, j, :], k.ident[:])
                    last.then_inc(T_ps, 1)

                def up(c, u):
                    pe.wait_ge(T_sb, c + 1)
                    for m in range(M):
                        after(pe, G_sb, M * (c - 1) + m + 1)
                        nc.tensor.matmul(psG[m][:], w1[:, m * P:(m + 1) * P], t[:, u, :], start=True, stop=True).then_inc(G_ps, 1)

                def down(c, u):
                    after(pe, U_sb, c - 1)
                    for m in range(M):
                        pe.wait_ge(G_sb, M * c + m + 1)
                        last = nc.tensor.matmul(psU[u][:], w2[:, m, :], g[:, u, m, :], start=m == 0, stop=m == M - 1)
                    last.then_inc(U_ps, 1)

                def step(c, u):
                    up(c, u)
                    if not (isinstance(c, int) and c == n - 1):
                        turn(c + 1, 1 - u)
                turn(0, 0)
                each_lagged(pe, n, step, down)

            @block.scalar
            def _(act):
                act.wait_ge(weights, 16 * 6)

                def turn(c, u):
                    act.wait_ge(T_ps, c + 1)
                    after(act, U_sb, c - 1)
                    nc.scalar.activation(t[:, u, :], psT[0][:], ACT.Identity, bias=offset[:], scale=scale[:]).then_inc(T_sb, 1)

                def step(c, u):
                    after(act, U_ps, c - 1)
                    for m in range(M):
                        act.wait_ge(G_ps, M * c + m + 1)
                        nc.scalar.activation(g[:, u, m, :], psG[m][:], ACT.Gelu, bias=b1[:, m:m + 1]).then_inc(G_sb, 1)
                    if not (isinstance(c, int) and c == n - 1):
                        turn(c + 1, 1 - u)
                turn(0, 0)
                each(act, n, step)
                act.wait_ge(moments, 1)
                nc.scalar.activation(std[:], mv[:, 1:2], ACT.Sqrt, bias=k.eps_col[:]).then_inc(root, 1)

            @block.vector
            def _(dve):
                dve.wait_ge(weights, 16 * 6)

                def finish(c, u):
                    dve.wait_ge(U_ps, c + 1)
                    sent(dve, us, c, u)
                    nc.vector.scalar_tensor_tensor(u_sb[:, u, :], psU[u][:], b2[:], t[:, u, :], ALU.add, ALU.add).then_inc(U_sb, 1)
                    dve.wait_ge(U_sb, c + 1)
                    out = stats[:].rearrange("p c x -> p (c x)")[:, bass.ds(c * 6, 6)]
                    real = u_sb[:, u, :]
                    if isinstance(c, int) and c == n - 1:
                        real = real.rearrange("f (j p) -> f j p", j=J)[:, :, 0:s.tp]
                    nc.vector.bn_stats(out, real).then_inc(stat, 1)
                each(dve, n, finish)
                dve.wait_ge(stat, n)
                nc.vector.bn_aggr(mv[:], stats[:].rearrange("p c x -> p (c x)")).then_inc(moments, 1)
                ch = Chain(dve, chain, 99)
                batch_coefs(nc, dve, root, ch, k, gain, shift, mv[:, 0:1], None, std, scale2, offset2)


def second_norm(nc, k, s, x, U, X, H, scale2, offset2):
    with Stage(nc, "norm1") as st:
        norm = Norm(nc, st, k)
        uin, z = st.sb("uin", [P, 2, CH]), st.sb("z", [P, 2, CH])
        xin, x1, h = (st.sb(v, [P, 2, J, D]) for v in ("xin", "x1", "h"))
        psZ = [st.ps(f"psZ{i}", [P, CH]) for i in range(2)]
        ul, xl, xs, hs = ([st.sem(f"{v}{i}") for i in range(2)] for v in ("ul", "xl", "xs", "hs"))
        z_done, z_ps, x_done, h_done = (st.sem(v) for v in ("z_done", "z_ps", "x_done", "h_done"))
        n = s.chunks
        with st.run() as block:

            @block.sync
            def _(sp):
                def load(c, u):
                    after(sp, z_done, c - 1)
                    sp.dma_start(uin[:, u, :], U[bass.ds(c * P, P), :]).then_inc(ul[u], 16)
                    after(sp, x_done, c - 1)
                    load_x(nc, sp, s, x, xin[:, u], c, xl[u])

                def store(c, u):
                    sp.wait_ge(x_done, c + 1)
                    sp.dma_start(rows(X, c), x1[:, u]).then_inc(xs[u], 16)
                    sp.wait_ge(h_done, c + 1)
                    sp.dma_start(rows(H, c), h[:, u]).then_inc(hs[u], 16)
                each_lagged(sp, n, load, store)
                all_landed(sp, xs, n)
                all_landed(sp, hs, n)

            @block.scalar
            def _(act):
                def scaled(c, u):
                    landed(act, ul, c, u)
                    after(act, z_ps, c - 1)
                    nc.scalar.activation(z[:, u, :], uin[:, u, :], ACT.Identity, bias=offset2[:], scale=scale2[:]).then_inc(z_done, 1)

                def normed(c, u):
                    norm.act_root(act, c, u)
                    sent(act, hs, c, u)
                    norm.act_apply(act, h[:, u], x1[:, u], c, u).then_inc(h_done, 1)
                each_lagged(act, n, scaled, normed)

            @block.tensor
            def _(pe):
                def turn(c, u):
                    pe.wait_ge(z_done, c + 1)
                    after(pe, x_done, c - 1)
                    for j in range(J):
                        last = nc.tensor.transpose(psZ[u][:, j * D:(j + 1) * D], z[:, u, j * P:(j + 1) * P], k.ident[:])
                    last.then_inc(z_ps, 1)
                each(pe, n, turn)

            @block.vector
            def _(dve):
                def add(c, u):
                    if isinstance(c, int) and c == n - 1:
                        dve.wait_ge(xl[u], 16 * (n // 2 + 1))
                    else:
                        landed(dve, xl, c, u)
                    dve.wait_ge(z_ps, c + 1)
                    sent(dve, xs, c, u)
                    after(dve, h_done, c - 1)
                    flat = x1[:, u].rearrange("p j d -> p (j d)")
                    nc.vector.tensor_tensor(flat, psZ[u][:], xin[:, u].rearrange("p j d -> p (j d)"), ALU.add).then_inc(x_done, 1)
                    dve.wait_ge(x_done, c + 1)
                    norm.dve_moments(dve, x1[:, u], c, u)
                    norm.dve_coefs(dve, c, u, lambda: after(dve, h_done, c - 1))
                each(dve, n, add)


def gather_rows(pool, dst, table, idx, bound, sem):
    pool.indirect_dma_start(out=dst, out_offset=None, in_=table,
                            in_offset=bass.IndirectOffsetOnAxis(ap=idx, axis=0),
                            bounds_check=bound, oob_is_err=False).then_inc(sem, 16)


def scatter_rows(pool, table, src, idx, bound, sem):
    pool.indirect_dma_start(out=table, out_offset=bass.IndirectOffsetOnAxis(ap=idx, axis=0),
                            in_=src, in_offset=None, bounds_check=bound, oob_is_err=False).then_inc(sem, 16)


def zero_table(nc, s, S):
    parts = 14
    width = s.NP * D // P // parts
    with Stage(nc, "zero") as st:
        z = st.sb("z", [P, width])
        made, stored = st.sem("made"), st.sem("stored")
        flat = S.rearrange("(p r) d -> p (r d)", p=P)
        with st.run() as block:

            @block.vector
            def _(dve):
                nc.vector.memset(z[:], 0.0).then_inc(made, 1)

            @block.sync
            def _(sp):
                sp.wait_ge(made, 1)
                for i in range(parts):
                    sp.dma_start(flat[:, i * width:(i + 1) * width], z[:]).then_inc(stored, 16)
                sp.wait_ge(stored, 16 * parts)


def edge_messages(nc, k, s, plan, L1, H, edges, carry):
    with Stage(nc, "edge1") as st:
        got_rows = st.sb("rows", [P, 2, 2, J, D])
        idx = st.sb("idx", [P, 2, 2, J], U32)
        turned = st.sb("turned", [P, 2, 2, CH])
        m = st.sb("m", [P, 2, CH])
        ws, wd, b = st.sb("ws", [P, D]), st.sb("wd", [P, D]), st.sb("b", [P, 1])
        psS = [st.ps(f"psS{i}", [P, CH]) for i in range(2)]
        psD = [st.ps(f"psD{i}", [P, CH]) for i in range(2)]
        psM = [st.ps(f"psM{i}", [P, CH]) for i in range(2)]
        psR = [st.ps(f"psR{i}", [P, CH]) for i in range(2)]
        got = [st.sem(f"got{i}") for i in range(2)]
        weights, idx_ready, tick, T_ps, S_sb, D_sb, M_ps, M_sb, R_ps, chain, zeroed, carried, taken = (
            st.sem(v) for v in ("weights", "idx_ready", "tick", "T_ps", "S_sb", "D_sb", "M_ps", "M_sb", "R_ps",
                                "chain", "zeroed", "carried", "taken"))
        n = s.echunks
        with st.run() as block:

            @block.sync
            def _(sp):
                sp.dma_start(ws[:], L1["W_edge"][0:D, :]).then_inc(weights, 16)
                sp.dma_start(wd[:], L1["W_edge"][D:2 * D, :]).then_inc(weights, 16)
                sp.dma_start(b[:], column(L1["b_edge"])).then_inc(weights, 16)

            @block.gpsimd
            def _(pool):
                bound = pool.to_reg(s.N - 1)

                def gather(c, u):
                    pool.wait_ge(idx_ready, c + 1)
                    after(pool, T_ps, c - 1)
                    pool.sem_inc(tick, 1)
                    for side in range(2):
                        for q in range(J):
                            gather_rows(pool, got_rows[:, u, side, q, :], H, idx[:, u, side, q:q + 1], bound, got[u])
                each(pool, n, gather)

            @block.scalar
            def _(act):
                act.wait_ge(weights, 48)

                def index(c, u):
                    sent(act, got, c, u, 2 * J)
                    nc.scalar.copy(idx[:, u, 0, :], plan.other[:, bass.ds(c * J, J)])
                    nc.scalar.copy(idx[:, u, 1, :], plan.key[:, bass.ds(c * J, J)]).then_inc(idx_ready, 1)

                def take(c, u):
                    act.wait_ge(T_ps, c + 1)
                    after(act, M_ps, c - 1)
                    nc.scalar.copy(turned[:, u, 0, :], psS[u][:]).then_inc(S_sb, 1)

                def relu(c, u):
                    act.wait_ge(M_ps, c + 1)
                    after(act, R_ps, c - 1)
                    nc.scalar.activation(m[:, u, :], psM[u][:], ACT.Relu, bias=b[:]).then_inc(M_sb, 1)
                each_phases(act, n, [index, take, relu])

            @block.vector
            def _(dve):
                ch = Chain(dve, chain, J)
                nc.vector.memset(edges[:, 0:D], 0.0).then_inc(zeroed, 1)
                dve.wait_ge(zeroed, 1)

                def take(c, u):
                    dve.wait_ge(T_ps, c + 1)
                    after(dve, M_ps, c - 1)
                    nc.vector.tensor_copy(turned[:, u, 1, :], psD[u][:]).then_inc(D_sb, 1)

                def add(c, u):
                    dve.wait_ge(R_ps, c + 1)
                    ch.step(c)
                    for q in range(J):
                        ch.link(nc.vector.scalar_tensor_tensor(
                            edges[:, bass.ds((c * J + q + 1) * D, D)], edges[:, bass.ds((c * J + q) * D, D)],
                            plan.same[:, bass.ds(c * J + q, 1)], psR[u][:, q * D:(q + 1) * D], ALU.mult, ALU.add))
                each_phases(dve, n, [None, take, None, add])
                dve.wait_ge(carried, 1)
                nc.vector.tensor_copy(carry[:], psM[0][:, 0:D]).then_inc(taken, 1)
                dve.wait_ge(taken, 1)

            @block.tensor
            def _(pe):
                pe.wait_ge(weights, 48)

                def turn(c, u):
                    landed(pe, got, c, u, 2 * J)
                    after(pe, S_sb, c - 1)
                    after(pe, D_sb, c - 1)
                    for side, ps in ((0, psS), (1, psD)):
                        for q in range(J):
                            last = nc.tensor.transpose(ps[u][:, q * P:(q + 1) * P], got_rows[:, u, side, q, :], k.ident[:])
                    last.then_inc(T_ps, 1)

                def mix(c, u):
                    pe.wait_ge(S_sb, c + 1)
                    pe.wait_ge(D_sb, c + 1)
                    after(pe, M_sb, c - 1)
                    nc.tensor.matmul(psM[u][:], ws[:], turned[:, u, 0, :], start=True, stop=False)
                    nc.tensor.matmul(psM[u][:], wd[:], turned[:, u, 1, :], start=False, stop=True).then_inc(M_ps, 1)

                def back(c, u):
                    pe.wait_ge(M_sb, c + 1)
                    after(pe, chain, (c - 1) * J)
                    for q in range(J):
                        last = nc.tensor.transpose(psR[u][:, q * D:(q + 1) * D], m[:, u, q * P:(q + 1) * P], k.ident[:])
                    last.then_inc(R_ps, 1)
                each_phases(pe, n, [None, turn, mix, back])
                pe.wait_ge(chain, n * J)
                nc.tensor.matmul(psM[0][:, 0:D], plan.carry[:], edges[:, s.T * D:], start=True, stop=True).then_inc(carried, 1)


def scatter_sums(nc, s, plan, S, edges, carry, name):
    R = 4
    with Stage(nc, name) as st:
        y, idx = st.sb("y", [P, R, D]), st.sb("idx", [P, R], U32)
        put = [st.sem(f"put{i}") for i in range(R)]
        y_done, idx_ready, tick = st.sem("y_done"), st.sem("idx_ready"), st.sem("tick")
        n = s.T
        with st.run() as block:

            @block.vector
            def _(dve):
                def total(t, u):
                    sent(dve, put, t, u)
                    nc.vector.scalar_tensor_tensor(y[:, u, :], carry[:], plan.first[:, bass.ds(t, 1)],
                                                   edges[:, bass.ds((t + 1) * D, D)], ALU.mult, ALU.add).then_inc(y_done, 1)
                each(dve, n, total, R)

            @block.scalar
            def _(act):
                def index(t, u):
                    sent(act, put, t, u)
                    nc.scalar.copy(idx[:, u:u + 1], plan.last[:, bass.ds(t, 1)]).then_inc(idx_ready, 1)
                each(act, n, index, R)

            @block.gpsimd
            def _(pool):
                bound = pool.to_reg(s.N - 1)

                def scatter(t, u):
                    pool.wait_ge(idx_ready, t + 1)
                    pool.wait_ge(y_done, t + 1)
                    pool.sem_inc(tick, 1)
                    scatter_rows(pool, S, y[:, u, :], idx[:, u:u + 1], bound, put[u])
                each(pool, n, scatter, R)
                all_landed(pool, put, n)


def node_update(nc, k, s, L1, X, H, S):
    with Stage(nc, "node1") as st:
        norm = Norm(nc, st, k)
        xin, hin, sin, rst, x2, h2 = (st.sb(v, [P, 2, J, D]) for v in ("xin", "hin", "sin", "rst", "x2", "h2"))
        rT, a_sb = st.sb("rT", [P, 2, CH]), st.sb("a", [P, 2, CH])
        w1, w2, b1 = st.sb("w1", [P, D]), st.sb("w2", [P, D]), st.sb("b1", [P, 1])
        bias, eps1 = st.sb("bias", [1, J, D]), st.sb("eps1", [P, 1])
        psT = [st.ps(f"psT{i}", [P, CH]) for i in range(2)]
        psA = [st.ps(f"psA{i}", [P, CH]) for i in range(2)]
        psB = [st.ps(f"psB{i}", [P, CH]) for i in range(2)]
        xl, hl, xs, hs = ([st.sem(f"{v}{i}") for i in range(2)] for v in ("xl", "hl", "xs", "hs"))
        weights, eps_done, r_done, T_ps, T_sb, A_ps, A_sb, B_ps, x_done, h_done = (
            st.sem(v) for v in ("weights", "eps_done", "r_done", "T_ps", "T_sb", "A_ps", "A_sb", "B_ps", "x_done", "h_done"))
        n = s.chunks
        with st.run() as block:

            @block.sync
            def _(sp):
                for j in range(J):
                    sp.dma_start(bias[:, j, :], row(L1["b2"])).then_inc(weights, 16)
                sp.dma_start(w1[:], L1["W1"][:, :]).then_inc(weights, 16)
                sp.dma_start(w2[:], L1["W2"][:, :]).then_inc(weights, 16)
                sp.dma_start(b1[:], column(L1["b1"])).then_inc(weights, 16)
                sp.dma_start(eps1[:], L1["eps"].rearrange("(a b) -> a b", a=1).broadcast_to([P, 1])).then_inc(weights, 16)

                def load(c, u):
                    after(sp, r_done, c - 1)
                    sp.dma_start(hin[:, u], rows(H, c)).then_inc(hl[u], 16)
                    sp.dma_start(sin[:, u], rows(S, c)).then_inc(hl[u], 16)

                def load2(c, u):
                    after(sp, x_done, c - 1)
                    sp.dma_start(xin[:, u], rows(X, c)).then_inc(xl[u], 16)

                def store(c, u):
                    sp.wait_ge(x_done, c + 1)
                    sp.dma_start(rows(X, c), x2[:, u]).then_inc(xs[u], 16)
                    sp.wait_ge(h_done, c + 1)
                    sp.dma_start(rows(H, c), h2[:, u]).then_inc(hs[u], 16)
                each_phases(sp, n, [load, load2, None, store])
                all_landed(sp, xs, n)
                all_landed(sp, hs, n)

            @block.vector
            def _(dve):
                dve.wait_ge(weights, 16 * (J + 4))
                nc.vector.tensor_scalar(eps1[:], eps1[:], 1.0, None, ALU.add).then_inc(eps_done, 1)
                dve.wait_ge(eps_done, 1)

                def rest(c, u):
                    landed(dve, hl, c, u, 2)
                    after(dve, T_ps, c - 1)
                    nc.vector.scalar_tensor_tensor(rst[:, u], hin[:, u], eps1[:], sin[:, u], ALU.mult, ALU.add).then_inc(r_done, 1)

                def finish(c, u):
                    dve.wait_ge(B_ps, c + 1)
                    landed(dve, xl, c, u)
                    sent(dve, xs, c, u)
                    after(dve, h_done, c - 1)
                    nc.vector.tensor_tensor(x2[:, u].rearrange("p j d -> p (j d)"), psB[u][:],
                                            xin[:, u].rearrange("p j d -> p (j d)"), ALU.add).then_inc(x_done, 1)
                    dve.wait_ge(x_done, c + 1)
                    norm.dve_moments(dve, x2[:, u], c, u)
                    norm.dve_coefs(dve, c, u, lambda: after(dve, h_done, c - 1))
                each_phases(dve, n, [rest, None, finish])

            @block.scalar
            def _(act):
                act.wait_ge(weights, 16 * (J + 4))

                def take(c, u):
                    act.wait_ge(T_ps, c + 1)
                    after(act, A_ps, c - 1)
                    nc.scalar.copy(rT[:, u, :], psT[u][:]).then_inc(T_sb, 1)

                def relu(c, u):
                    act.wait_ge(A_ps, c + 1)
                    after(act, B_ps, c - 1)
                    nc.scalar.activation(a_sb[:, u, :], psA[u][:], ACT.Relu, bias=b1[:]).then_inc(A_sb, 1)

                def normed(c, u):
                    norm.act_root(act, c, u)
                    sent(act, hs, c, u)
                    norm.act_apply(act, h2[:, u], x2[:, u], c, u).then_inc(h_done, 1)
                each_phases(act, n, [take, relu, normed])

            @block.tensor
            def _(pe):
                pe.wait_ge(weights, 16 * (J + 4))

                def turn(c, u):
                    pe.wait_ge(r_done, c + 1)
                    after(pe, T_sb, c - 1)
                    for j in range(J):
                        last = nc.tensor.transpose(psT[u][:, j * P:(j + 1) * P], rst[:, u, j, :], k.ident[:])
                    last.then_inc(T_ps, 1)

                def up(c, u):
                    pe.wait_ge(T_sb, c + 1)
                    after(pe, A_sb, c - 1)
                    nc.tensor.matmul(psA[u][:], w1[:], rT[:, u, :], start=True, stop=True).then_inc(A_ps, 1)

                def down(c, u):
                    pe.wait_ge(A_sb, c + 1)
                    after(pe, x_done, c - 1)
                    rows_product(nc, psB[u], a_sb[:, u], w2, bias[:].rearrange("a j d -> a (j d)"), k).then_inc(B_ps, 1)
                each_phases(pe, n, [turn, up, down])


def hyperbolic_messages(nc, k, s, plan, H, edges, norms):
    with Stage(nc, "mobius") as st:
        got_rows = st.sb("rows", [P, 2, 2, J, D])
        idx = st.sb("idx", [P, 2, 2, J], U32)
        sq, dot = st.sb("sq", [P, 2, 2, J]), st.sb("dot", [P, 2, J])
        c1, al, den, be = (st.sb(v, [P, 2, J]) for v in ("c1", "al", "den", "be"))
        scaled = st.sb("scaled", [P, 2, J, D])
        junk, junk2, junk3 = st.sb("junk", [P, J, D]), st.sb("junk2", [P, 2, J, D]), st.sb("junk3", [P, J, D])
        got = [st.sem(f"got{i}") for i in range(2)]
        idx_ready, tick, sq_done, dot_done, chain, coef, tmp_done, m_done, norm_done = (
            st.sem(v) for v in ("idx_ready", "tick", "sq_done", "dot_done", "chain", "coef", "tmp_done", "m_done", "norm_done"))
        n = s.echunks
        with st.run() as block:

            @block.gpsimd
            def _(pool):
                bound = pool.to_reg(s.N - 1)

                def gather(c, u):
                    pool.wait_ge(idx_ready, c + 1)
                    after(pool, m_done, c - 1)
                    pool.sem_inc(tick, 1)
                    for side in range(2):
                        for q in range(J):
                            gather_rows(pool, got_rows[:, u, side, q, :], H, idx[:, u, side, q:q + 1], bound, got[u])
                each(pool, n, gather)

            @block.scalar
            def _(act):
                def index(c, u):
                    sent(act, got, c, u, 2 * J)
                    nc.scalar.copy(idx[:, u, 0, :], plan.other[:, bass.ds(c * J, J)])
                    nc.scalar.copy(idx[:, u, 1, :], plan.key[:, bass.ds(c * J, J)]).then_inc(idx_ready, 1)

                def squares(c, u):
                    landed(act, got, c, u, 2 * J)
                    after(act, coef, c - 1)
                    after(act, sq_done, c)
                    for side in range(2):
                        for q in range(J):
                            last = nc.scalar.activation(junk2[:, side, q, :], got_rows[:, u, side, q, :], ACT.Square,
                                                        accum_out=sq[:, u, side, q:q + 1])
                    last.then_inc(sq_done, 1)

                def scale(c, u):
                    act.wait_ge(coef, c + 1)
                    after(act, m_done, c - 1)
                    for q in range(J):
                        last = nc.scalar.mul(scaled[:, u, q, :], got_rows[:, u, 1, q, :], be[:, u, q:q + 1])
                    last.then_inc(tmp_done, 1)

                def norm(c, u):
                    act.wait_ge(m_done, c + 1)
                    after(act, norm_done, c)
                    for q in range(J):
                        last = nc.scalar.activation(junk3[:, q, :], edges[:, bass.ds((c * J + q + 1) * D, D)], ACT.Square,
                                                    accum_out=norms[:, bass.ds(c * J + q, 1)])
                    last.then_inc(norm_done, 1)

                def late(c, u):
                    scale(c, u)
                    norm(c, u)
                each_phases(act, n, [index, squares, late])

            @block.vector
            def _(dve):
                ch = Chain(dve, chain, 6)

                def coefs(c, u):
                    landed(dve, got, c, u, 2 * J)
                    after(dve, dot_done, c)
                    for q in range(J):
                        last = nc.vector.scalar_tensor_tensor(junk[:, q, :], got_rows[:, u, 0, q, :], 1.0, got_rows[:, u, 1, q, :],
                                                              ALU.mult, ALU.mult, accum_out=dot[:, u, q:q + 1])
                    last.then_inc(dot_done, 1)
                    dve.wait_ge(dot_done, c + 1)
                    dve.wait_ge(sq_done, c + 1)
                    after(dve, tmp_done, c - 1)
                    after(dve, m_done, c - 1)
                    x2, y2 = sq[:, u, 0, :], sq[:, u, 1, :]
                    ch.step(c)
                    nc.vector.tensor_scalar(c1[:, u], dot[:, u], -2.0, 1.0, ALU.mult, ALU.add)
                    ch.link(nc.vector.tensor_tensor(den[:, u], x2, y2, ALU.mult))
                    nc.vector.tensor_tensor(al[:, u], c1[:, u], y2, ALU.add)
                    ch.link(nc.vector.tensor_tensor(den[:, u], den[:, u], c1[:, u], ALU.add))
                    ch.link(nc.vector.tensor_scalar(den[:, u], den[:, u], HYP_EPS, None, ALU.max))
                    ch.link(nc.vector.reciprocal(den[:, u], den[:, u]))
                    ch.link(nc.vector.tensor_tensor(al[:, u], al[:, u], den[:, u], ALU.mult))
                    nc.vector.scalar_tensor_tensor(be[:, u], x2, -1.0, den[:, u], ALU.add, ALU.mult).then_inc(coef, 1)
                    ch.link(nc.vector.tensor_copy(c1[:, u], c1[:, u]))

                def finish(c, u):
                    dve.wait_ge(tmp_done, c + 1)
                    for q in range(J):
                        last = nc.vector.scalar_tensor_tensor(edges[:, bass.ds((c * J + q + 1) * D, D)], got_rows[:, u, 0, q, :],
                                                              al[:, u, q:q + 1], scaled[:, u, q, :], ALU.mult, ALU.add)
                    last.then_inc(m_done, 1)
                each_phases(dve, n, [None, coefs, finish])


class FoldScratch:
    def __init__(self, st):
        self.junk, self.scaled = st.sb("junk", [P, D]), st.sb("scaled", [P, D])
        self.dot, self.a1, self.x2, self.al, self.be = (st.sb(v, [P, 1]) for v in ("dot", "a1", "x2", "al", "be"))
        self.den, self.cut, self.inv, self.al2, self.be2 = (st.sb(v, [P, 1]) for v in ("den", "cut", "inv", "al2", "be2"))


def fold_step(nc, b, plan, norms, t, state, m, out, q, link, q_ready, r_ready):
    link(nc.vector.scalar_tensor_tensor(b.junk[:], m, plan.same[:, bass.ds(t, 1)], state, ALU.mult, ALU.mult,
                                        accum_out=b.dot[:]))
    q_ready()
    nc.vector.tensor_scalar(b.a1[:], b.dot[:], 2.0, 1.0, ALU.mult, ALU.add)
    link(nc.vector.tensor_scalar(b.x2[:], q, plan.same[:, bass.ds(t, 1)], None, ALU.mult))
    nc.vector.tensor_scalar(b.al[:], b.a1[:], norms[:, bass.ds(t, 1)], plan.same[:, bass.ds(t, 1)], ALU.add, ALU.mult)
    nc.vector.tensor_scalar(b.be[:], b.x2[:], -1.0, 1.0, ALU.mult, ALU.add)
    link(nc.vector.tensor_scalar(b.den[:], b.x2[:], norms[:, bass.ds(t, 1)], b.a1[:], ALU.mult, ALU.add))
    link(nc.vector.tensor_scalar(b.cut[:], b.den[:], HYP_EPS, None, ALU.max))
    link(nc.vector.reciprocal(b.inv[:], b.cut[:]))
    nc.vector.tensor_tensor(b.al2[:], b.al[:], b.inv[:], ALU.mult)
    link(nc.vector.tensor_tensor(b.be2[:], b.be[:], b.inv[:], ALU.mult))
    link(nc.vector.tensor_scalar(b.scaled[:], m, b.be2[:], None, ALU.mult))
    r_ready()
    return nc.vector.scalar_tensor_tensor(out, state, b.al2[:], b.scaled[:], ALU.mult, ALU.add)


FOLD_LINKS = 7


def hyperbolic_fold(nc, k, s, plan, edges, norms, lengths):
    with Stage(nc, "fold") as st:
        state = st.sb("state", [P, 2, D])
        final = st.sb("final", [P, D])
        flag = st.sb("flag", [P, 1], I32)
        q = st.sb("q", [P, 2])
        qjunk = st.sb("qjunk", [P, D])
        b = FoldScratch(st)
        psC, psF = st.ps("psC", [P, D]), st.ps("psF", [P, 1])
        tick = st.sem("tick")
        (zeroed, flagged, flag_done, s1_chain, s1_state, s1_q, slow_chain, slow_state, slow_moved, state_done, moved,
         start_done, s2_chain, s2_state, s2_q) = (
            st.sem(v) for v in ("zeroed", "flagged", "flag_done", "s1_chain", "s1_state", "s1_q", "slow_chain", "slow_state",
                                "slow_moved", "state_done", "moved", "start_done", "s2_chain", "s2_state", "s2_q"))
        n = s.T
        rounds = P - 2
        per = FOLD_LINKS
        with st.run() as block:

            @block.vector
            def _(dve):
                dve.wait_ge(flagged, 1)
                nc.vector.tensor_copy(flag[:], psF[:]).then_inc(flag_done, 1)
                nc.vector.memset(state[:], 0.0).then_inc(zeroed, 1)
                dve.wait_ge(zeroed, 1)
                dve.wait_ge(flag_done, 1)
                ch = Chain(dve, s1_chain, per)

                def first_sweep(t, u):
                    ch.step(t)
                    last = fold_step(nc, b, plan, norms, t, state[:, u, :], edges[:, bass.ds((t + 1) * D, D)], state[:, 1 - u, :],
                                     q[:, u:u + 1], ch.link, lambda: dve.wait_ge(s1_q, t + 1), lambda: None)
                    last.then_inc(s1_state, 1)
                    dve.wait_ge(s1_state, t + 1)
                each(dve, n, first_sweep)

                crossing = dve.value_load(flag[0:1, 0:1], min_val=0, max_val=P)
                with dve.If(crossing > 0):
                    dve.sem_inc(slow_state, 1)
                    with dve.Fori(0, rounds) as r:
                        dve.wait_ge(slow_moved, r + 1)
                        nc.vector.tensor_scalar(state[:, 0, :], psC[:], plan.cont[:], None, ALU.mult).then_inc(slow_chain, 1)
                        dve.wait_ge(slow_chain, r * ((per + 2) * n + 1) + 1)
                        dve.sem_inc(tick, 1)
                        with dve.Fori(0, n // 2) as i:
                            for u in range(2):
                                count = [0]

                                def link(ins, u=u):
                                    ins.then_inc(slow_chain, 1)
                                    count[0] += 1
                                    dve.wait_ge(slow_chain, r * ((per + 2) * n + 1) + 1 + (i * 2 + u) * (per + 2) + count[0])
                                link(nc.vector.scalar_tensor_tensor(b.junk[:], state[:, u, :], 1.0, state[:, u, :], ALU.mult, ALU.mult,
                                                                    accum_out=q[:, u:u + 1]))
                                link(fold_step(nc, b, plan, norms, i * 2 + u, state[:, u, :],
                                               edges[:, bass.ds((i * 2 + u + 1) * D, D)], state[:, 1 - u, :],
                                               q[:, u:u + 1], link, lambda: None, lambda: None))
                                assert count[0] == per + 2
                        nc.vector.tensor_copy(final[:], state[:, 0, :]).then_inc(slow_state, 1)
                        dve.wait_ge(slow_state, r + 2)
                nc.vector.tensor_copy(final[:], state[:, 0, :]).then_inc(state_done, 1)

                dve.wait_ge(moved, 1)
                nc.vector.tensor_scalar(edges[:, 0:D], psC[:], plan.cont[:], None, ALU.mult).then_inc(start_done, 1)
                dve.wait_ge(start_done, 1)
                ch2 = Chain(dve, s2_chain, per)

                def last_sweep(t, u):
                    ch2.step(t)
                    here = edges[:, bass.ds((t + 1) * D, D)]
                    last = fold_step(nc, b, plan, norms, t, edges[:, bass.ds(t * D, D)], here, here,
                                     q[:, u:u + 1], ch2.link, lambda: dve.wait_ge(s2_q, t + 1), lambda: None)
                    last.then_inc(s2_state, 1)
                    dve.wait_ge(s2_state, t + 1)
                each(dve, n, last_sweep)

            @block.scalar
            def _(act):
                def first_sweep(t, u):
                    if isinstance(t, int) and t == 0:
                        act.wait_ge(zeroed, 1)
                    else:
                        act.wait_ge(s1_state, t)
                    after(act, s1_q, t)
                    nc.scalar.activation(qjunk[:], state[:, u, :], ACT.Square, accum_out=q[:, u:u + 1]).then_inc(s1_q, 1)
                each(act, n, first_sweep)
                act.wait_ge(start_done, 1)

                def last_sweep(t, u):
                    if not (isinstance(t, int) and t == 0):
                        act.wait_ge(s2_state, t)
                        act.wait_ge(s2_q, t)
                    nc.scalar.activation(qjunk[:], edges[:, bass.ds(t * D, D)], ACT.Square, accum_out=q[:, u:u + 1]).then_inc(s2_q, 1)
                each(act, n, last_sweep)

            @block.tensor
            def _(pe):
                nc.tensor.matmul(psF[:], k.ones[:], plan.through[:], start=True, stop=True).then_inc(flagged, 1)
                pe.wait_ge(flag_done, 1)
                crossing = pe.value_load(flag[0:1, 0:1], min_val=0, max_val=P)
                pe.wait_ge(s1_state, n)
                with pe.If(crossing > 0):
                    with pe.Fori(0, rounds) as r:
                        pe.wait_ge(slow_state, r + 1)
                        nc.tensor.matmul(psC[:], k.shift[:], state[:, 0, :], start=True, stop=True).then_inc(slow_moved, 1)
                pe.wait_ge(state_done, 1)
                nc.tensor.matmul(psC[:], k.shift[:], final[:], start=True, stop=True).then_inc(moved, 1)


def hyperbolic_results(nc, k, s, plan, H, edges, lengths):
    T = s.T
    with Stage(nc, "aggregate") as st:
        rows_in = st.sb("rows", [P, 2, J, D])
        res = st.sb("res", [P, 2, J, D])
        scaled = st.sb("scaled", [P, 2, J, D])
        junk, junk2, junk3 = st.sb("junk", [P, 4, D]), st.sb("junk2", [P, J, D]), st.sb("junk3", [P, J, D])
        idx = st.sb("idx", [P, 2, J], U32)
        nrm, cut, low, lg, th, factor, alive, y2, y2in = (
            st.sb(v, [P, T]) for v in ("nrm", "cut", "low", "lg", "th", "factor", "alive", "y2", "y2in"))
        x2, dot = st.sb("x2", [P, 2, J]), st.sb("dot", [P, 2, J])
        c1, al, den, be, xy = (st.sb(v, [P, 2, J]) for v in ("c1", "al", "den", "be", "xy"))
        got = [st.sem(f"got{i}") for i in range(2)]
        put = [st.sem(f"put{i}") for i in range(2)]
        len_done, root, ratio, logged, argd, thd, prep, batch, cleared = (
            st.sem(v) for v in ("len_done", "root", "ratio", "logged", "argd", "thd", "prep", "batch", "cleared"))
        idx_ready, tick, sq_done, dot_done, chain, coef, tmp_done, res_done = (
            st.sem(v) for v in ("idx_ready", "tick", "sq_done", "dot_done", "chain", "coef", "tmp_done", "res_done"))
        n = s.echunks
        with st.run() as block:

            @block.gpsimd
            def _(pool):
                bound = pool.to_reg(s.N - 1)
                pool.wait_ge(cleared, 1)

                def gather(c, u):
                    pool.wait_ge(idx_ready, c + 1)
                    after(pool, res_done, c - 1)
                    pool.sem_inc(tick, 1)
                    for q in range(J):
                        gather_rows(pool, rows_in[:, u, q, :], H, idx[:, u, q:q + 1], bound, got[u])

                def scatter(c, u):
                    pool.wait_ge(res_done, c + 1)
                    pool.sem_inc(tick, 1)
                    for q in range(J):
                        scatter_rows(pool, H, res[:, u, q, :], idx[:, u, q:q + 1], bound, put[u])
                each_phases(pool, n, [gather, scatter])
                all_landed(pool, put, n, J)

            @block.scalar
            def _(act):
                def length(c, u):
                    after(act, len_done, c)
                    for q in range(J):
                        last = nc.scalar.activation(junk[:, q, :], edges[:, bass.ds((c * J + q + 1) * D, D)], ACT.Square,
                                                    accum_out=lengths[:, bass.ds(c * J + q, 1)])
                    last.then_inc(len_done, 1)
                each(act, n, length)
                act.wait_ge(prep, 1)
                nc.scalar.activation(nrm[:], cut[:], ACT.Sqrt).then_inc(root, 1)
                act.wait_ge(ratio, 1)
                nc.scalar.activation(lg[:], low[:], ACT.Ln).then_inc(logged, 1)
                act.wait_ge(argd, 1)
                nc.scalar.activation(th[:], lg[:], ACT.Tanh).then_inc(thd, 1)

                def index(c, u):
                    sent(act, put, c, u, J)
                    nc.scalar.copy(idx[:, u, :], plan.last[:, bass.ds(c * J, J)]).then_inc(idx_ready, 1)

                def squares(c, u):
                    landed(act, got, c, u, J)
                    after(act, coef, c - 1)
                    after(act, sq_done, c)
                    for q in range(J):
                        last = nc.scalar.activation(junk2[:, q, :], rows_in[:, u, q, :], ACT.Square, accum_out=x2[:, u, q:q + 1])
                    last.then_inc(sq_done, 1)
                    act.wait_ge(coef, c + 1)
                    after(act, res_done, c - 1)
                    for q in range(J):
                        last = nc.scalar.mul(scaled[:, u, q, :], rows_in[:, u, q, :], al[:, u, q:q + 1])
                    last.then_inc(tmp_done, 1)
                each_phases(act, n, [index, squares])

            @block.vector
            def _(dve):
                ch = Chain(dve, batch, 99)
                nc.vector.memset(rows_in[:], 0.0).then_inc(cleared, 1)
                dve.wait_ge(len_done, n)
                nc.vector.tensor_scalar(cut[:], lengths[:], 1e-30, None, ALU.max).then_inc(prep, 1)
                dve.wait_ge(root, 1)
                ch.link(nc.vector.tensor_scalar(alive[:], nrm[:], HYP_EPS, None, ALU.is_gt))
                ch.link(nc.vector.tensor_scalar(cut[:], nrm[:], HYP_EPS, 1.0 - HYP_EPS, ALU.max, ALU.min))
                ch.link(nc.vector.tensor_scalar(low[:], cut[:], -1.0, 1.0, ALU.mult, ALU.add))
                ch.link(nc.vector.reciprocal(low[:], low[:]))
                ch.link(nc.vector.tensor_scalar(nrm[:], cut[:], 1.0, None, ALU.add))
                nc.vector.tensor_tensor(low[:], low[:], nrm[:], ALU.mult).then_inc(ratio, 1)
                dve.wait_ge(logged, 1)
                nc.vector.scalar_tensor_tensor(lg[:], lg[:], 0.5, plan.inv[:], ALU.mult, ALU.mult).then_inc(argd, 1)
                ch.link(nc.vector.reciprocal(factor[:], cut[:]))
                ch.link(nc.vector.tensor_tensor(factor[:], factor[:], alive[:], ALU.mult))
                dve.wait_ge(thd, 1)
                ch.link(nc.vector.tensor_tensor(factor[:], factor[:], th[:], ALU.mult))
                ch.link(nc.vector.tensor_tensor(y2[:], factor[:], factor[:], ALU.mult))
                ch.link(nc.vector.tensor_tensor(y2[:], y2[:], lengths[:], ALU.mult))
                ch2 = Chain(dve, chain, 10)

                def step(c, u):
                    landed(dve, got, c, u, J)
                    after(dve, dot_done, c)
                    for q in range(J):
                        last = nc.vector.scalar_tensor_tensor(junk3[:, q, :], rows_in[:, u, q, :], 1.0, edges[:, bass.ds((c * J + q + 1) * D, D)],
                                                              ALU.mult, ALU.mult, accum_out=dot[:, u, q:q + 1])
                    last.then_inc(dot_done, 1)
                    dve.wait_ge(dot_done, c + 1)
                    dve.wait_ge(sq_done, c + 1)
                    f, y = factor[:, bass.ds(c * J, J)], y2[:, bass.ds(c * J, J)]
                    ch2.step(c)
                    ch2.link(nc.vector.tensor_tensor(xy[:, u], dot[:, u], f, ALU.mult))
                    ch2.link(nc.vector.tensor_scalar(c1[:, u], xy[:, u], 2.0, 1.0, ALU.mult, ALU.add))
                    ch2.link(nc.vector.tensor_tensor(den[:, u], x2[:, u], y, ALU.mult))
                    ch2.link(nc.vector.tensor_tensor(den[:, u], den[:, u], c1[:, u], ALU.add))
                    ch2.link(nc.vector.tensor_scalar(den[:, u], den[:, u], HYP_EPS, None, ALU.max))
                    ch2.link(nc.vector.reciprocal(den[:, u], den[:, u]))
                    ch2.link(nc.vector.tensor_scalar(be[:, u], x2[:, u], -1.0, 1.0, ALU.mult, ALU.add))
                    ch2.link(nc.vector.tensor_tensor(be[:, u], be[:, u], f, ALU.mult))
                    ch2.link(nc.vector.tensor_tensor(c1[:, u], c1[:, u], y, ALU.add))
                    after(dve, tmp_done, c - 1)
                    ch2.link(nc.vector.tensor_tensor(be[:, u], be[:, u], den[:, u], ALU.mult))
                    nc.vector.tensor_tensor(al[:, u], c1[:, u], den[:, u], ALU.mult).then_inc(coef, 1)
                    dve.wait_ge(tmp_done, c + 1)
                    sent(dve, put, c, u, J)
                    for q in range(J):
                        last = nc.vector.scalar_tensor_tensor(res[:, u, q, :], edges[:, bass.ds((c * J + q + 1) * D, D)], be[:, u, q:q + 1],
                                                              scaled[:, u, q, :], ALU.mult, ALU.add)
                    last.then_inc(res_done, 1)
                each(dve, n, step)


def third_norm(nc, k, s, X, H):
    with Stage(nc, "norm3") as st:
        norm = Norm(nc, st, k)
        xin, hin, x3, h3 = (st.sb(v, [P, 2, J, D]) for v in ("xin", "hin", "x3", "h3"))
        ld, xs, hs = ([st.sem(f"{v}{i}") for i in range(2)] for v in ("ld", "xs", "hs"))
        x_done, h_done = st.sem("x_done"), st.sem("h_done")
        n = s.chunks
        with st.run() as block:

            @block.sync
            def _(sp):
                def load(c, u):
                    after(sp, x_done, c - 1)
                    sp.dma_start(xin[:, u], rows(X, c)).then_inc(ld[u], 16)
                    sp.dma_start(hin[:, u], rows(H, c)).then_inc(ld[u], 16)

                def store(c, u):
                    sp.wait_ge(x_done, c + 1)
                    sp.dma_start(rows(X, c), x3[:, u]).then_inc(xs[u], 16)
                    sp.wait_ge(h_done, c + 1)
                    sp.dma_start(rows(H, c), h3[:, u]).then_inc(hs[u], 16)
                each_lagged(sp, n, load, store)
                all_landed(sp, xs, n)
                all_landed(sp, hs, n)

            @block.vector
            def _(dve):
                def add(c, u):
                    landed(dve, ld, c, u, 2)
                    sent(dve, xs, c, u)
                    after(dve, h_done, c - 1)
                    nc.vector.tensor_tensor(x3[:, u], xin[:, u], hin[:, u], ALU.add).then_inc(x_done, 1)
                    dve.wait_ge(x_done, c + 1)
                    norm.dve_moments(dve, x3[:, u], c, u)
                    norm.dve_coefs(dve, c, u, lambda: after(dve, h_done, c - 1))
                each(dve, n, add)

            @block.scalar
            def _(act):
                def normed(c, u):
                    norm.act_root(act, c, u)
                    sent(act, hs, c, u)
                    norm.act_apply(act, h3[:, u], x3[:, u], c, u).then_inc(h_done, 1)
                each(act, n, normed)


class Ssp:

    def __init__(self, nc, st, k, b):
        self.nc, self.b, self.k = nc, b, k
        self.v, self.mag, self.dec, self.log = (st.sb(x, [P, 2, CH]) for x in ("ssp_v", "ssp_mag", "ssp_dec", "ssp_log"))
        self.taken, self.a, self.e, self.logged, self.used = (
            st.sem(x) for x in ("ssp_taken", "ssp_a", "ssp_e", "ssp_logged", "ssp_used"))

    def dve_take(self, dve, psum, c, u):
        after(dve, self.used, c - 1)
        after(dve, self.a, c - 1)
        self.nc.vector.tensor_scalar(self.v[:, u], psum, self.b[:], None, ALU.add).then_inc(self.taken, 1)

    def act_log(self, act, c, u):
        nc = self.nc
        act.wait_ge(self.taken, c + 1)
        nc.scalar.activation(self.mag[:, u], self.v[:, u], ACT.Abs).then_inc(self.a, 1)
        act.wait_ge(self.a, c + 1)
        nc.scalar.activation(self.dec[:, u], self.mag[:, u], ACT.Exp, scale=-1.0).then_inc(self.e, 1)
        act.wait_ge(self.e, c + 1)
        after(act, self.used, c - 1)
        nc.scalar.activation(self.log[:, u], self.dec[:, u], ACT.Ln, bias=self.k.half_col[:], scale=0.5).then_inc(self.logged, 1)

    def dve_result(self, dve, out, c, u):
        dve.wait_ge(self.logged, c + 1)
        self.nc.vector.scalar_tensor_tensor(out, self.v[:, u], 0.0, self.log[:, u], ALU.max, ALU.add).then_inc(self.used, 1)


def filter_messages(nc, k, s, plan, L3, attr, H, edges, carry):
    T = s.T
    with Stage(nc, "edge3") as st:
        rows_in = st.sb("rows", [P, 2, J, D])
        attr_in = st.sb("attr", [P, 2, J, D])
        idx = st.sb("idx", [P, 2, 2, J], U32)
        aT, hT, hl, msg = (st.sb(v, [P, 2, CH]) for v in ("aT", "hT", "hl", "msg"))
        sp_out = st.sb("sp_out", [P, 2, CH])
        cut_rows = st.sb("cut_rows", [P, 2, J, D])
        phase, whole, cosine = st.sb("phase", [P, T]), st.sb("whole", [P, T]), st.sb("cosine", [P, T])
        w1, w2, lin1 = st.sb("w1", [P, D]), st.sb("w2", [P, D]), st.sb("lin1", [P, D])
        b1, b2 = st.sb("b1", [P, 1]), st.sb("b2", [P, 1])
        ssp = Ssp(nc, st, k, b1)
        psA = st.ps("psA", [P, CH])
        psH = st.ps("psH", [P, CH])
        psV = [st.ps(f"psV{i}", [P, CH]) for i in range(2)]
        psL = st.ps("psL", [P, CH])
        psW = st.ps("psW", [P, CH])
        psR = [st.ps(f"psR{i}", [P, CH]) for i in range(2)]
        got = [st.sem(f"got{i}") for i in range(2)]
        weights, padded, idx_ready, tick, A_ps, A_sb, H_sb, V_ps, L_ps, L_sb, W_ps, msg_done, R_ps, R_sb = (
            st.sem(v) for v in ("weights", "padded", "idx_ready", "tick", "A_ps", "A_sb", "H_sb", "V_ps", "L_ps", "L_sb",
                                "W_ps", "msg_done", "R_ps", "R_sb"))
        chain, zeroed, carried, taken, turns, cos_done, sin_done = (
            st.sem(v) for v in ("chain", "zeroed", "carried", "taken", "turns", "cos_done", "sin_done"))
        n = s.echunks
        big = 1.5 * 2.0 ** 23
        with st.run() as block:

            @block.sync
            def _(sp):
                sp.wait_ge(padded, 2)
                for dst, src in ((w1[0:NG, :], L3["mlp_w1"][:, :]), (w2[:], L3["mlp_w2"][:, :]), (lin1[:], L3["lin1_w"][:, :]),
                                 (b1[:], column(L3["mlp_b1"])), (b2[:], column(L3["mlp_b2"]))):
                    sp.dma_start(dst, src).then_inc(weights, 16)

            @block.gpsimd
            def _(pool):
                bound = pool.to_reg(s.N - 1)
                ebound = pool.to_reg(s.E - 1)
                pool.memset(w1[:], 0.0).then_inc(padded, 1)
                pool.memset(attr_in[:], 0.0).then_inc(padded, 1)
                pool.wait_ge(padded, 2)

                def gather(c, u):
                    pool.wait_ge(idx_ready, c + 1)
                    after(pool, A_ps, c - 1)
                    pool.sem_inc(tick, 1)
                    for q in range(J):
                        gather_rows(pool, rows_in[:, u, q, :], H, idx[:, u, 0, q:q + 1], bound, got[u])
                        gather_rows(pool, attr_in[:, u, q, 0:NG], attr, idx[:, u, 1, q:q + 1], ebound, got[u])
                each(pool, n, gather)

            @block.scalar
            def _(act):
                act.wait_ge(weights, 80)
                act.wait_ge(turns, 1)
                nc.scalar.activation(cosine[:], phase[:], ACT.Sin, scale=2.0 * math.pi).then_inc(sin_done, 1)

                def index(c, u):
                    sent(act, got, c, u, 2 * J)
                    nc.scalar.copy(idx[:, u, 0, :], plan.other[:, bass.ds(c * J, J)])
                    nc.scalar.copy(idx[:, u, 1, :], plan.edge[:, bass.ds(c * J, J)]).then_inc(idx_ready, 1)

                def take(c, u):
                    act.wait_ge(A_ps, c + 1)
                    after(act, V_ps, c - 1)
                    nc.scalar.copy(aT[:, u, :], psA[:]).then_inc(A_sb, 1)
                    act.wait_ge(L_ps, c + 1)
                    after(act, msg_done, c - 1)
                    nc.scalar.copy(hl[:, u, :], psL[:]).then_inc(L_sb, 1)

                def soft(c, u):
                    ssp.act_log(act, c, u)

                def cutoff(c, u):
                    act.wait_ge(R_ps, c + 1)
                    act.wait_ge(cos_done, 1)
                    after(act, chain, (c - 1) * J)
                    for q in range(J):
                        last = nc.scalar.mul(cut_rows[:, u, q, :], psR[u][:, q * D:(q + 1) * D], cosine[:, bass.ds(c * J + q, 1)])
                    last.then_inc(R_sb, 1)
                each_phases(act, n, [index, take, soft, cutoff])

            @block.vector
            def _(dve):
                ch = Chain(dve, chain, J)
                nc.vector.memset(edges[:, 0:D], 0.0).then_inc(zeroed, 1)
                dve.wait_ge(zeroed, 1)
                nc.vector.tensor_scalar(phase[:], plan.weight[:], 0.5 / CUTOFF, 0.25, ALU.mult, ALU.add).then_inc(zeroed, 1)
                dve.wait_ge(zeroed, 2)
                nc.vector.tensor_scalar(whole[:], phase[:], big, None, ALU.add).then_inc(zeroed, 1)
                dve.wait_ge(zeroed, 3)
                nc.vector.tensor_scalar(whole[:], whole[:], -big, None, ALU.add).then_inc(zeroed, 1)
                dve.wait_ge(zeroed, 4)
                nc.vector.tensor_tensor(phase[:], phase[:], whole[:], ALU.subtract).then_inc(zeroed, 1)
                dve.wait_ge(zeroed, 5)
                nc.vector.tensor_scalar(phase[:], phase[:], 0.4999999, -0.4999999, ALU.min, ALU.max).then_inc(turns, 1)
                dve.wait_ge(sin_done, 1)
                nc.vector.tensor_scalar(cosine[:], cosine[:], 0.5, 0.5, ALU.mult, ALU.add).then_inc(cos_done, 1)
                dve.wait_ge(weights, 80)

                def take(c, u):
                    dve.wait_ge(A_ps, c + 1)
                    after(dve, L_ps, c - 1)
                    nc.vector.tensor_copy(hT[:, u, :], psH[:]).then_inc(H_sb, 1)

                def soft(c, u):
                    dve.wait_ge(V_ps, c + 1)
                    ssp.dve_take(dve, psV[u][:], c, u)
                    after(dve, W_ps, c - 1)
                    ssp.dve_result(dve, sp_out[:, u, :], c, u)
                    dve.wait_ge(W_ps, c + 1)
                    dve.wait_ge(L_sb, c + 1)
                    after(dve, R_ps, c - 1)
                    nc.vector.scalar_tensor_tensor(msg[:, u, :], psW[:], b2[:], hl[:, u, :], ALU.add, ALU.mult).then_inc(msg_done, 1)

                def add(c, u):
                    dve.wait_ge(R_sb, c + 1)
                    ch.step(c)
                    for q in range(J):
                        ch.link(nc.vector.scalar_tensor_tensor(
                            edges[:, bass.ds((c * J + q + 1) * D, D)], edges[:, bass.ds((c * J + q) * D, D)],
                            plan.same[:, bass.ds(c * J + q, 1)], cut_rows[:, u, q, :], ALU.mult, ALU.add))
                each_phases(dve, n, [None, take, soft, add])
                dve.wait_ge(carried, 1)
                nc.vector.tensor_copy(carry[:], psA[:, 0:D]).then_inc(taken, 1)
                dve.wait_ge(taken, 1)

            @block.tensor
            def _(pe):
                pe.wait_ge(weights, 80)

                def turn(c, u):
                    landed(pe, got, c, u, 2 * J)
                    after(pe, A_sb, c)
                    after(pe, H_sb, c)
                    for q in range(J):
                        nc.tensor.transpose(psA[:, q * P:(q + 1) * P], attr_in[:, u, q, :], k.ident[:])
                    for q in range(J):
                        last = nc.tensor.transpose(psH[:, q * P:(q + 1) * P], rows_in[:, u, q, :], k.ident[:])
                    last.then_inc(A_ps, 1)
                    pe.wait_ge(H_sb, c + 1)
                    after(pe, L_sb, c)
                    nc.tensor.matmul(psL[:], lin1[:], hT[:, u, :], start=True, stop=True).then_inc(L_ps, 1)
                    pe.wait_ge(A_sb, c + 1)
                    after(pe, ssp.taken, c - 1)
                    nc.tensor.matmul(psV[u][:], w1[:], aT[:, u, :], start=True, stop=True).then_inc(V_ps, 1)

                def filt(c, u):
                    pe.wait_ge(ssp.used, c + 1)
                    after(pe, msg_done, c)
                    nc.tensor.matmul(psW[:], w2[:], sp_out[:, u, :], start=True, stop=True).then_inc(W_ps, 1)

                def back(c, u):
                    pe.wait_ge(msg_done, c + 1)
                    after(pe, R_sb, c - 1)
                    for q in range(J):
                        last = nc.tensor.transpose(psR[u][:, q * D:(q + 1) * D], msg[:, u, q * P:(q + 1) * P], k.ident[:])
                    last.then_inc(R_ps, 1)
                each_phases(pe, n, [None, turn, filt, back])
                pe.wait_ge(chain, n * J)
                nc.tensor.matmul(psA[:, 0:D], plan.carry[:], edges[:, s.T * D:], start=True, stop=True).then_inc(carried, 1)


def last_update(nc, k, s, L3, X, S, out):
    with Stage(nc, "node3") as st:
        xin, sin, y = (st.sb(v, [P, 2, J, D]) for v in ("xin", "sin", "y"))
        sT, a_sb = st.sb("sT", [P, 2, CH]), st.sb("a", [P, 2, CH])
        w1, w2, b1 = st.sb("w1", [P, D]), st.sb("w2", [P, D]), st.sb("b1", [P, 1])
        bias = st.sb("bias", [1, J, D])
        ssp = Ssp(nc, st, k, b1)
        psT = [st.ps(f"psT{i}", [P, CH]) for i in range(2)]
        psA = [st.ps(f"psA{i}", [P, CH]) for i in range(2)]
        psB = [st.ps(f"psB{i}", [P, CH]) for i in range(2)]
        xl, sl, ys = ([st.sem(f"{v}{i}") for i in range(2)] for v in ("xl", "sl", "ys"))
        weights, T_ps, T_sb, A_ps, B_ps, y_done = (
            st.sem(v) for v in ("weights", "T_ps", "T_sb", "A_ps", "B_ps", "y_done"))
        n = s.chunks
        with st.run() as block:

            @block.sync
            def _(sp):
                for j in range(J):
                    sp.dma_start(bias[:, j, :], row(L3["lin_b"])).then_inc(weights, 16)
                sp.dma_start(w1[:], L3["lin2_w"][:, :]).then_inc(weights, 16)
                sp.dma_start(w2[:], L3["lin_w"][:, :]).then_inc(weights, 16)
                sp.dma_start(b1[:], column(L3["lin2_b"])).then_inc(weights, 16)

                def load(c, u):
                    after(sp, T_ps, c - 1)
                    sp.dma_start(sin[:, u], rows(S, c)).then_inc(sl[u], 16)

                def load2(c, u):
                    after(sp, y_done, c - 1)
                    sp.dma_start(xin[:, u], rows(X, c)).then_inc(xl[u], 16)

                def store(c, u):
                    sp.wait_ge(y_done, c + 1)
                    if isinstance(c, int) and c == n - 1:
                        sp.dma_start(out[c * CH:s.N, :].rearrange("(p j) d -> p j d", j=J), y[0:s.tp, u]).then_inc(ys[u], 16)
                    else:
                        sp.dma_start(rows(out, c), y[:, u]).then_inc(ys[u], 16)
                each_phases(sp, n, [load, load2, None, store])
                all_landed(sp, ys, n)

            @block.tensor
            def _(pe):
                pe.wait_ge(weights, 16 * (J + 3))

                def turn(c, u):
                    landed(pe, sl, c, u)
                    after(pe, T_sb, c - 1)
                    for j in range(J):
                        last = nc.tensor.transpose(psT[u][:, j * P:(j + 1) * P], sin[:, u, j, :], k.ident[:])
                    last.then_inc(T_ps, 1)

                def up(c, u):
                    pe.wait_ge(T_sb, c + 1)
                    after(pe, ssp.taken, c - 1)
                    nc.tensor.matmul(psA[u][:], w1[:], sT[:, u, :], start=True, stop=True).then_inc(A_ps, 1)

                def down(c, u):
                    pe.wait_ge(ssp.used, c + 1)
                    after(pe, y_done, c - 1)
                    rows_product(nc, psB[u], a_sb[:, u], w2, bias[:].rearrange("a j d -> a (j d)"), k).then_inc(B_ps, 1)
                each_phases(pe, n, [turn, up, down])

            @block.scalar
            def _(act):
                act.wait_ge(weights, 16 * (J + 3))

                def take(c, u):
                    act.wait_ge(T_ps, c + 1)
                    after(act, A_ps, c - 1)
                    nc.scalar.copy(sT[:, u, :], psT[u][:]).then_inc(T_sb, 1)

                def soft(c, u):
                    ssp.act_log(act, c, u)
                each_phases(act, n, [take, soft])

            @block.vector
            def _(dve):
                dve.wait_ge(weights, 16 * (J + 3))

                def soft(c, u):
                    dve.wait_ge(A_ps, c + 1)
                    ssp.dve_take(dve, psA[u][:], c, u)
                    after(dve, B_ps, c - 1)
                    ssp.dve_result(dve, a_sb[:, u, :], c, u)

                def finish(c, u):
                    dve.wait_ge(B_ps, c + 1)
                    landed(dve, xl, c, u)
                    sent(dve, ys, c, u)
                    nc.vector.tensor_tensor(y[:, u].rearrange("p j d -> p (j d)"), psB[u][:],
                                            xin[:, u].rearrange("p j d -> p (j d)"), ALU.add).then_inc(y_done, 1)
                each_phases(dve, n, [None, soft, finish])


def program(nc, a, t):
    s = Shapes(a["x"].shape[0], a["src"].shape[0])
    L0 = {n[7:]: v for n, v in a.items() if n.startswith("L0_gnn_")}
    with ExitStack() as stack:
        k = Constants(stack, nc)
        make_constants(nc, k)
        first_norm(nc, k, s, a["x"], L0["wv"], L0["bv"], L0["wo"], L0["bo"], t["H"], t["Y"])
        src_plan = Plan(stack, nc, s, "src")
        edges = stack.enter_context(nc.sbuf_tensor("edges", [P, (s.T + 1) * D], F32))
        carry = stack.enter_context(nc.sbuf_tensor("carry", [P, D], F32))
        sort_edges(nc, k, s, a["src"], a["dst"], a["edge_weight"], t["rec_src"])
        edge_plan(nc, k, s, t["rec_src"], src_plan)
        sum_neighbours(nc, k, s, src_plan, t["H"], edges, carry)
        attend(nc, k, s, src_plan, L0, t["H"], t["Y"], edges, carry)
        coefs = [stack.enter_context(nc.sbuf_tensor(f"bn_{x}", [P, 1], F32)) for x in ("scale1", "offset1", "scale2", "offset2")]
        node_moments(nc, k, s, t["Y"], L0["g1"], L0["be1"], coefs[0], coefs[1])
        node_mlp(nc, k, s, L0, t["Y"], t["U"], *coefs)
        second_norm(nc, k, s, a["x"], t["U"], t["X"], t["H"], coefs[2], coefs[3])
        L1 = {n[7:]: v for n, v in a.items() if n.startswith("L1_gnn_")}
        dst_plan = Plan(stack, nc, s, "dst")
        zero_table(nc, s, t["S"])
        sort_edges(nc, k, s, a["dst"], a["src"], a["edge_weight"], t["rec_dst"])
        edge_plan(nc, k, s, t["rec_dst"], dst_plan)
        edge_messages(nc, k, s, dst_plan, L1, t["H"], edges, carry)
        scatter_sums(nc, s, dst_plan, t["S"], edges, carry, "scatter1")
        node_update(nc, k, s, L1, t["X"], t["H"], t["S"])
        L3 = {n[7:]: v for n, v in a.items() if n.startswith("L3_gnn_")}
        norms = stack.enter_context(nc.sbuf_tensor("norms", [P, s.T], F32))
        lengths = stack.enter_context(nc.sbuf_tensor("lengths", [P, s.T], F32))
        hyperbolic_messages(nc, k, s, dst_plan, t["H"], edges, norms)
        hyperbolic_fold(nc, k, s, dst_plan, edges, norms, lengths)
        hyperbolic_results(nc, k, s, dst_plan, t["H"], edges, lengths)
        third_norm(nc, k, s, t["X"], t["H"])
        filter_messages(nc, k, s, dst_plan, L3, a["edge_attr_50"], t["H"], edges, carry)
        scatter_sums(nc, s, dst_plan, t["S"], edges, carry, "scatter3")
        last_update(nc, k, s, L3, t["X"], t["S"], t["out"])


def tables(nc, s):
    def dram(name, shape):
        return nc.dram_tensor(name, shape, F32, kind="Internal").ap()
    return {"H": dram("normed", (s.NP, D)), "Y": dram("attended", (s.NP, D)), "U": dram("mlp_out", (s.chunks * P, CH)),
            "X": dram("stream", (s.NP, D)), "S": dram("sums", (s.NP, D)),
            "rec_src": dram("rec_src", (s.EP, REC)), "rec_dst": dram("rec_dst", (s.EP, REC))}


def kernel(**inputs):
    import numpy as np
    from concourse import bacc
    from concourse.bass_utils import run_bass_kernel_spmd

    nc = bacc.Bacc("TRN2", target_bir_lowering=False, num_devices=1)
    arrays, a = {}, {}
    for name, value in inputs.items():
        arrays[f"in_{name}"] = np.ascontiguousarray(value)
        a[name] = nc.dram_tensor(f"in_{name}", arrays[f"in_{name}"].shape, mybir.dt.from_np(arrays[f"in_{name}"].dtype),
                                 kind="ExternalInput").ap()
    a["out"] = nc.dram_tensor("out", inputs["x"].shape, F32, kind="ExternalOutput").ap()
    t = tables(nc, Shapes(inputs["x"].shape[0], inputs["src"].shape[0]))
    t["out"] = a["out"]
    program(nc, a, t)
    r = run_bass_kernel_spmd(nc, [arrays], core_ids=[0])
    return r.results[0]["out"]
```

```python
import math
from contextlib import ExitStack


import concourse.bass as bass
import concourse.mybir as mybir

P = 128
D = 128
J = 4
R = 4
CH = P * J
HID = 512
HEADS = 8
DH = D // HEADS
NG = 50
LO_BITS = 9
LO = 1 << LO_BITS
SKIP = 1 << 20
LN_EPS = 1e-5
HYP_EPS = 1e-7
CUTOFF = 6.0

F32 = mybir.dt.float32
F16 = mybir.dt.float16
BF16 = mybir.dt.bfloat16
I32 = mybir.dt.int32
U32 = mybir.dt.uint32
ALU = mybir.AluOpType
ACT = mybir.ActivationFunctionType
AX = mybir.AxisListType

REC_KEY, REC_OTHER, REC_ID, REC_WEIGHT, REC = 0, 1, 2, 3, 4


class Shapes:

    def __init__(self, n_nodes, n_edges):
        self.N, self.E = n_nodes, n_edges
        self.chunks = -(-n_nodes // CH)
        self.chunks += self.chunks % 2
        self.NP = self.chunks * CH
        self.full = (n_nodes // CH)
        self.tail = n_nodes - (self.chunks - 1) * CH
        assert 0 < self.tail < CH and self.tail % J == 0
        self.tp = self.tail // J
        self.tiles = -(-n_edges // P)
        self.tiles += self.tiles % 2
        self.echunks = self.tiles * P // CH + 1
        self.echunks += self.echunks % 2
        self.T = self.echunks * J
        self.EP = self.T * P
        assert self.EP > self.tiles * P and n_nodes + 1 <= P * LO


def after(eng, sem, value):
    if isinstance(value, int) and value <= 0:
        return
    eng.wait_ge(sem, value)


def each(eng, n, body, ring=2, peel=1):
    front = min(peel * ring, n)
    loops = max((n - front - 1) // ring, 0)
    for c in range(front):
        body(c, c % ring)
    if loops:
        with eng.Fori(peel, peel + loops) as i:
            for u in range(ring):
                body(i * ring + u, u)
    for c in range(front + loops * ring, n):
        body(c, c % ring)


def each_phases(eng, n, phases, ring=2):
    lags = len(phases)
    peel = -(-(lags + ring - 1) // ring)

    def body(c, u):
        for i, f in enumerate(phases):
            if f is not None and not (isinstance(c, int) and c < i):
                f(c - i, (u - i) % ring)
    each(eng, n, body, ring, peel)
    for c in range(n, n + lags - 1):
        for i, f in enumerate(phases):
            if f is not None and c - i < n:
                f(c - i, (c - i) % ring)




class Chain:

    def __init__(self, eng, sem, per):
        self.eng, self.sem, self.per = eng, sem, per
        self.base, self.n = 0, 0

    def step(self, c):
        self.base, self.n = c * self.per, 0

    def link(self, ins):
        ins.then_inc(self.sem, 1)
        self.n += 1
        assert self.n <= self.per
        self.eng.wait_ge(self.sem, self.base + self.n)


class Stage:

    def __init__(self, nc, name):
        self.nc, self.name, self.stack, self.sems = nc, name, ExitStack(), []

    def __enter__(self):
        return self

    def __exit__(self, *e):
        self.stack.close()
        if e[0] is None:
            self.nc.clear_and_free_semaphores([s.num for s in self.sems])
            self.nc.all_engine_barrier()

    def sb(self, name, shape, dt=F32):
        return self.stack.enter_context(self.nc.sbuf_tensor(f"{self.name}_{name}", shape, dt))

    def ps(self, name, shape, dt=F32):
        return self.stack.enter_context(self.nc.psum_tensor(f"{self.name}_{name}", shape, dt))

    def sem(self, name):
        s = self.nc.alloc_semaphore(f"{self.name}_{name}")
        self.sems.append(s)
        return s

    def run(self):
        return self.nc.Block()


def rows(table, c):
    return table[bass.ds(c * CH, CH), :].rearrange("(p j) d -> p j d", j=J)


def make_constants(nc, k):
    with Stage(nc, "consts") as st:
        made = st.sem("made")
        seen = st.sem("seen")
        with st.run() as block:

            @block.gpsimd
            def _(pool):
                n = 0
                for t, v in ((k.ident, 0.0), (k.lower, 1.0), (k.strict, 1.0), (k.shift, 0.0),
                             (k.unshift, 0.0), (k.ones, 1.0), (k.zero_col, 0.0), (k.e_first, 0.0),
                             (k.eps_col, LN_EPS), (k.half_col, 0.5)):
                    pool.memset(t[:], v).then_inc(made, 1)
                    n += 1
                pool.wait_ge(made, n)
                pool.affine_select(out=k.ident[:], in_=k.ident[:], compare_op=ALU.not_equal, fill=1.0,
                                   base=0, pattern=[[-1, P]], channel_multiplier=1).then_inc(made, 1)
                pool.affine_select(out=k.lower[:], in_=k.lower[:], compare_op=ALU.is_gt, fill=0.0,
                                   base=0, pattern=[[-1, P]], channel_multiplier=1).then_inc(made, 1)
                pool.affine_select(out=k.strict[:], in_=k.strict[:], compare_op=ALU.is_gt, fill=0.0,
                                   base=0, pattern=[[1, P]], channel_multiplier=-1).then_inc(made, 1)
                pool.affine_select(out=k.shift[:], in_=k.shift[:], compare_op=ALU.not_equal, fill=1.0,
                                   base=1, pattern=[[-1, P]], channel_multiplier=1).then_inc(made, 1)
                pool.affine_select(out=k.unshift[:], in_=k.unshift[:], compare_op=ALU.not_equal, fill=1.0,
                                   base=-1, pattern=[[-1, P]], channel_multiplier=1).then_inc(made, 1)
                pool.affine_select(out=k.e_first[:], in_=k.e_first[:], compare_op=ALU.not_equal, fill=1.0,
                                   base=0, pattern=[[0, 1]], channel_multiplier=1).then_inc(made, 1)
                n += 6
                pool.wait_ge(made, n)

            @block.vector
            def _(dve):
                dve.wait_ge(made, 16)
                nc.vector.tensor_copy(k.ident16[:], k.ident[:]).then_inc(seen, 1)
                dve.wait_ge(seen, 1)


def sort_edges(nc, k, s, key, other, weight, rec):
    full = s.E // P
    rem = s.E - full * P
    halves = [(0, min(full, P)), (P, max(full - P, 0))]
    with Stage(nc, f"sort_{key.tensor.name}") as st:
        raw = st.sb("raw", [P, 4, 2, P], I32)
        asf = st.sb("asf", [P, 5, 2, P])
        lanes = st.sb("lanes", [P, 5, 2 * P])
        recs = st.sb("recs", [P, 2 * P, REC])
        iota_i = st.sb("iota_i", [P, LO], I32)
        iota_h = st.sb("iota_h", [P, LO], F16)
        ids = st.sb("ids", [P, 2 * P], I32)
        pad = st.sb("pad", [P, (s.EP // P - s.tiles) * REC])
        hot_hi = st.sb("hot_hi", [P, R, P], BF16)
        hot_lo = st.sb("hot_lo", [P, R, LO], BF16)
        zeros = st.sb("zeros", [P, LO], BF16)
        scan = st.sb("scan", [P, LO])
        onesf = st.sb("onesf", [P, LO])
        rowtot = st.sb("rowtot", [P, 1])
        table = st.sb("table", [P, R, LO])
        hotT = st.sb("hotT", [P, R, P])
        diag = st.sb("diag", [P, R, P])
        junk = st.sb("junk", [P, LO])
        junk2 = st.sb("junk2", [P, P])
        rank = st.sb("rank", [P, R])
        base = st.sb("base", [P, R])
        place = st.sb("place", [P, R], U32)
        outrec = st.sb("outrec", [P, R, REC])
        psT = [st.ps(f"psT{i}", [P, 2 * P]) for i in range(2)]
        count = st.ps("count", [P, LO])
        look = [st.ps(f"look{i}", [P, LO]) for i in range(2)]
        psH = [st.ps(f"psH{i}", [P, P], BF16) for i in range(2)]
        psR = psT[0][:, 0:1]
        psK = [psT[i][:, 0:P] for i in range(2)]

        loaded, cleared, chain = st.sem("loaded"), st.sem("cleared"), st.sem("chain")
        split, turned, taken = st.sem("split"), st.sem("turned"), st.sem("taken")
        iotas, hot, counted = st.sem("iotas"), st.sem("hot"), st.sem("counted")
        totals, offsets, started = st.sem("totals"), st.sem("offsets"), st.sem("started")
        seeded = st.sem("seeded")
        t_hot, t_updated, t_hotT, t_copied, t_hotT_sb = (st.sem("t_hot"), st.sem("t_updated"), st.sem("t_hotT"),
                                                         st.sem("t_copied"), st.sem("t_hotT_sb"))
        t_diag, t_keys, t_rank, t_look, t_place = (st.sem("t_diag"), st.sem("t_keys"), st.sem("t_rank"),
                                                   st.sem("t_look"), st.sem("t_place"))
        t_rec, padded, pad_sent, tick = st.sem("t_rec"), st.sem("padded"), st.sem("pad_sent"), st.sem("tick")
        t_sent = [st.sem(f"t_sent{i}") for i in range(R)]
        n_loads = 3 * ((1 if halves[0][1] else 0) + (1 if halves[1][1] else 0) + (1 if rem else 0))
        rem_half, rem_row = full // P, full % P
        first_pad = s.tiles * P

        with st.run() as block:

            @block.sync
            def _(sp):
                sp.wait_ge(cleared, 4)
                for a, src in ((0, key), (1, other)):
                    for h, (t0, nt) in enumerate(halves):
                        if nt:
                            sp.dma_start(raw[0:nt, a, h, :], src[t0 * P:(t0 + nt) * P].rearrange("(t e) -> t e", e=P)).then_inc(loaded, 16)
                    if rem:
                        sp.dma_start(raw[rem_row:rem_row + 1, a, rem_half, 0:rem],
                                     src[full * P:s.E].rearrange("(t e) -> t e", t=1)).then_inc(loaded, 16)
                for h, (t0, nt) in enumerate(halves):
                    if nt:
                        sp.dma_start(asf[0:nt, 4, h, :], weight[t0 * P:(t0 + nt) * P].rearrange("(t e) -> t e", e=P)).then_inc(loaded, 16)
                if rem:
                    sp.dma_start(asf[rem_row:rem_row + 1, 4, rem_half, 0:rem],
                                 weight[full * P:s.E].rearrange("(t e) -> t e", t=1)).then_inc(loaded, 16)
                sp.wait_ge(padded, 2)
                sp.dma_start(rec[first_pad:s.EP, :].rearrange("(p t) r -> p (t r)", p=P), pad[:]).then_inc(pad_sent, 16)
                sp.wait_ge(pad_sent, 16)

            @block.gpsimd
            def _(pool):
                pool.memset(raw[:, 0], s.N).then_inc(cleared, 1)
                pool.memset(raw[:, 1], 0).then_inc(cleared, 1)
                pool.memset(asf[:, 4], 0.0).then_inc(cleared, 1)
                pool.memset(zeros[:], 0.0).then_inc(cleared, 1)
                pool.memset(onesf[:], 1.0).then_inc(iotas, 1)
                pool.iota(iota_i[:], [[1, LO]], base=0, channel_multiplier=0).then_inc(iotas, 1)
                pool.iota(ids[:], [[P, 2 * P]], base=0, channel_multiplier=1).then_inc(iotas, 1)
                pool.memset(pad[:], 0.0).then_inc(padded, 1)
                pool.wait_ge(padded, 1)
                pool.memset(pad[:].rearrange("p (t r) -> p t r", r=REC)[:, :, REC_KEY], float(s.N)).then_inc(padded, 1)

                bound = pool.to_reg(s.EP - 1)

                def send(t, u):
                    pool.wait_ge(t_place, t + 1)
                    pool.wait_ge(t_rec, t + 1)
                    pool.sem_inc(tick, 1)
                    pool.indirect_dma_start(out=rec, out_offset=bass.IndirectOffsetOnAxis(ap=place[:, u:u + 1], axis=0),
                                            in_=outrec[:, u, :], in_offset=None, bounds_check=bound,
                                            oob_is_err=False).then_inc(t_sent[u], 16)
                each(pool, s.tiles, send, R)
                all_landed(pool, t_sent, s.tiles)

            @block.vector
            def _(dve):
                ch = Chain(dve, chain, 8)
                dve.wait_ge(loaded, 16 * n_loads)
                dve.wait_ge(iotas, 3)
                nc.vector.tensor_scalar(raw[:, 2], raw[:, 0], LO_BITS, None, ALU.logical_shift_right).then_inc(chain, 1)
                nc.vector.tensor_scalar(raw[:, 3], raw[:, 0], LO - 1, None, ALU.bitwise_and).then_inc(chain, 1)
                nc.vector.tensor_copy(iota_h[:], iota_i[:]).then_inc(chain, 1)
                dve.wait_ge(chain, 3)
                nc.vector.tensor_copy(asf[:, 0:4], raw[:]).then_inc(split, 1)
                nc.vector.tensor_copy(recs[:, :, REC_ID], ids[:]).then_inc(chain, 1)
                for a in range(5):
                    dve.wait_ge(turned, a + 1)
                    nc.vector.tensor_copy(lanes[:, a, :], psT[a % 2][:]).then_inc(taken, 1)
                dve.wait_ge(taken, 5)
                nc.vector.tensor_copy(recs[:, :, REC_KEY], lanes[:, 0, :]).then_inc(chain, 1)
                nc.vector.tensor_copy(recs[:, :, REC_OTHER], lanes[:, 1, :]).then_inc(chain, 1)
                nc.vector.tensor_copy(recs[:, :, REC_WEIGHT], lanes[:, 4, :]).then_inc(chain, 1)
                dve.wait_ge(chain, 7)

                def one_hots(t, u):
                    nc.vector.tensor_scalar(hot_hi[:, u, :], iota_h[:, 0:P], lanes[:, 2, bass.ds(t, 1)], None, ALU.is_equal)
                    return nc.vector.tensor_scalar(hot_lo[:, u, :], iota_h[:], lanes[:, 3, bass.ds(t, 1)], None, ALU.is_equal)

                def count_step(t, u):
                    after(dve, counted, t - R + 1)
                    one_hots(t, u).then_inc(hot, 1)
                each(dve, s.tiles, count_step, R)
                dve.wait_ge(counted, s.tiles)
                nc.vector.tensor_tensor_scan(scan[:], onesf[:], count[:], 0.0, ALU.mult, ALU.add).then_inc(chain, 1)
                dve.wait_ge(chain, 8)
                nc.vector.tensor_copy(rowtot[:], scan[:, LO - 1:LO]).then_inc(totals, 1)
                nc.vector.tensor_tensor(junk[:], scan[:], count[:], ALU.subtract).then_inc(chain, 1)
                dve.wait_ge(offsets, 1)
                dve.wait_ge(chain, 9)
                nc.vector.tensor_scalar(table[:, 1, :], junk[:], psR, None, ALU.add).then_inc(started, 1)

                def hot_rows(t, u):
                    after(dve, t_updated, t - R + 1)
                    one_hots(t, u).then_inc(t_hot, 1)
                    after(dve, t_keys, t - R + 1)
                    nc.vector.tensor_scalar(diag[:, u, :], k.ident[:], lanes[:, 0, bass.ds(t, 1)], None, ALU.mult).then_inc(t_diag, 1)

                def look_up(t, u):
                    dve.wait_ge(t_keys, t + 1)
                    after(dve, t_rank, 2 * t)
                    after(dve, t_place, t - R + 1)
                    nc.vector.scalar_tensor_tensor(junk2[:], psK[u % 2], lanes[:, 0, bass.ds(t, 1)], k.lower[:],
                                                   ALU.is_equal, ALU.mult, accum_out=rank[:, u:u + 1]).then_inc(t_rank, 1)
                    dve.wait_ge(t_look, t + 1)
                    nc.vector.scalar_tensor_tensor(junk[:], look[u % 2][:], 1.0, hot_lo[:, u, :],
                                                   ALU.mult, ALU.mult, accum_out=base[:, u:u + 1]).then_inc(t_rank, 1)

                def put(t, u):
                    dve.wait_ge(t_rank, 2 * t + 2)
                    sent(dve, t_sent, t, u)
                    nc.vector.tensor_tensor(place[:, u:u + 1], rank[:, u:u + 1], base[:, u:u + 1], ALU.add).then_inc(t_place, 1)
                    nc.vector.tensor_copy(outrec[:, u, :], recs[:].rearrange("p t r -> p (t r)")[:, bass.ds(t * REC, REC)]).then_inc(t_rec, 1)
                each_phases(dve, s.tiles, [hot_rows, None, look_up, put], R)

            @block.tensor
            def _(pe):
                pe.wait_ge(split, 1)
                for a in range(5):
                    after(pe, taken, a - 1)
                    nc.tensor.transpose(psT[a % 2][:, 0:P], asf[:, a, 0, :], k.ident[:])
                    nc.tensor.transpose(psT[a % 2][:, P:2 * P], asf[:, a, 1, :], k.ident[:]).then_inc(turned, 1)
                pe.wait_ge(cleared, 4)
                nc.tensor.matmul(count[:], zeros[:, 0:P], zeros[:], start=True, stop=False, skip_group_check=True)

                def count_step(t, u):
                    pe.wait_ge(hot, t + 1)
                    nc.tensor.matmul(count[:], hot_hi[:, u, :], hot_lo[:, u, :], start=False, stop=False,
                                     skip_group_check=True).then_inc(counted, 1)
                each(pe, s.tiles, count_step, R)
                pe.wait_ge(totals, 1)
                nc.tensor.matmul(psR, k.strict[:], rowtot[:], start=True, stop=True).then_inc(offsets, 1)
                pe.wait_ge(started, 1)
                nc.tensor.matmul(count[:], k.ident[:], table[:, 1, :], start=True, stop=False,
                                 skip_group_check=True).then_inc(seeded, 1)

                def update(t, u):
                    pe.wait_ge(t_hot, t + 1)
                    after(pe, t_hotT_sb, t - 1)
                    nc.tensor.transpose(psH[u % 2][:], hot_hi[:, u, :], k.ident16[:]).then_inc(t_hotT, 1)
                    pe.wait_ge(t_copied, t + 1)
                    nc.tensor.matmul(count[:], hot_hi[:, u, :], hot_lo[:, u, :], start=False, stop=False,
                                     skip_group_check=True).then_inc(t_updated, 1)

                def look_up(t, u):
                    pe.wait_ge(t_hotT_sb, t + 1)
                    after(pe, t_rank, 2 * t - 2)
                    nc.tensor.matmul(look[u % 2][:], hotT[:, u, :], table[:, u, :], start=True, stop=True).then_inc(t_look, 1)
                    pe.wait_ge(t_diag, t + 1)
                    nc.tensor.matmul(psK[u % 2], k.ones[:], diag[:, u, :], start=True, stop=True).then_inc(t_keys, 1)
                each_phases(pe, s.tiles, [update, look_up], R)

            @block.scalar
            def _(act):
                act.wait_ge(seeded, 1)

                def copies(t, u):
                    after(act, t_updated, t)
                    after(act, t_look, t - R + 1)
                    nc.scalar.copy(table[:, u, :], count[:]).then_inc(t_copied, 1)
                    act.wait_ge(t_hotT, t + 1)
                    nc.scalar.copy(hotT[:, u, :], psH[u % 2][:]).then_inc(t_hotT_sb, 1)
                each(act, s.tiles, copies, R)


def edge_plan(nc, k, s, rec, plan):
    T = s.T
    with Stage(nc, f"plan_{plan.name}") as st:
        r = st.sb("r", [P, T, REC])
        keyf = st.sb("keyf", [P, T + 2])
        tmp = st.sb("tmp", [P, T])
        real = st.sb("real", [P, T])
        lastf = st.sb("lastf", [P, T])
        ones = st.sb("ones", [P, T])
        diag = st.sb("diag", [P, P])
        cc = st.sb("cc", [P, 1])
        psE = st.ps("psE", [P, 8])
        psB = st.ps("psB", [P, P])
        loaded, chain = st.sem("loaded"), st.sem("chain")
        keys, ends, first, firsts = st.sem("keys"), st.sem("ends"), st.sem("first"), st.sem("firsts")
        counts, carried = st.sem("counts"), st.sem("carried")
        ones_made = st.sem("ones_made")
        with st.run() as block:

            @block.sync
            def _(sp):
                sp.dma_start(r[:], rec[:, :].rearrange("(p t) r -> p t r", p=P)).then_inc(loaded, 16)
                sp.wait_ge(loaded, 16)

            @block.gpsimd
            def _(pool):
                pool.memset(ones[:], 1.0).then_inc(ones_made, 1)

            @block.vector
            def _(dve):
                ch = Chain(dve, chain, 99)
                key = keyf[:, 1:T + 1]
                dve.wait_ge(loaded, 16)
                nc.vector.tensor_copy(key, r[:, :, REC_KEY]).then_inc(keys, 1)
                nc.vector.tensor_copy(plan.other[:], r[:, :, REC_OTHER])
                nc.vector.tensor_copy(plan.edge[:], r[:, :, REC_ID])
                nc.vector.tensor_copy(plan.weight[:], r[:, :, REC_WEIGHT])
                dve.wait_ge(keys, 1)
                nc.vector.tensor_scalar(diag[:], k.ident[:], keyf[:, 1:2], None, ALU.mult).then_inc(first, 1)
                dve.wait_ge(ends, 1)
                nc.vector.tensor_tensor(keyf[:, 0:1], psE[:, 0:1], k.e_first[:], ALU.subtract)
                ch.link(nc.vector.tensor_copy(keyf[:, T + 1:T + 2], psE[:, 1:2]))
                nc.vector.tensor_tensor(plan.same[:], key, keyf[:, 0:T], ALU.is_equal)
                nc.vector.tensor_tensor(lastf[:], key, keyf[:, 2:T + 2], ALU.not_equal)
                nc.vector.tensor_scalar(real[:], key, float(s.N), None, ALU.is_lt)
                nc.vector.tensor_scalar(plan.first[:], key, keyf[:, 1:2], None, ALU.is_equal)
                ch.link(nc.vector.tensor_tensor(tmp[:], key, key, ALU.bypass))
                ch.link(nc.vector.tensor_tensor(lastf[:], lastf[:], real[:], ALU.mult))
                nc.vector.tensor_copy(plan.cont[:], plan.same[:, 0:1])
                ch.link(nc.vector.tensor_tensor(tmp[:], key, real[:], ALU.mult))
                ch.link(nc.vector.tensor_copy(plan.key[:], tmp[:]))
                ch.link(nc.vector.tensor_scalar(tmp[:], lastf[:], -float(SKIP), float(SKIP), ALU.mult, ALU.add))
                ch.link(nc.vector.tensor_tensor(lastf[:], lastf[:], key, ALU.mult))
                ch.link(nc.vector.tensor_tensor(plan.last[:], tmp[:], lastf[:], ALU.add))
                ch.link(nc.vector.memset(plan.same[:, 0:1], 1.0))
                dve.wait_ge(firsts, 1)
                ch.link(nc.vector.scalar_tensor_tensor(plan.carry[:], psB[:], keyf[:, T:T + 1], k.strict[:],
                                                       ALU.is_equal, ALU.mult))
                dve.wait_ge(ones_made, 1)
                ch.link(nc.vector.tensor_tensor_scan(plan.count[:], plan.same[:], ones[:], 0.0, ALU.mult, ALU.add))
                nc.vector.tensor_copy(tmp[:, 0:1], plan.count[:, T - 1:T]).then_inc(counts, 1)
                dve.wait_ge(carried, 1)
                ch.link(nc.vector.tensor_copy(cc[:], psE[:, 2:3]))
                ch.link(nc.vector.scalar_tensor_tensor(plan.count[:], plan.first[:], cc[:], plan.count[:],
                                                       ALU.mult, ALU.add))
                ch.link(nc.vector.reciprocal(plan.inv[:], plan.count[:]))
                ch.link(nc.vector.tensor_tensor(plan.through[:], keyf[:, 1:2], keyf[:, T:T + 1], ALU.is_equal))
                ch.link(nc.vector.tensor_tensor(plan.through[:], plan.through[:], plan.cont[:], ALU.mult))
                ch.link(nc.vector.tensor_tensor(plan.through[:], plan.through[:], real[:, 0:1], ALU.mult))

            @block.tensor
            def _(pe):
                pe.wait_ge(keys, 1)
                nc.tensor.matmul(psE[:, 0:1], k.shift[:], keyf[:, T:T + 1], start=True, stop=True)
                nc.tensor.matmul(psE[:, 1:2], k.unshift[:], keyf[:, 1:2], start=True, stop=True).then_inc(ends, 1)
                pe.wait_ge(first, 1)
                nc.tensor.matmul(psB[:], k.ones[:], diag[:], start=True, stop=True).then_inc(firsts, 1)
                pe.wait_ge(counts, 1)
                nc.tensor.matmul(psE[:, 2:3], plan.carry[:], tmp[:, 0:1], start=True, stop=True).then_inc(carried, 1)


class Constants:
    def __init__(self, stack, nc):
        def sb(name, shape, dt=F32):
            return stack.enter_context(nc.sbuf_tensor(name, shape, dt))
        self.ident, self.ident16 = sb("ident", [P, P]), sb("ident16", [P, P], BF16)
        self.ones = sb("ones", [P, P])
        self.lower, self.strict = sb("lower", [P, P]), sb("strict", [P, P])
        self.shift, self.unshift = sb("shift", [P, P]), sb("unshift", [P, P])
        self.zero_col, self.e_first = sb("zero_col", [P, 1]), sb("e_first", [P, 1])
        self.eps_col, self.half_col = sb("eps_col", [P, 1]), sb("half_col", [P, 1])


class Plan:

    def __init__(self, stack, nc, s, name):
        def sb(n, shape, dt=F32):
            return stack.enter_context(nc.sbuf_tensor(f"{name}_{n}", shape, dt))
        T = s.T
        self.name = name
        self.key, self.other, self.edge = sb("key", [P, T], U32), sb("other", [P, T], U32), sb("edge", [P, T], U32)
        self.last = sb("last", [P, T], U32)
        self.weight = sb("weight", [P, T])
        self.same = sb("same", [P, T])
        self.first = sb("first", [P, T])
        self.count, self.inv = sb("count", [P, T]), sb("inv", [P, T])
        self.carry = sb("carry", [P, P])
        self.cont, self.through = sb("cont", [P, 1]), sb("through", [P, 1])


def sent(eng, sems, c, u, per=1):
    ring = len(sems)
    if isinstance(c, int):
        after(eng, sems[u], 16 * per * ((c - u) // ring))
    else:
        eng.wait_ge(sems[u], (c - u) * (16 * per // ring))


def landed(eng, sems, c, u, per=1):
    eng.wait_ge(sems[u], (c - u) * (16 * per // len(sems)) + 16 * per)


def all_landed(eng, sems, n, per=1):
    for u, sem in enumerate(sems):
        eng.wait_ge(sem, -(-(n - u) // len(sems)) * 16 * per)


class Norm:

    def __init__(self, nc, st, k):
        self.nc, self.k = nc, k
        self.stats = st.sb("ln_stats", [P, R, J, 6])
        self.mv = st.sb("ln_mv", [P, R, J, 2])
        self.std = st.sb("ln_std", [P, R, J])
        self.scale = st.sb("ln_scale", [P, R, J])
        self.bias = st.sb("ln_bias", [P, R, J])
        self.halves, self.moments, self.roots, self.coefs = (st.sem("ln_halves"), st.sem("ln_moments"),
                                                             st.sem("ln_roots"), st.sem("ln_coefs"))
        self.scaled, self.tick = st.sem("ln_scaled"), st.sem("ln_tick")

    def dve_moments(self, dve, x, c, u):
        for j in range(J):
            last = self.nc.vector.bn_stats(self.stats[:, u, j, :], x[:, j, :])
        last.then_inc(self.halves, 1)
        dve.wait_ge(self.halves, c + 1)
        after(dve, self.coefs, c - R + 1)
        dve.sem_inc(self.tick, 1)
        for j in range(J):
            last = self.nc.vector.bn_aggr(self.mv[:, u, j, :], self.stats[:, u, j, :])
        last.then_inc(self.moments, 1)

    def act_root(self, act, c, u):
        act.wait_ge(self.moments, c + 1)
        after(act, self.scaled, c - R + 1)
        self.nc.scalar.activation(self.std[:, u, :], self.mv[:, u, :, 1], ACT.Sqrt,
                                  bias=self.k.eps_col[:]).then_inc(self.roots, 1)

    def dve_coefs(self, dve, c, u, used):
        dve.wait_ge(self.roots, c + 1)
        used()
        self.nc.vector.reciprocal(self.scale[:, u, :], self.std[:, u, :]).then_inc(self.scaled, 1)
        dve.wait_ge(self.scaled, c + 1)
        self.nc.vector.scalar_tensor_tensor(self.bias[:, u, :], self.mv[:, u, :, 0], -1.0, self.scale[:, u, :],
                                            ALU.mult, ALU.mult).then_inc(self.coefs, 1)

    def act_apply(self, act, h, x, c, u):
        act.wait_ge(self.coefs, c + 1)
        for j in range(J):
            last = self.nc.scalar.activation(h[:, j, :], x[:, j, :], ACT.Relu, bias=self.bias[:, u, j:j + 1],
                                             scale=self.scale[:, u, j:j + 1])
        return last


def rows_product(nc, out, lhsT, w, bias, k):
    for j in range(J):
        nc.tensor.matmul(out[:, j * D:(j + 1) * D], lhsT[:, j * P:(j + 1) * P], w[:], start=j == 0, stop=False,
                         skip_group_check=True)
    return nc.tensor.matmul(out[:], k.ones[0:1, :], bias, start=False, stop=True, skip_group_check=True)


def load_x(nc, sp, s, x, dst, c, sem):
    if isinstance(c, int) and c == s.chunks - 1:
        r0 = c * CH
        sp.dma_start(dst[0:s.tp], x[r0:s.N, :].rearrange("(p j) d -> p j d", j=J)).then_inc(sem, 16)
        sp.dma_start(dst[s.tp:P], x[0:(P - s.tp) * J, :].rearrange("(p j) d -> p j d", j=J)).then_inc(sem, 16)
    else:
        sp.dma_start(dst, rows(x, c)).then_inc(sem, 16)


def first_norm(nc, k, s, x, wv, bv, wo, bo, H, Y):
    with Stage(nc, "norm0") as st:
        norm = Norm(nc, st, k)
        xin = st.sb("xin", [P, R, J, D])
        h = st.sb("h", [P, R, J, D])
        hT = st.sb("hT", [P, R, CH])
        y = st.sb("y", [P, R, J, D])
        wv_sb, wo_sb, mean = st.sb("wv", [P, D]), st.sb("wo", [P, D]), st.sb("mean", [P, D])
        wvT, wmean, wc = st.sb("wvT", [P, D]), st.sb("wmean", [P, D]), st.sb("wc", [P, D])
        bv_sb, bo_sb = st.sb("bv", [P, 1]), st.sb("bo", [1, D])
        bias = st.sb("bias", [1, J, D])
        headi = st.sb("headi", [P, D], I32)
        psT = [st.ps(f"psT{i}", [P, CH]) for i in range(2)]
        psY = [st.ps(f"psY{i}", [P, CH]) for i in range(2)]
        psW = st.ps("psW", [P, 4, P])
        weights, prep, mixed, used = st.sem("weights"), st.sem("prep"), st.sem("mixed"), st.sem("used")
        xl = [st.sem(f"xl{i}") for i in range(R)]
        hs = [st.sem(f"hs{i}") for i in range(R)]
        ys = [st.sem(f"ys{i}") for i in range(R)]
        h_done, hT_ps, hT_sb, y_ps, y_sb = (st.sem("h_done"), st.sem("hT_ps"), st.sem("hT_sb"),
                                            st.sem("y_ps"), st.sem("y_sb"))
        n = s.chunks
        with st.run() as block:

            @block.sync
            def _(sp):
                for dst, src in ((wv_sb, wv[:, :]), (wo_sb, wo[:, :]), (bv_sb, column(bv)), (bo_sb, row(bo))):
                    sp.dma_start(dst[:], src).then_inc(weights, 16)

                def load(c, u):
                    after(sp, h_done, c - R + 1)
                    load_x(nc, sp, s, x, xin[:, u], c, xl[u])

                def store(c, u):
                    sp.wait_ge(h_done, c + 1)
                    sp.dma_start(rows(H, c), h[:, u]).then_inc(hs[u], 16)
                    sp.wait_ge(y_sb, c + 1)
                    sp.dma_start(rows(Y, c), y[:, u]).then_inc(ys[u], 16)
                each_phases(sp, n, [load, None, None, store], R)
                all_landed(sp, hs, n)
                all_landed(sp, ys, n)

            @block.gpsimd
            def _(pool):
                pool.iota(headi[:], [[-1, D]], base=D, channel_multiplier=1).then_inc(prep, 1)

            @block.vector
            def _(dve):
                dve.wait_ge(prep, 1)
                nc.vector.tensor_scalar(headi[:], headi[:], DH - 1, None, ALU.bitwise_and).then_inc(prep, 1)
                dve.wait_ge(prep, 2)
                nc.vector.tensor_copy(mean[:], headi[:]).then_inc(prep, 1)
                dve.wait_ge(prep, 3)
                nc.vector.tensor_scalar(mean[:], mean[:], 0.0, 1.0 / HEADS, ALU.is_equal, ALU.mult).then_inc(prep, 1)
                dve.wait_ge(mixed, 2)
                nc.vector.tensor_copy(wvT[:], psW[:, 0, :])
                nc.vector.tensor_copy(wmean[:], psW[:, 1, :]).then_inc(used, 1)
                dve.wait_ge(mixed, 4)
                nc.vector.tensor_tensor(wc[:], psW[:, 2, :], k.ident[:], ALU.add)
                for j in range(J):
                    last = nc.vector.tensor_tensor(bias[0:1, j, :], psW[0:1, 3, :], bo_sb[:], ALU.add)
                last.then_inc(used, 1)

                def stats(c, u):
                    if isinstance(c, int) and c == n - 1:
                        dve.wait_ge(xl[u], 16 * (c // R + 2))
                    else:
                        landed(dve, xl, c, u)
                    norm.dve_moments(dve, xin[:, u], c, u)
                    norm.dve_coefs(dve, c, u, lambda: after(dve, h_done, c - R + 1))

                def take(c, u):
                    dve.wait_ge(hT_ps, c + 1)
                    after(dve, y_ps, c - R + 1)
                    nc.vector.tensor_copy(hT[:, u, :], psT[u % 2][:]).then_inc(hT_sb, 1)
                each_phases(dve, n, [stats, take], R)

            @block.scalar
            def _(act):
                def normed(c, u):
                    norm.act_root(act, c, u)
                    sent(act, hs, c, u)
                    after(act, hT_ps, c - R + 1)
                    norm.act_apply(act, h[:, u], xin[:, u], c, u).then_inc(h_done, 1)

                def take(c, u):
                    act.wait_ge(y_ps, c + 1)
                    sent(act, ys, c, u)
                    nc.scalar.copy(y[:, u].rearrange("p j d -> p (j d)"), psY[u % 2][:]).then_inc(y_sb, 1)
                each_phases(act, n, [normed, take], R)

            @block.tensor
            def _(pe):
                pe.wait_ge(weights, 16 * 4)
                pe.wait_ge(prep, 4)
                nc.tensor.transpose(psW[:, 0, :], wv_sb[:], k.ident[:]).then_inc(mixed, 1)
                nc.tensor.matmul(psW[:, 1, :], mean[:], wo_sb[:], start=True, stop=True).then_inc(mixed, 1)
                pe.wait_ge(used, 1)
                nc.tensor.matmul(psW[:, 2, :], wvT[:], wmean[:], start=True, stop=True).then_inc(mixed, 1)
                nc.tensor.matmul(psW[0:1, 3, :], bv_sb[:], wmean[:], start=True, stop=True).then_inc(mixed, 1)
                pe.wait_ge(used, 2)

                def turn(c, u):
                    pe.wait_ge(h_done, c + 1)
                    after(pe, hT_sb, c - 1)
                    for j in range(J):
                        last = nc.tensor.transpose(psT[u % 2][:, j * P:(j + 1) * P], h[:, u, j, :], k.ident[:])
                    last.then_inc(hT_ps, 1)

                def mix(c, u):
                    pe.wait_ge(hT_sb, c + 1)
                    after(pe, y_sb, c - 1)
                    rows_product(nc, psY[u % 2], hT[:, u], wc, bias[:].rearrange("a j d -> a (j d)"), k).then_inc(y_ps, 1)
                each_phases(pe, n, [turn, mix], R)


def column(v):
    return v.rearrange("(p a) -> p a", a=1)


def row(v):
    return v.rearrange("(a p) -> a p", a=1)


def sum_neighbours(nc, k, s, plan, H, edges, carry):
    with Stage(nc, "sum0") as st:
        got_rows = st.sb("rows", [P, 2, J, D])
        idx = st.sb("idx", [P, 2, J], U32)
        psC = st.ps("psC", [P, D])
        idx_ready, chain, tick = st.sem("idx_ready"), st.sem("chain"), st.sem("tick")
        zeroed, carried, taken = st.sem("zeroed"), st.sem("carried"), st.sem("taken")
        got = [st.sem(f"got{i}") for i in range(2)]
        n = s.echunks
        with st.run() as block:

            @block.gpsimd
            def _(pool):
                bound = pool.to_reg(s.NP - 1)

                def gather(c, u):
                    pool.wait_ge(idx_ready, c + 1)
                    after(pool, chain, (c - 1) * J)
                    pool.sem_inc(tick, 1)
                    for q in range(J):
                        pool.indirect_dma_start(out=got_rows[:, u, q, :], out_offset=None, in_=H,
                                                in_offset=bass.IndirectOffsetOnAxis(ap=idx[:, u, q:q + 1], axis=0),
                                                bounds_check=bound, oob_is_err=False).then_inc(got[u], 16)
                each(pool, n, gather)

            @block.scalar
            def _(act):
                def index(c, u):
                    sent(act, got, c, u, J)
                    nc.scalar.copy(idx[:, u, :], plan.other[:, bass.ds(c * J, J)]).then_inc(idx_ready, 1)
                each(act, n, index)

            @block.vector
            def _(dve):
                ch = Chain(dve, chain, J)
                nc.vector.memset(edges[:, 0:D], 0.0).then_inc(zeroed, 1)
                dve.wait_ge(zeroed, 1)

                def add(c, u):
                    landed(dve, got, c, u, J)
                    ch.step(c)
                    for q in range(J):
                        ch.link(nc.vector.scalar_tensor_tensor(
                            edges[:, bass.ds((c * J + q + 1) * D, D)], edges[:, bass.ds((c * J + q) * D, D)],
                            plan.same[:, bass.ds(c * J + q, 1)], got_rows[:, u, q, :], ALU.mult, ALU.add))
                each(dve, n, add)
                dve.wait_ge(carried, 1)
                nc.vector.tensor_copy(carry[:], psC[:]).then_inc(taken, 1)
                dve.wait_ge(taken, 1)

            @block.tensor
            def _(pe):
                pe.wait_ge(chain, n * J)
                nc.tensor.matmul(psC[:], plan.carry[:], edges[:, s.T * D:], start=True, stop=True).then_inc(carried, 1)


def attend(nc, k, s, plan, L0, H, Y, edges, carry):
    with Stage(nc, "attend") as st:
        hs = st.sb("hs", [P, R, D])
        y = st.sb("y", [P, R, D])
        gidx, sidx = st.sb("gidx", [P, R], U32), st.sb("sidx", [P, R], U32)
        kin, kmean = st.sb("kin", [P, R, D]), st.sb("kmean", [P, R, D])
        turned = st.sb("turned", [P, 2, 2 * D])
        qvk = st.sb("qvk", [P, R, 3 * D])
        prod = st.sb("prod", [P, 1024])
        score, shifted, expd, prob = (st.sb("score", [P, 2, 64]), st.sb("shifted", [P, 2, 64]),
                                      st.sb("expd", [P, R, 64]), st.sb("prob", [P, 2, 64]))
        top, total, inv = st.sb("top", [P, 2, HEADS]), st.sb("total", [P, 2, HEADS]), st.sb("inv", [P, 2, HEADS])
        prod2 = st.sb("prod2", [P, 1024])
        mixed, mixedT = st.sb("mixed", [P, R, D]), st.sb("mixedT", [P, 2, D])
        wqv, wk, wo = st.sb("wqv", [P, 2 * D]), st.sb("wk", [P, D]), st.sb("wo", [P, D])
        bias, bo = st.sb("bias", [1, 3 * D]), st.sb("bo", [1, D])
        psT = [st.ps(f"psT{i}", [P, 2 * D]) for i in range(2)]
        psQ = [st.ps(f"psQ{i}", [P, 3 * D]) for i in range(2)]
        psM = st.ps("psM", [P, D])
        psO = [st.ps(f"psO{i}", [P, D]) for i in range(2)]
        weights, tick = st.sem("weights"), st.sem("tick")
        got = [st.sem(f"got{i}") for i in range(R)]
        put = [st.sem(f"put{i}") for i in range(R)]
        (gidx_ready, sidx_ready, kin_done, kmean_done, T_ps, T_sb, q_ps, q_sb) = (
            st.sem(x) for x in ("gidx_ready", "sidx_ready", "kin_done", "kmean_done", "T_ps", "T_sb", "q_ps", "q_sb"))
        chain, score_done, exp_done, mix_done, m_ps, m_sb, o_ps, y_done = (
            st.sem(x) for x in ("chain", "score_done", "exp_done", "mix_done", "m_ps", "m_sb", "o_ps", "y_done"))
        chain2 = st.sem("chain2")
        n = s.T
        with st.run() as block:

            @block.sync
            def _(sp):
                for dst, src in ((wqv[:, 0:D], L0["wq"][:, :]), (wqv[:, D:2 * D], L0["wv"][:, :]), (wk[:], L0["wk"][:, :]),
                                 (wo[:], L0["wo"][:, :]), (bias[:, 0:D], row(L0["bq"])), (bias[:, D:2 * D], row(L0["bv"])),
                                 (bias[:, 2 * D:3 * D], row(L0["bk"])), (bo[:], row(L0["bo"]))):
                    sp.dma_start(dst, src).then_inc(weights, 16)

            @block.gpsimd
            def _(pool):
                bound = pool.to_reg(s.N - 1)

                def gather(t, u):
                    pool.wait_ge(gidx_ready, t + 1)
                    after(pool, y_done, t - R + 1)
                    pool.sem_inc(tick, 1)
                    pool.indirect_dma_start(out=hs[:, u, :], out_offset=None, in_=H,
                                            in_offset=bass.IndirectOffsetOnAxis(ap=gidx[:, u:u + 1], axis=0),
                                            bounds_check=bound, oob_is_err=False).then_inc(got[u], 16)

                def scatter(t, u):
                    pool.wait_ge(y_done, t + 1)
                    pool.wait_ge(sidx_ready, t + 1)
                    pool.sem_inc(tick, 1)
                    pool.indirect_dma_start(out=Y, out_offset=bass.IndirectOffsetOnAxis(ap=sidx[:, u:u + 1], axis=0),
                                            in_=y[:, u, :], in_offset=None, bounds_check=bound,
                                            oob_is_err=False).then_inc(put[u], 16)
                each_phases(pool, n, [gather, None, None, None, scatter], R)
                all_landed(pool, put, n)

            @block.vector
            def _(dve):
                ch, ch2 = Chain(dve, chain, 3), Chain(dve, chain2, 4)

                def keys(t, u):
                    after(dve, kmean_done, t - R + 1)
                    nc.vector.scalar_tensor_tensor(kin[:, u, :], carry[:], plan.first[:, bass.ds(t, 1)],
                                                   edges[:, bass.ds((t + 1) * D, D)], ALU.mult, ALU.add).then_inc(kin_done, 1)

                def scores(t, u):
                    dve.wait_ge(q_sb, t + 1)
                    v = u % 2
                    q4 = qvk[:, u, 0:D].rearrange("p (h a d) -> p h a d", h=HEADS, a=1).broadcast_to([P, HEADS, HEADS, DH])
                    k4 = qvk[:, u, 2 * D:3 * D].rearrange("p (a g d) -> p a g d", a=1, g=HEADS).broadcast_to([P, HEADS, HEADS, DH])
                    ch.step(t)
                    ch.link(nc.vector.tensor_tensor(prod[:].rearrange("p (h g d) -> p h g d", h=HEADS, g=HEADS), q4, k4, ALU.mult))
                    ch.link(nc.vector.tensor_reduce(score[:, v, :], prod[:].rearrange("p (a d) -> p a d", d=DH), AX.X, ALU.add))
                    s3 = score[:, v, :].rearrange("p (h g) -> p h g", h=HEADS)
                    ch.link(nc.vector.tensor_reduce(top[:, v, :], s3, AX.X, ALU.max))
                    after(dve, exp_done, t - 1)
                    nc.vector.tensor_tensor(shifted[:, v, :].rearrange("p (h g) -> p h g", h=HEADS), s3,
                                            top[:, v, :].rearrange("p (h a) -> p h a", a=1).broadcast_to([P, HEADS, HEADS]),
                                            ALU.subtract).then_inc(score_done, 1)

                def mix(t, u):
                    dve.wait_ge(exp_done, t + 1)
                    v = u % 2
                    e3 = expd[:, u, :].rearrange("p (h g) -> p h g", h=HEADS)
                    ch2.step(t)
                    ch2.link(nc.vector.tensor_reduce(total[:, v, :], e3, AX.X, ALU.add))
                    ch2.link(nc.vector.reciprocal(inv[:, v, :], total[:, v, :]))
                    ch2.link(nc.vector.tensor_tensor(prob[:, v, :].rearrange("p (h g) -> p h g", h=HEADS), e3,
                                                     inv[:, v, :].rearrange("p (h a) -> p h a", a=1).broadcast_to([P, HEADS, HEADS]), ALU.mult))
                    p4 = prob[:, v, :].rearrange("p (h a g) -> p h a g", h=HEADS, a=1).broadcast_to([P, HEADS, DH, HEADS])
                    v4 = qvk[:, u, D:2 * D].rearrange("p (a g d) -> p a d g", a=1, g=HEADS).broadcast_to([P, HEADS, DH, HEADS])
                    ch2.link(nc.vector.tensor_tensor(prod2[:].rearrange("p (h d g) -> p h d g", h=HEADS, d=DH), p4, v4, ALU.mult))
                    after(dve, m_ps, t - R + 1)
                    nc.vector.tensor_reduce(mixed[:, u, :], prod2[:].rearrange("p (a g) -> p a g", g=HEADS), AX.X, ALU.add).then_inc(mix_done, 1)

                def result(t, u):
                    dve.wait_ge(o_ps, t + 1)
                    sent(dve, put, t, u)
                    nc.vector.tensor_tensor(y[:, u, :], psO[u % 2][:], hs[:, u, :], ALU.add).then_inc(y_done, 1)
                each_phases(dve, n, [None, keys, scores, mix, result], R)

            @block.scalar
            def _(act):
                def index(t, u):
                    sent(act, got, t, u)
                    nc.scalar.copy(gidx[:, u:u + 1], plan.key[:, bass.ds(t, 1)]).then_inc(gidx_ready, 1)

                def project(t, u):
                    act.wait_ge(kin_done, t + 1)
                    after(act, T_ps, t - R + 1)
                    nc.scalar.mul(kmean[:, u, :], kin[:, u, :], plan.inv[:, bass.ds(t, 1)]).then_inc(kmean_done, 1)
                    act.wait_ge(T_ps, t + 1)
                    after(act, q_ps, t - 1)
                    nc.scalar.copy(turned[:, u % 2, :], psT[u % 2][:]).then_inc(T_sb, 1)
                    act.wait_ge(q_ps, t + 1)
                    after(act, mix_done, t - R + 1)
                    nc.scalar.copy(qvk[:, u, :], psQ[u % 2][:]).then_inc(q_sb, 1)

                def exps(t, u):
                    act.wait_ge(score_done, t + 1)
                    after(act, mix_done, t - R + 1)
                    nc.scalar.activation(expd[:, u, :], shifted[:, u % 2, :], ACT.Exp).then_inc(exp_done, 1)

                def turn(t, u):
                    act.wait_ge(m_ps, t + 1)
                    after(act, o_ps, t - 1)
                    nc.scalar.copy(mixedT[:, u % 2, :], psM[:]).then_inc(m_sb, 1)
                    sent(act, put, t, u)
                    nc.scalar.copy(sidx[:, u:u + 1], plan.last[:, bass.ds(t, 1)]).then_inc(sidx_ready, 1)
                each_phases(act, n, [index, project, exps, turn], R)

            @block.tensor
            def _(pe):
                pe.wait_ge(weights, 16 * 8)

                def project(t, u):
                    v = u % 2
                    pe.wait_ge(kmean_done, t + 1)
                    landed(pe, got, t, u)
                    after(pe, T_sb, t - 1)
                    nc.tensor.transpose(psT[v][:, 0:D], kmean[:, u, :], k.ident[:])
                    nc.tensor.transpose(psT[v][:, D:2 * D], hs[:, u, :], k.ident[:]).then_inc(T_ps, 1)
                    pe.wait_ge(T_sb, t + 1)
                    after(pe, q_sb, t - 1)
                    nc.tensor.matmul(psQ[v][:, 0:2 * D], turned[:, v, D:2 * D], wqv[:], start=True, stop=False, skip_group_check=True)
                    nc.tensor.matmul(psQ[v][:, 2 * D:3 * D], turned[:, v, 0:D], wk[:], start=False, stop=False, skip_group_check=True)
                    nc.tensor.matmul(psQ[v][:], k.ones[0:1, :], bias[:], start=False, stop=True, skip_group_check=True).then_inc(q_ps, 1)

                def out(t, u):
                    v = u % 2
                    pe.wait_ge(mix_done, t + 1)
                    after(pe, m_sb, t)
                    nc.tensor.transpose(psM[:], mixed[:, u, :], k.ident[:]).then_inc(m_ps, 1)
                    pe.wait_ge(m_sb, t + 1)
                    after(pe, y_done, t - 1)
                    nc.tensor.matmul(psO[v][:], mixedT[:, v, :], wo[:], start=True, stop=False)
                    nc.tensor.matmul(psO[v][:], k.ones[0:1, :], bo[:], start=False, stop=True).then_inc(o_ps, 1)
                each_phases(pe, n, [None, project, None, out], R)


def batch_coefs(nc, dve, act_ready, ch, k, gain, shift, mean, var, std, scale, offset):
    dve.wait_ge(act_ready, 1)
    ch.link(nc.vector.reciprocal(scale[:], std[:]))
    ch.link(nc.vector.tensor_tensor(scale[:], scale[:], gain[:], ALU.mult))
    ch.link(nc.vector.tensor_tensor(offset[:], mean, scale[:], ALU.mult))
    ch.link(nc.vector.tensor_tensor(offset[:], shift[:], offset[:], ALU.subtract))


def node_moments(nc, k, s, Y, g1, be1, scale, offset):
    with Stage(nc, "moments") as st:
        y = st.sb("y", [P, R, J, D])
        sq = st.sb("sq", [P, R, J, D])
        acc = st.sb("acc", [P, J, D])
        acc2 = st.sb("acc2", [P, J, D])
        gain, shift = st.sb("gain", [P, 1]), st.sb("shift", [P, 1])
        mean, second, var, std = (st.sb(x, [P, 1]) for x in ("mean", "second", "var", "std"))
        psS = st.ps("psS", [P, 2])
        weights, zeroed, zeroed2 = st.sem("weights"), st.sem("zeroed"), st.sem("zeroed2")
        yl = [st.sem(f"yl{i}") for i in range(R)]
        added, squared, added2, folded, chain, root, var_done = (
            st.sem(x) for x in ("added", "squared", "added2", "folded", "chain", "root", "var_done"))
        n = s.chunks
        with st.run() as block:

            def live(buf, c, u):
                last = isinstance(c, int) and c == n - 1
                return buf[0:s.tp if last else P, u] if u is not None else buf[0:s.tp if last else P]

            @block.sync
            def _(sp):
                sp.dma_start(gain[:], column(g1)).then_inc(weights, 16)
                sp.dma_start(shift[:], column(be1)).then_inc(weights, 16)

                def load(c, u):
                    after(sp, added, c - R + 1)
                    after(sp, squared, c - R + 1)
                    sp.dma_start(y[:, u], rows(Y, c)).then_inc(yl[u], 16)
                each(sp, n, load, R)

            @block.vector
            def _(dve):
                nc.vector.memset(acc[:], 0.0).then_inc(zeroed, 1)
                dve.wait_ge(zeroed, 1)

                def add(c, u):
                    landed(dve, yl, c, u)
                    nc.vector.tensor_tensor(live(acc, c, None), live(acc, c, None), live(y, c, u), ALU.add).then_inc(added, 1)
                    dve.wait_ge(added, c + 1)
                each(dve, n, add, R)
                ch = Chain(dve, chain, 99)
                dve.wait_ge(folded, 1)
                ch.link(nc.vector.tensor_scalar(mean[:], psS[:, 0:1], 1.0 / s.N, None, ALU.mult))
                ch.link(nc.vector.tensor_scalar(second[:], psS[:, 1:2], 1.0 / s.N, None, ALU.mult))
                ch.link(nc.vector.tensor_tensor(var[:], mean[:], mean[:], ALU.mult))
                nc.vector.tensor_tensor(var[:], second[:], var[:], ALU.subtract).then_inc(var_done, 1)
                dve.wait_ge(weights, 32)
                batch_coefs(nc, dve, root, ch, k, gain, shift, mean[:], var, std, scale, offset)

            @block.scalar
            def _(act):
                def square(c, u):
                    landed(act, yl, c, u)
                    after(act, added2, c - R + 1)
                    nc.scalar.activation(sq[:, u], y[:, u], ACT.Square).then_inc(squared, 1)
                each(act, n, square, R)
                act.wait_ge(var_done, 1)
                nc.scalar.activation(std[:], var[:], ACT.Sqrt, bias=k.eps_col[:]).then_inc(root, 1)

            @block.gpsimd
            def _(pool):
                pool.memset(acc2[:], 0.0).then_inc(zeroed2, 1)
                pool.wait_ge(zeroed2, 1)

                def add(c, u):
                    pool.wait_ge(squared, c + 1)
                    nc.gpsimd.tensor_tensor(live(acc2, c, None), live(acc2, c, None), live(sq, c, u), ALU.add).then_inc(added2, 1)
                    pool.wait_ge(added2, c + 1)
                each(pool, n, add, R)

            @block.tensor
            def _(pe):
                for a, (src, done) in enumerate(((acc, added), (acc2, added2))):
                    pe.wait_ge(done, n)
                    for j in range(J):
                        last = nc.tensor.matmul(psS[:, a:a + 1], src[:, j, :], k.ones[:, 0:1], start=j == 0, stop=j == J - 1)
                last.then_inc(folded, 1)


def node_mlp(nc, k, s, L0, Y, U, scale, offset, scale2, offset2):
    M = HID // P
    with Stage(nc, "mlp") as st:
        y = st.sb("y", [P, R, J, D])
        t = st.sb("t", [P, R, CH])
        g = st.sb("g", [P, 2, M, CH])
        u_sb = st.sb("u", [P, R, CH])
        w1, w2 = st.sb("w1", [P, HID]), st.sb("w2", [P, M, D])
        b1, b2 = st.sb("b1", [P, M]), st.sb("b2", [P, 1])
        gain, shift, std = st.sb("gain", [P, 1]), st.sb("shift", [P, 1]), st.sb("std", [P, 1])
        stats, mv = st.sb("stats", [P, s.chunks, 6]), st.sb("mv", [P, 2])
        psT = [st.ps("psT0", [P, CH])]
        psG = [st.ps(f"psG{i}", [P, CH]) for i in range(M)]
        psU = [st.ps(f"psU{i}", [P, CH]) for i in range(2)]
        weights = st.sem("weights")
        yl = [st.sem(f"yl{i}") for i in range(R)]
        us = [st.sem(f"us{i}") for i in range(R)]
        T_ps, T_sb, G_ps, G_sb, U_ps, U_sb, stat, moments, root, chain = (
            st.sem(x) for x in ("T_ps", "T_sb", "G_ps", "G_sb", "U_ps", "U_sb", "stat", "moments", "root", "chain"))
        n = s.chunks
        with st.run() as block:

            @block.sync
            def _(sp):
                with nc.allow_non_contiguous_dma("biases as columns"):
                    for dst, src in ((w1[:], L0["w1"][:, :]), (w2[:], L0["w2"].rearrange("(m p) d -> p m d", p=P)),
                                     (b1[:], L0["b1"].rearrange("(m p) -> p m", p=P)), (b2[:], column(L0["b2"])),
                                     (gain[:], column(L0["g2"])), (shift[:], column(L0["be2"]))):
                        sp.dma_start(dst, src).then_inc(weights, 16)

                def load(c, u):
                    after(sp, T_ps, c - R + 1)
                    sp.dma_start(y[:, u], rows(Y, c)).then_inc(yl[u], 16)

                def store(c, u):
                    sp.wait_ge(U_sb, c + 1)
                    sp.dma_start(U[bass.ds(c * P, P), :], u_sb[:, u, :]).then_inc(us[u], 16)
                each_phases(sp, n, [load, None, None, store], R)
                all_landed(sp, us, n)

            @block.tensor
            def _(pe):
                pe.wait_ge(weights, 16 * 6)

                def turn(c, u):
                    landed(pe, yl, c, u)
                    after(pe, T_sb, c)
                    for j in range(J):
                        last = nc.tensor.transpose(psT[0][:, j * P:(j + 1) * P], y[:, u, j, :], k.ident[:])
                    last.then_inc(T_ps, 1)

                def up(c, u):
                    pe.wait_ge(T_sb, c + 1)
                    for m in range(M):
                        after(pe, G_sb, M * (c - 1) + m + 1)
                        nc.tensor.matmul(psG[m][:], w1[:, m * P:(m + 1) * P], t[:, u, :], start=True, stop=True).then_inc(G_ps, 1)

                def down(c, u):
                    after(pe, U_sb, c - 1)
                    for m in range(M):
                        pe.wait_ge(G_sb, M * c + m + 1)
                        last = nc.tensor.matmul(psU[u % 2][:], w2[:, m, :], g[:, u % 2, m, :], start=m == 0, stop=m == M - 1)
                    last.then_inc(U_ps, 1)

                def step(c, u):
                    up(c, u)
                    if not (isinstance(c, int) and c == n - 1):
                        turn(c + 1, (u + 1) % R)
                turn(0, 0)
                each_phases(pe, n, [step, down], R)

            @block.scalar
            def _(act):
                act.wait_ge(weights, 16 * 6)

                def turn(c, u):
                    act.wait_ge(T_ps, c + 1)
                    after(act, U_sb, c - R + 1)
                    nc.scalar.activation(t[:, u, :], psT[0][:], ACT.Identity, bias=offset[:], scale=scale[:]).then_inc(T_sb, 1)

                def step(c, u):
                    after(act, U_ps, c - 1)
                    for m in range(M):
                        act.wait_ge(G_ps, M * c + m + 1)
                        nc.scalar.activation(g[:, u % 2, m, :], psG[m][:], ACT.Gelu, bias=b1[:, m:m + 1]).then_inc(G_sb, 1)
                    if not (isinstance(c, int) and c == n - 1):
                        turn(c + 1, (u + 1) % R)
                turn(0, 0)
                each(act, n, step, R)
                act.wait_ge(moments, 1)
                nc.scalar.activation(std[:], mv[:, 1:2], ACT.Sqrt, bias=k.eps_col[:]).then_inc(root, 1)

            @block.vector
            def _(dve):
                dve.wait_ge(weights, 16 * 6)

                def finish(c, u):
                    dve.wait_ge(U_ps, c + 1)
                    sent(dve, us, c, u)
                    nc.vector.scalar_tensor_tensor(u_sb[:, u, :], psU[u % 2][:], b2[:], t[:, u, :], ALU.add, ALU.add).then_inc(U_sb, 1)
                    dve.wait_ge(U_sb, c + 1)
                    out = stats[:].rearrange("p c x -> p (c x)")[:, bass.ds(c * 6, 6)]
                    real = u_sb[:, u, :]
                    if isinstance(c, int) and c == n - 1:
                        real = real.rearrange("f (j p) -> f j p", j=J)[:, :, 0:s.tp]
                    nc.vector.bn_stats(out, real).then_inc(stat, 1)
                each(dve, n, finish, R)
                dve.wait_ge(stat, n)
                nc.vector.bn_aggr(mv[:], stats[:].rearrange("p c x -> p (c x)")).then_inc(moments, 1)
                ch = Chain(dve, chain, 99)
                batch_coefs(nc, dve, root, ch, k, gain, shift, mv[:, 0:1], None, std, scale2, offset2)


def second_norm(nc, k, s, x, U, X, H, scale2, offset2):
    with Stage(nc, "norm1") as st:
        norm = Norm(nc, st, k)
        uin, z = st.sb("uin", [P, R, CH]), st.sb("z", [P, R, CH])
        xin, x1, h = (st.sb(v, [P, R, J, D]) for v in ("xin", "x1", "h"))
        psZ = [st.ps(f"psZ{i}", [P, CH]) for i in range(2)]
        ul, xl, xs, hs = ([st.sem(f"{v}{i}") for i in range(R)] for v in ("ul", "xl", "xs", "hs"))
        z_done, z_ps, x_done, h_done = (st.sem(v) for v in ("z_done", "z_ps", "x_done", "h_done"))
        n = s.chunks
        with st.run() as block:

            @block.sync
            def _(sp):
                def load(c, u):
                    after(sp, z_done, c - R + 1)
                    sp.dma_start(uin[:, u, :], U[bass.ds(c * P, P), :]).then_inc(ul[u], 16)
                    after(sp, x_done, c - R + 1)
                    load_x(nc, sp, s, x, xin[:, u], c, xl[u])

                def store(c, u):
                    sp.wait_ge(x_done, c + 1)
                    sp.dma_start(rows(X, c), x1[:, u]).then_inc(xs[u], 16)
                    sp.wait_ge(h_done, c + 1)
                    sp.dma_start(rows(H, c), h[:, u]).then_inc(hs[u], 16)
                each_phases(sp, n, [load, None, None, store], R)
                all_landed(sp, xs, n)
                all_landed(sp, hs, n)

            @block.scalar
            def _(act):
                def scaled(c, u):
                    landed(act, ul, c, u)
                    after(act, z_ps, c - R + 1)
                    nc.scalar.activation(z[:, u, :], uin[:, u, :], ACT.Identity, bias=offset2[:], scale=scale2[:]).then_inc(z_done, 1)

                def normed(c, u):
                    norm.act_root(act, c, u)
                    sent(act, hs, c, u)
                    norm.act_apply(act, h[:, u], x1[:, u], c, u).then_inc(h_done, 1)
                each_phases(act, n, [scaled, None, normed], R)

            @block.tensor
            def _(pe):
                def turn(c, u):
                    pe.wait_ge(z_done, c + 1)
                    after(pe, x_done, c - 1)
                    for j in range(J):
                        last = nc.tensor.transpose(psZ[u % 2][:, j * D:(j + 1) * D], z[:, u, j * P:(j + 1) * P], k.ident[:])
                    last.then_inc(z_ps, 1)
                each_phases(pe, n, [None, turn], R)

            @block.vector
            def _(dve):
                def add(c, u):
                    if isinstance(c, int) and c == n - 1:
                        dve.wait_ge(xl[u], 16 * (c // R + 2))
                    else:
                        landed(dve, xl, c, u)
                    dve.wait_ge(z_ps, c + 1)
                    sent(dve, xs, c, u)
                    after(dve, h_done, c - R + 1)
                    flat = x1[:, u].rearrange("p j d -> p (j d)")
                    nc.vector.tensor_tensor(flat, psZ[u % 2][:], xin[:, u].rearrange("p j d -> p (j d)"), ALU.add).then_inc(x_done, 1)
                    dve.wait_ge(x_done, c + 1)
                    norm.dve_moments(dve, x1[:, u], c, u)
                    norm.dve_coefs(dve, c, u, lambda: after(dve, h_done, c - R + 1))
                each_phases(dve, n, [None, add], R)


def gather_rows(pool, dst, table, idx, bound, sem):
    pool.indirect_dma_start(out=dst, out_offset=None, in_=table,
                            in_offset=bass.IndirectOffsetOnAxis(ap=idx, axis=0),
                            bounds_check=bound, oob_is_err=False).then_inc(sem, 16)


def scatter_rows(pool, table, src, idx, bound, sem):
    pool.indirect_dma_start(out=table, out_offset=bass.IndirectOffsetOnAxis(ap=idx, axis=0),
                            in_=src, in_offset=None, bounds_check=bound, oob_is_err=False).then_inc(sem, 16)


def zero_table(nc, s, S):
    parts = 14
    width = s.NP * D // P // parts
    with Stage(nc, "zero") as st:
        z = st.sb("z", [P, width])
        made, stored = st.sem("made"), st.sem("stored")
        flat = S.rearrange("(p r) d -> p (r d)", p=P)
        with st.run() as block:

            @block.vector
            def _(dve):
                nc.vector.memset(z[:], 0.0).then_inc(made, 1)

            @block.sync
            def _(sp):
                sp.wait_ge(made, 1)
                for i in range(parts):
                    sp.dma_start(flat[:, i * width:(i + 1) * width], z[:]).then_inc(stored, 16)
                sp.wait_ge(stored, 16 * parts)


def edge_messages(nc, k, s, plan, L1, H, edges, carry):
    with Stage(nc, "edge1") as st:
        got_rows = st.sb("rows", [P, 2, 2, J, D])
        idx = st.sb("idx", [P, 2, 2, J], U32)
        turned = st.sb("turned", [P, 2, 2, CH])
        m = st.sb("m", [P, 2, CH])
        ws, wd, b = st.sb("ws", [P, D]), st.sb("wd", [P, D]), st.sb("b", [P, 1])
        psS = [st.ps(f"psS{i}", [P, CH]) for i in range(2)]
        psD = [st.ps(f"psD{i}", [P, CH]) for i in range(2)]
        psM = [st.ps(f"psM{i}", [P, CH]) for i in range(2)]
        psR = [st.ps(f"psR{i}", [P, CH]) for i in range(2)]
        got = [st.sem(f"got{i}") for i in range(2)]
        weights, idx_ready, tick, T_ps, S_sb, D_sb, M_ps, M_sb, R_ps, chain, zeroed, carried, taken = (
            st.sem(v) for v in ("weights", "idx_ready", "tick", "T_ps", "S_sb", "D_sb", "M_ps", "M_sb", "R_ps",
                                "chain", "zeroed", "carried", "taken"))
        n = s.echunks
        with st.run() as block:

            @block.sync
            def _(sp):
                sp.dma_start(ws[:], L1["W_edge"][0:D, :]).then_inc(weights, 16)
                sp.dma_start(wd[:], L1["W_edge"][D:2 * D, :]).then_inc(weights, 16)
                sp.dma_start(b[:], column(L1["b_edge"])).then_inc(weights, 16)

            @block.gpsimd
            def _(pool):
                bound = pool.to_reg(s.N - 1)

                def gather(c, u):
                    pool.wait_ge(idx_ready, c + 1)
                    after(pool, T_ps, c - 1)
                    pool.sem_inc(tick, 1)
                    for side in range(2):
                        for q in range(J):
                            gather_rows(pool, got_rows[:, u, side, q, :], H, idx[:, u, side, q:q + 1], bound, got[u])
                each(pool, n, gather)

            @block.scalar
            def _(act):
                act.wait_ge(weights, 48)

                def index(c, u):
                    sent(act, got, c, u, 2 * J)
                    nc.scalar.copy(idx[:, u, 0, :], plan.other[:, bass.ds(c * J, J)])
                    nc.scalar.copy(idx[:, u, 1, :], plan.key[:, bass.ds(c * J, J)]).then_inc(idx_ready, 1)

                def take(c, u):
                    act.wait_ge(T_ps, c + 1)
                    after(act, M_ps, c - 1)
                    nc.scalar.copy(turned[:, u, 0, :], psS[u][:]).then_inc(S_sb, 1)

                def relu(c, u):
                    act.wait_ge(M_ps, c + 1)
                    after(act, R_ps, c - 1)
                    nc.scalar.activation(m[:, u, :], psM[u][:], ACT.Relu, bias=b[:]).then_inc(M_sb, 1)
                each_phases(act, n, [index, take, relu])

            @block.vector
            def _(dve):
                ch = Chain(dve, chain, J)
                nc.vector.memset(edges[:, 0:D], 0.0).then_inc(zeroed, 1)
                dve.wait_ge(zeroed, 1)

                def take(c, u):
                    dve.wait_ge(T_ps, c + 1)
                    after(dve, M_ps, c - 1)
                    nc.vector.tensor_copy(turned[:, u, 1, :], psD[u][:]).then_inc(D_sb, 1)

                def add(c, u):
                    dve.wait_ge(R_ps, c + 1)
                    ch.step(c)
                    for q in range(J):
                        ch.link(nc.vector.scalar_tensor_tensor(
                            edges[:, bass.ds((c * J + q + 1) * D, D)], edges[:, bass.ds((c * J + q) * D, D)],
                            plan.same[:, bass.ds(c * J + q, 1)], psR[u][:, q * D:(q + 1) * D], ALU.mult, ALU.add))
                each_phases(dve, n, [None, take, None, add])
                dve.wait_ge(carried, 1)
                nc.vector.tensor_copy(carry[:], psM[0][:, 0:D]).then_inc(taken, 1)
                dve.wait_ge(taken, 1)

            @block.tensor
            def _(pe):
                pe.wait_ge(weights, 48)

                def turn(c, u):
                    landed(pe, got, c, u, 2 * J)
                    after(pe, S_sb, c - 1)
                    after(pe, D_sb, c - 1)
                    for side, ps in ((0, psS), (1, psD)):
                        for q in range(J):
                            last = nc.tensor.transpose(ps[u][:, q * P:(q + 1) * P], got_rows[:, u, side, q, :], k.ident[:])
                    last.then_inc(T_ps, 1)

                def mix(c, u):
                    pe.wait_ge(S_sb, c + 1)
                    pe.wait_ge(D_sb, c + 1)
                    after(pe, M_sb, c - 1)
                    nc.tensor.matmul(psM[u][:], ws[:], turned[:, u, 0, :], start=True, stop=False)
                    nc.tensor.matmul(psM[u][:], wd[:], turned[:, u, 1, :], start=False, stop=True).then_inc(M_ps, 1)

                def back(c, u):
                    pe.wait_ge(M_sb, c + 1)
                    after(pe, chain, (c - 1) * J)
                    for q in range(J):
                        last = nc.tensor.transpose(psR[u][:, q * D:(q + 1) * D], m[:, u, q * P:(q + 1) * P], k.ident[:])
                    last.then_inc(R_ps, 1)
                each_phases(pe, n, [None, turn, mix, back])
                pe.wait_ge(chain, n * J)
                nc.tensor.matmul(psM[0][:, 0:D], plan.carry[:], edges[:, s.T * D:], start=True, stop=True).then_inc(carried, 1)


def scatter_sums(nc, s, plan, S, edges, carry, name):
    with Stage(nc, name) as st:
        y, idx = st.sb("y", [P, R, D]), st.sb("idx", [P, R], U32)
        put = [st.sem(f"put{i}") for i in range(R)]
        y_done, idx_ready, tick = st.sem("y_done"), st.sem("idx_ready"), st.sem("tick")
        n = s.T
        with st.run() as block:

            @block.vector
            def _(dve):
                def total(t, u):
                    sent(dve, put, t, u)
                    nc.vector.scalar_tensor_tensor(y[:, u, :], carry[:], plan.first[:, bass.ds(t, 1)],
                                                   edges[:, bass.ds((t + 1) * D, D)], ALU.mult, ALU.add).then_inc(y_done, 1)
                each(dve, n, total, R)

            @block.scalar
            def _(act):
                def index(t, u):
                    sent(act, put, t, u)
                    nc.scalar.copy(idx[:, u:u + 1], plan.last[:, bass.ds(t, 1)]).then_inc(idx_ready, 1)
                each(act, n, index, R)

            @block.gpsimd
            def _(pool):
                bound = pool.to_reg(s.N - 1)

                def scatter(t, u):
                    pool.wait_ge(idx_ready, t + 1)
                    pool.wait_ge(y_done, t + 1)
                    pool.sem_inc(tick, 1)
                    scatter_rows(pool, S, y[:, u, :], idx[:, u:u + 1], bound, put[u])
                each(pool, n, scatter, R)
                all_landed(pool, put, n)


def node_update(nc, k, s, L1, X, H, S):
    with Stage(nc, "node1") as st:
        norm = Norm(nc, st, k)
        xin, hin, sin, rst, x2, h2 = (st.sb(v, [P, R, J, D]) for v in ("xin", "hin", "sin", "rst", "x2", "h2"))
        rT, a_sb = st.sb("rT", [P, R, CH]), st.sb("a", [P, R, CH])
        w1, w2, b1 = st.sb("w1", [P, D]), st.sb("w2", [P, D]), st.sb("b1", [P, 1])
        bias, eps1 = st.sb("bias", [1, J, D]), st.sb("eps1", [P, 1])
        psT = [st.ps(f"psT{i}", [P, CH]) for i in range(2)]
        psA = [st.ps(f"psA{i}", [P, CH]) for i in range(2)]
        psB = [st.ps(f"psB{i}", [P, CH]) for i in range(2)]
        xl, hl, xs, hs = ([st.sem(f"{v}{i}") for i in range(R)] for v in ("xl", "hl", "xs", "hs"))
        weights, eps_done, r_done, T_ps, T_sb, A_ps, A_sb, B_ps, x_done, h_done = (
            st.sem(v) for v in ("weights", "eps_done", "r_done", "T_ps", "T_sb", "A_ps", "A_sb", "B_ps", "x_done", "h_done"))
        n = s.chunks
        with st.run() as block:

            @block.sync
            def _(sp):
                for j in range(J):
                    sp.dma_start(bias[:, j, :], row(L1["b2"])).then_inc(weights, 16)
                sp.dma_start(w1[:], L1["W1"][:, :]).then_inc(weights, 16)
                sp.dma_start(w2[:], L1["W2"][:, :]).then_inc(weights, 16)
                sp.dma_start(b1[:], column(L1["b1"])).then_inc(weights, 16)
                sp.dma_start(eps1[:], L1["eps"].rearrange("(a b) -> a b", a=1).broadcast_to([P, 1])).then_inc(weights, 16)

                def load(c, u):
                    after(sp, r_done, c - R + 1)
                    sp.dma_start(hin[:, u], rows(H, c)).then_inc(hl[u], 16)
                    sp.dma_start(sin[:, u], rows(S, c)).then_inc(hl[u], 16)

                def load2(c, u):
                    after(sp, x_done, c - R + 1)
                    sp.dma_start(xin[:, u], rows(X, c)).then_inc(xl[u], 16)

                def store(c, u):
                    sp.wait_ge(x_done, c + 1)
                    sp.dma_start(rows(X, c), x2[:, u]).then_inc(xs[u], 16)
                    sp.wait_ge(h_done, c + 1)
                    sp.dma_start(rows(H, c), h2[:, u]).then_inc(hs[u], 16)
                each_phases(sp, n, [load, load2, None, None, store], R)
                all_landed(sp, xs, n)
                all_landed(sp, hs, n)

            @block.vector
            def _(dve):
                dve.wait_ge(weights, 16 * (J + 4))
                nc.vector.tensor_scalar(eps1[:], eps1[:], 1.0, None, ALU.add).then_inc(eps_done, 1)
                dve.wait_ge(eps_done, 1)

                def rest(c, u):
                    landed(dve, hl, c, u, 2)
                    after(dve, T_ps, c - R + 1)
                    nc.vector.scalar_tensor_tensor(rst[:, u], hin[:, u], eps1[:], sin[:, u], ALU.mult, ALU.add).then_inc(r_done, 1)

                def finish(c, u):
                    dve.wait_ge(B_ps, c + 1)
                    landed(dve, xl, c, u)
                    sent(dve, xs, c, u)
                    after(dve, h_done, c - R + 1)
                    nc.vector.tensor_tensor(x2[:, u].rearrange("p j d -> p (j d)"), psB[u % 2][:],
                                            xin[:, u].rearrange("p j d -> p (j d)"), ALU.add).then_inc(x_done, 1)
                    dve.wait_ge(x_done, c + 1)
                    norm.dve_moments(dve, x2[:, u], c, u)
                    norm.dve_coefs(dve, c, u, lambda: after(dve, h_done, c - R + 1))
                each_phases(dve, n, [rest, None, finish], R)

            @block.scalar
            def _(act):
                act.wait_ge(weights, 16 * (J + 4))

                def take(c, u):
                    act.wait_ge(T_ps, c + 1)
                    after(act, A_ps, c - R + 1)
                    nc.scalar.copy(rT[:, u, :], psT[u % 2][:]).then_inc(T_sb, 1)

                def relu(c, u):
                    act.wait_ge(A_ps, c + 1)
                    after(act, B_ps, c - R + 1)
                    nc.scalar.activation(a_sb[:, u, :], psA[u % 2][:], ACT.Relu, bias=b1[:]).then_inc(A_sb, 1)

                def normed(c, u):
                    norm.act_root(act, c, u)
                    sent(act, hs, c, u)
                    norm.act_apply(act, h2[:, u], x2[:, u], c, u).then_inc(h_done, 1)
                each_phases(act, n, [take, relu, normed], R)

            @block.tensor
            def _(pe):
                pe.wait_ge(weights, 16 * (J + 4))

                def turn(c, u):
                    pe.wait_ge(r_done, c + 1)
                    after(pe, T_sb, c - 1)
                    for j in range(J):
                        last = nc.tensor.transpose(psT[u % 2][:, j * P:(j + 1) * P], rst[:, u, j, :], k.ident[:])
                    last.then_inc(T_ps, 1)

                def up(c, u):
                    pe.wait_ge(T_sb, c + 1)
                    after(pe, A_sb, c - 1)
                    nc.tensor.matmul(psA[u % 2][:], w1[:], rT[:, u, :], start=True, stop=True).then_inc(A_ps, 1)

                def down(c, u):
                    pe.wait_ge(A_sb, c + 1)
                    after(pe, x_done, c - 1)
                    rows_product(nc, psB[u % 2], a_sb[:, u], w2, bias[:].rearrange("a j d -> a (j d)"), k).then_inc(B_ps, 1)
                each_phases(pe, n, [turn, up, down], R)


def hyperbolic_messages(nc, k, s, plan, H, edges, norms):
    with Stage(nc, "mobius") as st:
        got_rows = st.sb("rows", [P, R, 2, J, D])
        idx = st.sb("idx", [P, R, 2, J], U32)
        sq, dot = st.sb("sq", [P, R, 2, J]), st.sb("dot", [P, R, J])
        c1, al, den, be = (st.sb(v, [P, R, J]) for v in ("c1", "al", "den", "be"))
        scaled = st.sb("scaled", [P, R, J, D])
        junk, junk2, junk3 = st.sb("junk", [P, J, D]), st.sb("junk2", [P, 2, J, D]), st.sb("junk3", [P, J, D])
        got = [st.sem(f"got{i}") for i in range(R)]
        idx_ready, tick, sq_done, dot_done, chain, coef, tmp_done, m_done, norm_done = (
            st.sem(v) for v in ("idx_ready", "tick", "sq_done", "dot_done", "chain", "coef", "tmp_done", "m_done", "norm_done"))
        n = s.echunks
        with st.run() as block:

            @block.gpsimd
            def _(pool):
                bound = pool.to_reg(s.N - 1)

                def gather(c, u):
                    pool.wait_ge(idx_ready, c + 1)
                    after(pool, m_done, c - R + 1)
                    pool.sem_inc(tick, 1)
                    for side in range(2):
                        for q in range(J):
                            gather_rows(pool, got_rows[:, u, side, q, :], H, idx[:, u, side, q:q + 1], bound, got[u])
                each(pool, n, gather, R)

            @block.scalar
            def _(act):
                def index(c, u):
                    sent(act, got, c, u, 2 * J)
                    nc.scalar.copy(idx[:, u, 0, :], plan.other[:, bass.ds(c * J, J)])
                    nc.scalar.copy(idx[:, u, 1, :], plan.key[:, bass.ds(c * J, J)]).then_inc(idx_ready, 1)

                def squares(c, u):
                    landed(act, got, c, u, 2 * J)
                    after(act, coef, c - R + 1)
                    after(act, sq_done, c)
                    for side in range(2):
                        for q in range(J):
                            last = nc.scalar.activation(junk2[:, side, q, :], got_rows[:, u, side, q, :], ACT.Square,
                                                        accum_out=sq[:, u, side, q:q + 1])
                    last.then_inc(sq_done, 1)

                def scale(c, u):
                    act.wait_ge(coef, c + 1)
                    after(act, m_done, c - R + 1)
                    for q in range(J):
                        last = nc.scalar.mul(scaled[:, u, q, :], got_rows[:, u, 1, q, :], be[:, u, q:q + 1])
                    last.then_inc(tmp_done, 1)

                def norm(c, u):
                    act.wait_ge(m_done, c + 1)
                    after(act, norm_done, c)
                    for q in range(J):
                        last = nc.scalar.activation(junk3[:, q, :], edges[:, bass.ds((c * J + q + 1) * D, D)], ACT.Square,
                                                    accum_out=norms[:, bass.ds(c * J + q, 1)])
                    last.then_inc(norm_done, 1)

                def late(c, u):
                    scale(c, u)
                    norm(c, u)
                each_phases(act, n, [index, None, None, squares, late], R)

            @block.vector
            def _(dve):
                ch = Chain(dve, chain, 6)

                def coefs(c, u):
                    landed(dve, got, c, u, 2 * J)
                    after(dve, dot_done, c)
                    for q in range(J):
                        last = nc.vector.scalar_tensor_tensor(junk[:, q, :], got_rows[:, u, 0, q, :], 1.0, got_rows[:, u, 1, q, :],
                                                              ALU.mult, ALU.mult, accum_out=dot[:, u, q:q + 1])
                    last.then_inc(dot_done, 1)
                    dve.wait_ge(dot_done, c + 1)
                    dve.wait_ge(sq_done, c + 1)
                    after(dve, tmp_done, c - R + 1)
                    after(dve, m_done, c - R + 1)
                    x2, y2 = sq[:, u, 0, :], sq[:, u, 1, :]
                    ch.step(c)
                    nc.vector.tensor_scalar(c1[:, u], dot[:, u], -2.0, 1.0, ALU.mult, ALU.add)
                    ch.link(nc.vector.tensor_tensor(den[:, u], x2, y2, ALU.mult))
                    nc.vector.tensor_tensor(al[:, u], c1[:, u], y2, ALU.add)
                    ch.link(nc.vector.tensor_tensor(den[:, u], den[:, u], c1[:, u], ALU.add))
                    ch.link(nc.vector.tensor_scalar(den[:, u], den[:, u], HYP_EPS, None, ALU.max))
                    ch.link(nc.vector.reciprocal(den[:, u], den[:, u]))
                    ch.link(nc.vector.tensor_tensor(al[:, u], al[:, u], den[:, u], ALU.mult))
                    nc.vector.scalar_tensor_tensor(be[:, u], x2, -1.0, den[:, u], ALU.add, ALU.mult).then_inc(coef, 1)
                    ch.link(nc.vector.tensor_copy(c1[:, u], c1[:, u]))

                def finish(c, u):
                    dve.wait_ge(tmp_done, c + 1)
                    for q in range(J):
                        last = nc.vector.scalar_tensor_tensor(edges[:, bass.ds((c * J + q + 1) * D, D)], got_rows[:, u, 0, q, :],
                                                              al[:, u, q:q + 1], scaled[:, u, q, :], ALU.mult, ALU.add)
                    last.then_inc(m_done, 1)
                each_phases(dve, n, [coefs, finish], R)


class FoldScratch:
    def __init__(self, st):
        self.junk, self.scaled = st.sb("junk", [P, D]), st.sb("scaled", [P, D])
        self.dot, self.a1, self.x2, self.al, self.be = (st.sb(v, [P, 1]) for v in ("dot", "a1", "x2", "al", "be"))
        self.den, self.cut, self.inv, self.al2, self.be2 = (st.sb(v, [P, 1]) for v in ("den", "cut", "inv", "al2", "be2"))


def fold_step(nc, b, plan, norms, t, state, m, out, q, link, q_ready, r_ready):
    link(nc.vector.scalar_tensor_tensor(b.junk[:], m, plan.same[:, bass.ds(t, 1)], state, ALU.mult, ALU.mult,
                                        accum_out=b.dot[:]))
    q_ready()
    nc.vector.tensor_scalar(b.a1[:], b.dot[:], 2.0, 1.0, ALU.mult, ALU.add)
    link(nc.vector.tensor_scalar(b.x2[:], q, plan.same[:, bass.ds(t, 1)], None, ALU.mult))
    nc.vector.tensor_scalar(b.al[:], b.a1[:], norms[:, bass.ds(t, 1)], plan.same[:, bass.ds(t, 1)], ALU.add, ALU.mult)
    nc.vector.tensor_scalar(b.be[:], b.x2[:], -1.0, 1.0, ALU.mult, ALU.add)
    link(nc.vector.tensor_scalar(b.den[:], b.x2[:], norms[:, bass.ds(t, 1)], b.a1[:], ALU.mult, ALU.add))
    link(nc.vector.tensor_scalar(b.cut[:], b.den[:], HYP_EPS, None, ALU.max))
    link(nc.vector.reciprocal(b.inv[:], b.cut[:]))
    nc.vector.tensor_tensor(b.al2[:], b.al[:], b.inv[:], ALU.mult)
    link(nc.vector.tensor_tensor(b.be2[:], b.be[:], b.inv[:], ALU.mult))
    link(nc.vector.tensor_scalar(b.scaled[:], m, b.be2[:], None, ALU.mult))
    r_ready()
    return nc.vector.scalar_tensor_tensor(out, state, b.al2[:], b.scaled[:], ALU.mult, ALU.add)


FOLD_LINKS = 7


def hyperbolic_fold(nc, k, s, plan, edges, norms, lengths):
    with Stage(nc, "fold") as st:
        state = st.sb("state", [P, 2, D])
        final = st.sb("final", [P, D])
        flag = st.sb("flag", [P, 1], I32)
        q = st.sb("q", [P, 2])
        qjunk = st.sb("qjunk", [P, D])
        b = FoldScratch(st)
        psC, psF = st.ps("psC", [P, D]), st.ps("psF", [P, 1])
        tick = st.sem("tick")
        (zeroed, flagged, flag_done, s1_chain, s1_state, s1_q, slow_chain, slow_state, slow_moved, state_done, moved,
         start_done, s2_chain, s2_state, s2_q) = (
            st.sem(v) for v in ("zeroed", "flagged", "flag_done", "s1_chain", "s1_state", "s1_q", "slow_chain", "slow_state",
                                "slow_moved", "state_done", "moved", "start_done", "s2_chain", "s2_state", "s2_q"))
        n = s.T
        rounds = P - 2
        per = FOLD_LINKS
        with st.run() as block:

            @block.vector
            def _(dve):
                dve.wait_ge(flagged, 1)
                nc.vector.tensor_copy(flag[:], psF[:]).then_inc(flag_done, 1)
                nc.vector.memset(state[:], 0.0).then_inc(zeroed, 1)
                dve.wait_ge(zeroed, 1)
                dve.wait_ge(flag_done, 1)
                ch = Chain(dve, s1_chain, per)

                def first_sweep(t, u):
                    ch.step(t)
                    last = fold_step(nc, b, plan, norms, t, state[:, u, :], edges[:, bass.ds((t + 1) * D, D)], state[:, 1 - u, :],
                                     q[:, u:u + 1], ch.link, lambda: dve.wait_ge(s1_q, t + 1), lambda: None)
                    last.then_inc(s1_state, 1)
                    dve.wait_ge(s1_state, t + 1)
                each(dve, n, first_sweep)

                crossing = dve.value_load(flag[0:1, 0:1], min_val=0, max_val=P)
                with dve.If(crossing > 0):
                    dve.sem_inc(slow_state, 1)
                    with dve.Fori(0, rounds) as r:
                        dve.wait_ge(slow_moved, r + 1)
                        nc.vector.tensor_scalar(state[:, 0, :], psC[:], plan.cont[:], None, ALU.mult).then_inc(slow_chain, 1)
                        dve.wait_ge(slow_chain, r * ((per + 2) * n + 1) + 1)
                        dve.sem_inc(tick, 1)
                        with dve.Fori(0, n // 2) as i:
                            for u in range(2):
                                count = [0]

                                def link(ins, u=u):
                                    ins.then_inc(slow_chain, 1)
                                    count[0] += 1
                                    dve.wait_ge(slow_chain, r * ((per + 2) * n + 1) + 1 + (i * 2 + u) * (per + 2) + count[0])
                                link(nc.vector.scalar_tensor_tensor(b.junk[:], state[:, u, :], 1.0, state[:, u, :], ALU.mult, ALU.mult,
                                                                    accum_out=q[:, u:u + 1]))
                                link(fold_step(nc, b, plan, norms, i * 2 + u, state[:, u, :],
                                               edges[:, bass.ds((i * 2 + u + 1) * D, D)], state[:, 1 - u, :],
                                               q[:, u:u + 1], link, lambda: None, lambda: None))
                                assert count[0] == per + 2
                        nc.vector.tensor_copy(final[:], state[:, 0, :]).then_inc(slow_state, 1)
                        dve.wait_ge(slow_state, r + 2)
                nc.vector.tensor_copy(final[:], state[:, 0, :]).then_inc(state_done, 1)

                dve.wait_ge(moved, 1)
                nc.vector.tensor_scalar(edges[:, 0:D], psC[:], plan.cont[:], None, ALU.mult).then_inc(start_done, 1)
                dve.wait_ge(start_done, 1)
                ch2 = Chain(dve, s2_chain, per)

                def last_sweep(t, u):
                    ch2.step(t)
                    here = edges[:, bass.ds((t + 1) * D, D)]
                    last = fold_step(nc, b, plan, norms, t, edges[:, bass.ds(t * D, D)], here, here,
                                     q[:, u:u + 1], ch2.link, lambda: dve.wait_ge(s2_q, t + 1), lambda: None)
                    last.then_inc(s2_state, 1)
                    dve.wait_ge(s2_state, t + 1)
                each(dve, n, last_sweep)

            @block.scalar
            def _(act):
                def first_sweep(t, u):
                    if isinstance(t, int) and t == 0:
                        act.wait_ge(zeroed, 1)
                    else:
                        act.wait_ge(s1_state, t)
                    after(act, s1_q, t)
                    nc.scalar.activation(qjunk[:], state[:, u, :], ACT.Square, accum_out=q[:, u:u + 1]).then_inc(s1_q, 1)
                each(act, n, first_sweep)
                act.wait_ge(start_done, 1)

                def last_sweep(t, u):
                    if not (isinstance(t, int) and t == 0):
                        act.wait_ge(s2_state, t)
                        act.wait_ge(s2_q, t)
                    nc.scalar.activation(qjunk[:], edges[:, bass.ds(t * D, D)], ACT.Square, accum_out=q[:, u:u + 1]).then_inc(s2_q, 1)
                each(act, n, last_sweep)

            @block.tensor
            def _(pe):
                nc.tensor.matmul(psF[:], k.ones[:], plan.through[:], start=True, stop=True).then_inc(flagged, 1)
                pe.wait_ge(flag_done, 1)
                crossing = pe.value_load(flag[0:1, 0:1], min_val=0, max_val=P)
                pe.wait_ge(s1_state, n)
                with pe.If(crossing > 0):
                    with pe.Fori(0, rounds) as r:
                        pe.wait_ge(slow_state, r + 1)
                        nc.tensor.matmul(psC[:], k.shift[:], state[:, 0, :], start=True, stop=True).then_inc(slow_moved, 1)
                pe.wait_ge(state_done, 1)
                nc.tensor.matmul(psC[:], k.shift[:], final[:], start=True, stop=True).then_inc(moved, 1)


def hyperbolic_results(nc, k, s, plan, H, edges, lengths):
    T = s.T
    with Stage(nc, "aggregate") as st:
        rows_in = st.sb("rows", [P, R, J, D])
        res = st.sb("res", [P, R, J, D])
        scaled = st.sb("scaled", [P, R, J, D])
        junk, junk2, junk3 = st.sb("junk", [P, 4, D]), st.sb("junk2", [P, J, D]), st.sb("junk3", [P, J, D])
        idx = st.sb("idx", [P, R, J], U32)
        nrm, cut, low, lg, th, factor, alive, y2 = (
            st.sb(v, [P, T]) for v in ("nrm", "cut", "low", "lg", "th", "factor", "alive", "y2"))
        x2, dot = st.sb("x2", [P, R, J]), st.sb("dot", [P, R, J])
        c1, al, den, be, xy = (st.sb(v, [P, R, J]) for v in ("c1", "al", "den", "be", "xy"))
        got = [st.sem(f"got{i}") for i in range(R)]
        put = [st.sem(f"put{i}") for i in range(R)]
        len_done, root, ratio, logged, argd, thd, prep, batch, cleared = (
            st.sem(v) for v in ("len_done", "root", "ratio", "logged", "argd", "thd", "prep", "batch", "cleared"))
        idx_ready, tick, sq_done, dot_done, chain, coef, tmp_done, res_done = (
            st.sem(v) for v in ("idx_ready", "tick", "sq_done", "dot_done", "chain", "coef", "tmp_done", "res_done"))
        n = s.echunks
        with st.run() as block:

            @block.gpsimd
            def _(pool):
                bound = pool.to_reg(s.N - 1)
                pool.wait_ge(cleared, 1)

                def gather(c, u):
                    pool.wait_ge(idx_ready, c + 1)
                    after(pool, res_done, c - R + 1)
                    pool.sem_inc(tick, 1)
                    for q in range(J):
                        gather_rows(pool, rows_in[:, u, q, :], H, idx[:, u, q:q + 1], bound, got[u])

                def scatter(c, u):
                    pool.wait_ge(res_done, c + 1)
                    pool.sem_inc(tick, 1)
                    for q in range(J):
                        scatter_rows(pool, H, res[:, u, q, :], idx[:, u, q:q + 1], bound, put[u])
                each_phases(pool, n, [gather, None, scatter], R)
                all_landed(pool, put, n, J)

            @block.scalar
            def _(act):
                def length(c, u):
                    after(act, len_done, c)
                    for q in range(J):
                        last = nc.scalar.activation(junk[:, q, :], edges[:, bass.ds((c * J + q + 1) * D, D)], ACT.Square,
                                                    accum_out=lengths[:, bass.ds(c * J + q, 1)])
                    last.then_inc(len_done, 1)
                each(act, n, length)
                act.wait_ge(prep, 1)
                nc.scalar.activation(nrm[:], cut[:], ACT.Sqrt).then_inc(root, 1)
                act.wait_ge(ratio, 1)
                nc.scalar.activation(lg[:], low[:], ACT.Ln).then_inc(logged, 1)
                act.wait_ge(argd, 1)
                nc.scalar.activation(th[:], lg[:], ACT.Tanh).then_inc(thd, 1)

                def index(c, u):
                    sent(act, put, c, u, J)
                    nc.scalar.copy(idx[:, u, :], plan.last[:, bass.ds(c * J, J)]).then_inc(idx_ready, 1)

                def squares(c, u):
                    landed(act, got, c, u, J)
                    after(act, coef, c - R + 1)
                    after(act, sq_done, c)
                    for q in range(J):
                        last = nc.scalar.activation(junk2[:, q, :], rows_in[:, u, q, :], ACT.Square, accum_out=x2[:, u, q:q + 1])
                    last.then_inc(sq_done, 1)

                def scale(c, u):
                    act.wait_ge(coef, c + 1)
                    after(act, res_done, c - R + 1)
                    for q in range(J):
                        last = nc.scalar.mul(scaled[:, u, q, :], rows_in[:, u, q, :], al[:, u, q:q + 1])
                    last.then_inc(tmp_done, 1)
                each_phases(act, n, [index, None, squares, scale], R)

            @block.vector
            def _(dve):
                ch = Chain(dve, batch, 99)
                nc.vector.memset(rows_in[:], 0.0).then_inc(cleared, 1)
                dve.wait_ge(len_done, n)
                nc.vector.tensor_scalar(cut[:], lengths[:], 1e-30, None, ALU.max).then_inc(prep, 1)
                dve.wait_ge(root, 1)
                ch.link(nc.vector.tensor_scalar(alive[:], nrm[:], HYP_EPS, None, ALU.is_gt))
                ch.link(nc.vector.tensor_scalar(cut[:], nrm[:], HYP_EPS, 1.0 - HYP_EPS, ALU.max, ALU.min))
                ch.link(nc.vector.tensor_scalar(low[:], cut[:], -1.0, 1.0, ALU.mult, ALU.add))
                ch.link(nc.vector.reciprocal(low[:], low[:]))
                ch.link(nc.vector.tensor_scalar(nrm[:], cut[:], 1.0, None, ALU.add))
                nc.vector.tensor_tensor(low[:], low[:], nrm[:], ALU.mult).then_inc(ratio, 1)
                dve.wait_ge(logged, 1)
                nc.vector.scalar_tensor_tensor(lg[:], lg[:], 0.5, plan.inv[:], ALU.mult, ALU.mult).then_inc(argd, 1)
                ch.link(nc.vector.reciprocal(factor[:], cut[:]))
                ch.link(nc.vector.tensor_tensor(factor[:], factor[:], alive[:], ALU.mult))
                dve.wait_ge(thd, 1)
                ch.link(nc.vector.tensor_tensor(factor[:], factor[:], th[:], ALU.mult))
                ch.link(nc.vector.tensor_tensor(y2[:], factor[:], factor[:], ALU.mult))
                ch.link(nc.vector.tensor_tensor(y2[:], y2[:], lengths[:], ALU.mult))
                ch2 = Chain(dve, chain, 10)

                def coefs(c, u):
                    landed(dve, got, c, u, J)
                    after(dve, dot_done, c)
                    for q in range(J):
                        last = nc.vector.scalar_tensor_tensor(junk3[:, q, :], rows_in[:, u, q, :], 1.0, edges[:, bass.ds((c * J + q + 1) * D, D)],
                                                              ALU.mult, ALU.mult, accum_out=dot[:, u, q:q + 1])
                    last.then_inc(dot_done, 1)
                    dve.wait_ge(dot_done, c + 1)
                    dve.wait_ge(sq_done, c + 1)
                    f, y = factor[:, bass.ds(c * J, J)], y2[:, bass.ds(c * J, J)]
                    ch2.step(c)
                    ch2.link(nc.vector.tensor_tensor(xy[:, u], dot[:, u], f, ALU.mult))
                    ch2.link(nc.vector.tensor_scalar(c1[:, u], xy[:, u], 2.0, 1.0, ALU.mult, ALU.add))
                    ch2.link(nc.vector.tensor_tensor(den[:, u], x2[:, u], y, ALU.mult))
                    ch2.link(nc.vector.tensor_tensor(den[:, u], den[:, u], c1[:, u], ALU.add))
                    ch2.link(nc.vector.tensor_scalar(den[:, u], den[:, u], HYP_EPS, None, ALU.max))
                    ch2.link(nc.vector.reciprocal(den[:, u], den[:, u]))
                    ch2.link(nc.vector.tensor_scalar(be[:, u], x2[:, u], -1.0, 1.0, ALU.mult, ALU.add))
                    ch2.link(nc.vector.tensor_tensor(be[:, u], be[:, u], f, ALU.mult))
                    ch2.link(nc.vector.tensor_tensor(c1[:, u], c1[:, u], y, ALU.add))
                    after(dve, tmp_done, c - R + 1)
                    ch2.link(nc.vector.tensor_tensor(be[:, u], be[:, u], den[:, u], ALU.mult))
                    nc.vector.tensor_tensor(al[:, u], c1[:, u], den[:, u], ALU.mult).then_inc(coef, 1)

                def finish(c, u):
                    dve.wait_ge(tmp_done, c + 1)
                    sent(dve, put, c, u, J)
                    for q in range(J):
                        last = nc.vector.scalar_tensor_tensor(res[:, u, q, :], edges[:, bass.ds((c * J + q + 1) * D, D)], be[:, u, q:q + 1],
                                                              scaled[:, u, q, :], ALU.mult, ALU.add)
                    last.then_inc(res_done, 1)
                each_phases(dve, n, [coefs, finish], R)


def third_norm(nc, k, s, X, H):
    with Stage(nc, "norm3") as st:
        norm = Norm(nc, st, k)
        xin, hin, x3, h3 = (st.sb(v, [P, R, J, D]) for v in ("xin", "hin", "x3", "h3"))
        ld, xs, hs = ([st.sem(f"{v}{i}") for i in range(R)] for v in ("ld", "xs", "hs"))
        x_done, h_done = st.sem("x_done"), st.sem("h_done")
        n = s.chunks
        with st.run() as block:

            @block.sync
            def _(sp):
                def load(c, u):
                    after(sp, x_done, c - R + 1)
                    sp.dma_start(xin[:, u], rows(X, c)).then_inc(ld[u], 16)
                    sp.dma_start(hin[:, u], rows(H, c)).then_inc(ld[u], 16)

                def store(c, u):
                    sp.wait_ge(x_done, c + 1)
                    sp.dma_start(rows(X, c), x3[:, u]).then_inc(xs[u], 16)
                    sp.wait_ge(h_done, c + 1)
                    sp.dma_start(rows(H, c), h3[:, u]).then_inc(hs[u], 16)
                each_phases(sp, n, [load, None, store], R)
                all_landed(sp, xs, n)
                all_landed(sp, hs, n)

            @block.vector
            def _(dve):
                def add(c, u):
                    landed(dve, ld, c, u, 2)
                    sent(dve, xs, c, u)
                    after(dve, h_done, c - R + 1)
                    nc.vector.tensor_tensor(x3[:, u], xin[:, u], hin[:, u], ALU.add).then_inc(x_done, 1)
                    dve.wait_ge(x_done, c + 1)
                    norm.dve_moments(dve, x3[:, u], c, u)
                    norm.dve_coefs(dve, c, u, lambda: after(dve, h_done, c - R + 1))
                each(dve, n, add, R)

            @block.scalar
            def _(act):
                def normed(c, u):
                    norm.act_root(act, c, u)
                    sent(act, hs, c, u)
                    norm.act_apply(act, h3[:, u], x3[:, u], c, u).then_inc(h_done, 1)
                each(act, n, normed, R)


class Ssp:

    def __init__(self, nc, st, k, b, ring):
        self.nc, self.b, self.k, self.ring = nc, b, k, ring
        self.v, self.mag, self.dec, self.log = (st.sb(x, [P, ring, CH]) for x in ("ssp_v", "ssp_mag", "ssp_dec", "ssp_log"))
        self.taken, self.a, self.e, self.logged, self.used = (
            st.sem(x) for x in ("ssp_taken", "ssp_a", "ssp_e", "ssp_logged", "ssp_used"))

    def dve_take(self, dve, psum, c, u):
        after(dve, self.used, c - self.ring + 1)
        after(dve, self.a, c - self.ring + 1)
        self.nc.vector.tensor_scalar(self.v[:, u], psum, self.b[:], None, ALU.add).then_inc(self.taken, 1)

    def act_log(self, act, c, u):
        nc = self.nc
        act.wait_ge(self.taken, c + 1)
        nc.scalar.activation(self.mag[:, u], self.v[:, u], ACT.Abs).then_inc(self.a, 1)
        act.wait_ge(self.a, c + 1)
        nc.scalar.activation(self.dec[:, u], self.mag[:, u], ACT.Exp, scale=-1.0).then_inc(self.e, 1)
        act.wait_ge(self.e, c + 1)
        after(act, self.used, c - self.ring + 1)
        nc.scalar.activation(self.log[:, u], self.dec[:, u], ACT.Ln, bias=self.k.half_col[:], scale=0.5).then_inc(self.logged, 1)

    def dve_result(self, dve, out, c, u):
        dve.wait_ge(self.logged, c + 1)
        self.nc.vector.scalar_tensor_tensor(out, self.v[:, u], 0.0, self.log[:, u], ALU.max, ALU.add).then_inc(self.used, 1)


def filter_messages(nc, k, s, plan, L3, attr, H, edges, carry):
    T = s.T
    with Stage(nc, "edge3") as st:
        rows_in = st.sb("rows", [P, 2, J, D])
        attr_in = st.sb("attr", [P, 2, J, D])
        idx = st.sb("idx", [P, 2, 2, J], U32)
        aT, hT, hl, msg = (st.sb(v, [P, 2, CH]) for v in ("aT", "hT", "hl", "msg"))
        sp_out = st.sb("sp_out", [P, 2, CH])
        cut_rows = st.sb("cut_rows", [P, 2, J, D])
        phase, whole, cosine = st.sb("phase", [P, T]), st.sb("whole", [P, T]), st.sb("cosine", [P, T])
        w1, w2, lin1 = st.sb("w1", [P, D]), st.sb("w2", [P, D]), st.sb("lin1", [P, D])
        b1, b2 = st.sb("b1", [P, 1]), st.sb("b2", [P, 1])
        ssp = Ssp(nc, st, k, b1, 2)
        psA = st.ps("psA", [P, CH])
        psH = st.ps("psH", [P, CH])
        psV = [st.ps(f"psV{i}", [P, CH]) for i in range(2)]
        psL = st.ps("psL", [P, CH])
        psW = st.ps("psW", [P, CH])
        psR = [st.ps(f"psR{i}", [P, CH]) for i in range(2)]
        got = [st.sem(f"got{i}") for i in range(2)]
        weights, padded, idx_ready, tick, A_ps, A_sb, H_sb, V_ps, L_ps, L_sb, W_ps, msg_done, R_ps, R_sb = (
            st.sem(v) for v in ("weights", "padded", "idx_ready", "tick", "A_ps", "A_sb", "H_sb", "V_ps", "L_ps", "L_sb",
                                "W_ps", "msg_done", "R_ps", "R_sb"))
        chain, zeroed, carried, taken, turns, cos_done, sin_done = (
            st.sem(v) for v in ("chain", "zeroed", "carried", "taken", "turns", "cos_done", "sin_done"))
        n = s.echunks
        big = 1.5 * 2.0 ** 23
        with st.run() as block:

            @block.sync
            def _(sp):
                sp.wait_ge(padded, 2)
                for dst, src in ((w1[0:NG, :], L3["mlp_w1"][:, :]), (w2[:], L3["mlp_w2"][:, :]), (lin1[:], L3["lin1_w"][:, :]),
                                 (b1[:], column(L3["mlp_b1"])), (b2[:], column(L3["mlp_b2"]))):
                    sp.dma_start(dst, src).then_inc(weights, 16)

            @block.gpsimd
            def _(pool):
                bound = pool.to_reg(s.N - 1)
                ebound = pool.to_reg(s.E - 1)
                pool.memset(w1[:], 0.0).then_inc(padded, 1)
                pool.memset(attr_in[:], 0.0).then_inc(padded, 1)
                pool.wait_ge(padded, 2)

                def gather(c, u):
                    pool.wait_ge(idx_ready, c + 1)
                    after(pool, A_ps, c - 1)
                    pool.sem_inc(tick, 1)
                    for q in range(J):
                        gather_rows(pool, rows_in[:, u, q, :], H, idx[:, u, 0, q:q + 1], bound, got[u])
                        gather_rows(pool, attr_in[:, u, q, 0:NG], attr, idx[:, u, 1, q:q + 1], ebound, got[u])
                each(pool, n, gather)

            @block.scalar
            def _(act):
                act.wait_ge(weights, 80)
                act.wait_ge(turns, 1)
                nc.scalar.activation(cosine[:], phase[:], ACT.Sin, scale=2.0 * math.pi).then_inc(sin_done, 1)

                def index(c, u):
                    sent(act, got, c, u, 2 * J)
                    nc.scalar.copy(idx[:, u, 0, :], plan.other[:, bass.ds(c * J, J)])
                    nc.scalar.copy(idx[:, u, 1, :], plan.edge[:, bass.ds(c * J, J)]).then_inc(idx_ready, 1)

                def take(c, u):
                    act.wait_ge(A_ps, c + 1)
                    after(act, V_ps, c - 1)
                    nc.scalar.copy(aT[:, u, :], psA[:]).then_inc(A_sb, 1)
                    act.wait_ge(L_ps, c + 1)
                    after(act, msg_done, c - 1)
                    nc.scalar.copy(hl[:, u, :], psL[:]).then_inc(L_sb, 1)

                def soft(c, u):
                    ssp.act_log(act, c, u)

                def cutoff(c, u):
                    act.wait_ge(R_ps, c + 1)
                    act.wait_ge(cos_done, 1)
                    after(act, chain, (c - 1) * J)
                    for q in range(J):
                        last = nc.scalar.mul(cut_rows[:, u, q, :], psR[u][:, q * D:(q + 1) * D], cosine[:, bass.ds(c * J + q, 1)])
                    last.then_inc(R_sb, 1)
                each_phases(act, n, [index, take, soft, cutoff])

            @block.vector
            def _(dve):
                ch = Chain(dve, chain, J)
                nc.vector.memset(edges[:, 0:D], 0.0).then_inc(zeroed, 1)
                dve.wait_ge(zeroed, 1)
                nc.vector.tensor_scalar(phase[:], plan.weight[:], 0.5 / CUTOFF, 0.25, ALU.mult, ALU.add).then_inc(zeroed, 1)
                dve.wait_ge(zeroed, 2)
                nc.vector.tensor_scalar(whole[:], phase[:], big, None, ALU.add).then_inc(zeroed, 1)
                dve.wait_ge(zeroed, 3)
                nc.vector.tensor_scalar(whole[:], whole[:], -big, None, ALU.add).then_inc(zeroed, 1)
                dve.wait_ge(zeroed, 4)
                nc.vector.tensor_tensor(phase[:], phase[:], whole[:], ALU.subtract).then_inc(zeroed, 1)
                dve.wait_ge(zeroed, 5)
                nc.vector.tensor_scalar(phase[:], phase[:], 0.4999999, -0.4999999, ALU.min, ALU.max).then_inc(turns, 1)
                dve.wait_ge(sin_done, 1)
                nc.vector.tensor_scalar(cosine[:], cosine[:], 0.5, 0.5, ALU.mult, ALU.add).then_inc(cos_done, 1)
                dve.wait_ge(weights, 80)

                def take(c, u):
                    dve.wait_ge(A_ps, c + 1)
                    after(dve, L_ps, c - 1)
                    nc.vector.tensor_copy(hT[:, u, :], psH[:]).then_inc(H_sb, 1)

                def soft(c, u):
                    dve.wait_ge(V_ps, c + 1)
                    ssp.dve_take(dve, psV[u][:], c, u)
                    after(dve, W_ps, c - 1)
                    ssp.dve_result(dve, sp_out[:, u, :], c, u)
                    dve.wait_ge(W_ps, c + 1)
                    dve.wait_ge(L_sb, c + 1)
                    after(dve, R_ps, c - 1)
                    nc.vector.scalar_tensor_tensor(msg[:, u, :], psW[:], b2[:], hl[:, u, :], ALU.add, ALU.mult).then_inc(msg_done, 1)

                def add(c, u):
                    dve.wait_ge(R_sb, c + 1)
                    ch.step(c)
                    for q in range(J):
                        ch.link(nc.vector.scalar_tensor_tensor(
                            edges[:, bass.ds((c * J + q + 1) * D, D)], edges[:, bass.ds((c * J + q) * D, D)],
                            plan.same[:, bass.ds(c * J + q, 1)], cut_rows[:, u, q, :], ALU.mult, ALU.add))
                each_phases(dve, n, [None, take, soft, add])
                dve.wait_ge(carried, 1)
                nc.vector.tensor_copy(carry[:], psA[:, 0:D]).then_inc(taken, 1)
                dve.wait_ge(taken, 1)

            @block.tensor
            def _(pe):
                pe.wait_ge(weights, 80)

                def turn(c, u):
                    landed(pe, got, c, u, 2 * J)
                    after(pe, A_sb, c)
                    after(pe, H_sb, c)
                    for q in range(J):
                        nc.tensor.transpose(psA[:, q * P:(q + 1) * P], attr_in[:, u, q, :], k.ident[:])
                    for q in range(J):
                        last = nc.tensor.transpose(psH[:, q * P:(q + 1) * P], rows_in[:, u, q, :], k.ident[:])
                    last.then_inc(A_ps, 1)
                    pe.wait_ge(H_sb, c + 1)
                    after(pe, L_sb, c)
                    nc.tensor.matmul(psL[:], lin1[:], hT[:, u, :], start=True, stop=True).then_inc(L_ps, 1)
                    pe.wait_ge(A_sb, c + 1)
                    after(pe, ssp.taken, c - 1)
                    nc.tensor.matmul(psV[u][:], w1[:], aT[:, u, :], start=True, stop=True).then_inc(V_ps, 1)

                def filt(c, u):
                    pe.wait_ge(ssp.used, c + 1)
                    after(pe, msg_done, c)
                    nc.tensor.matmul(psW[:], w2[:], sp_out[:, u, :], start=True, stop=True).then_inc(W_ps, 1)

                def back(c, u):
                    pe.wait_ge(msg_done, c + 1)
                    after(pe, R_sb, c - 1)
                    for q in range(J):
                        last = nc.tensor.transpose(psR[u][:, q * D:(q + 1) * D], msg[:, u, q * P:(q + 1) * P], k.ident[:])
                    last.then_inc(R_ps, 1)
                each_phases(pe, n, [None, turn, filt, back])
                pe.wait_ge(chain, n * J)
                nc.tensor.matmul(psA[:, 0:D], plan.carry[:], edges[:, s.T * D:], start=True, stop=True).then_inc(carried, 1)


def last_update(nc, k, s, L3, X, S, out):
    with Stage(nc, "node3") as st:
        xin, sin, y = (st.sb(v, [P, R, J, D]) for v in ("xin", "sin", "y"))
        sT, a_sb = st.sb("sT", [P, R, CH]), st.sb("a", [P, R, CH])
        w1, w2, b1 = st.sb("w1", [P, D]), st.sb("w2", [P, D]), st.sb("b1", [P, 1])
        bias = st.sb("bias", [1, J, D])
        ssp = Ssp(nc, st, k, b1, R)
        psT = [st.ps(f"psT{i}", [P, CH]) for i in range(2)]
        psA = [st.ps(f"psA{i}", [P, CH]) for i in range(2)]
        psB = [st.ps(f"psB{i}", [P, CH]) for i in range(2)]
        xl, sl, ys = ([st.sem(f"{v}{i}") for i in range(R)] for v in ("xl", "sl", "ys"))
        weights, T_ps, T_sb, A_ps, B_ps, y_done = (
            st.sem(v) for v in ("weights", "T_ps", "T_sb", "A_ps", "B_ps", "y_done"))
        n = s.chunks
        with st.run() as block:

            @block.sync
            def _(sp):
                for j in range(J):
                    sp.dma_start(bias[:, j, :], row(L3["lin_b"])).then_inc(weights, 16)
                sp.dma_start(w1[:], L3["lin2_w"][:, :]).then_inc(weights, 16)
                sp.dma_start(w2[:], L3["lin_w"][:, :]).then_inc(weights, 16)
                sp.dma_start(b1[:], column(L3["lin2_b"])).then_inc(weights, 16)

                def load(c, u):
                    after(sp, T_ps, c - R + 1)
                    sp.dma_start(sin[:, u], rows(S, c)).then_inc(sl[u], 16)

                def load2(c, u):
                    after(sp, y_done, c - R + 1)
                    sp.dma_start(xin[:, u], rows(X, c)).then_inc(xl[u], 16)

                def store(c, u):
                    sp.wait_ge(y_done, c + 1)
                    if isinstance(c, int) and c == n - 1:
                        sp.dma_start(out[c * CH:s.N, :].rearrange("(p j) d -> p j d", j=J), y[0:s.tp, u]).then_inc(ys[u], 16)
                    else:
                        sp.dma_start(rows(out, c), y[:, u]).then_inc(ys[u], 16)
                each_phases(sp, n, [load, load2, None, None, store], R)
                all_landed(sp, ys, n)

            @block.tensor
            def _(pe):
                pe.wait_ge(weights, 16 * (J + 3))

                def turn(c, u):
                    landed(pe, sl, c, u)
                    after(pe, T_sb, c - 1)
                    for j in range(J):
                        last = nc.tensor.transpose(psT[u % 2][:, j * P:(j + 1) * P], sin[:, u, j, :], k.ident[:])
                    last.then_inc(T_ps, 1)

                def up(c, u):
                    pe.wait_ge(T_sb, c + 1)
                    after(pe, ssp.taken, c - 1)
                    nc.tensor.matmul(psA[u % 2][:], w1[:], sT[:, u, :], start=True, stop=True).then_inc(A_ps, 1)

                def down(c, u):
                    pe.wait_ge(ssp.used, c + 1)
                    after(pe, y_done, c - 1)
                    rows_product(nc, psB[u % 2], a_sb[:, u], w2, bias[:].rearrange("a j d -> a (j d)"), k).then_inc(B_ps, 1)
                each_phases(pe, n, [turn, up, None, down], R)

            @block.scalar
            def _(act):
                act.wait_ge(weights, 16 * (J + 3))

                def take(c, u):
                    act.wait_ge(T_ps, c + 1)
                    after(act, A_ps, c - R + 1)
                    nc.scalar.copy(sT[:, u, :], psT[u % 2][:]).then_inc(T_sb, 1)

                def soft(c, u):
                    ssp.act_log(act, c, u)
                each_phases(act, n, [take, None, soft], R)

            @block.vector
            def _(dve):
                dve.wait_ge(weights, 16 * (J + 3))

                def take(c, u):
                    dve.wait_ge(A_ps, c + 1)
                    ssp.dve_take(dve, psA[u % 2][:], c, u)

                def result(c, u):
                    after(dve, B_ps, c - R + 1)
                    ssp.dve_result(dve, a_sb[:, u, :], c, u)

                def finish(c, u):
                    dve.wait_ge(B_ps, c + 1)
                    landed(dve, xl, c, u)
                    sent(dve, ys, c, u)
                    nc.vector.tensor_tensor(y[:, u].rearrange("p j d -> p (j d)"), psB[u % 2][:],
                                            xin[:, u].rearrange("p j d -> p (j d)"), ALU.add).then_inc(y_done, 1)
                each_phases(dve, n, [None, take, result, finish], R)


def program(nc, a, t):
    s = Shapes(a["x"].shape[0], a["src"].shape[0])
    L0 = {n[7:]: v for n, v in a.items() if n.startswith("L0_gnn_")}
    with ExitStack() as stack:
        k = Constants(stack, nc)
        make_constants(nc, k)
        first_norm(nc, k, s, a["x"], L0["wv"], L0["bv"], L0["wo"], L0["bo"], t["H"], t["Y"])
        src_plan = Plan(stack, nc, s, "src")
        edges = stack.enter_context(nc.sbuf_tensor("edges", [P, (s.T + 1) * D], F32))
        carry = stack.enter_context(nc.sbuf_tensor("carry", [P, D], F32))
        sort_edges(nc, k, s, a["src"], a["dst"], a["edge_weight"], t["rec_src"])
        edge_plan(nc, k, s, t["rec_src"], src_plan)
        sum_neighbours(nc, k, s, src_plan, t["H"], edges, carry)
        attend(nc, k, s, src_plan, L0, t["H"], t["Y"], edges, carry)
        coefs = [stack.enter_context(nc.sbuf_tensor(f"bn_{x}", [P, 1], F32)) for x in ("scale1", "offset1", "scale2", "offset2")]
        node_moments(nc, k, s, t["Y"], L0["g1"], L0["be1"], coefs[0], coefs[1])
        node_mlp(nc, k, s, L0, t["Y"], t["U"], *coefs)
        second_norm(nc, k, s, a["x"], t["U"], t["X"], t["H"], coefs[2], coefs[3])
        L1 = {n[7:]: v for n, v in a.items() if n.startswith("L1_gnn_")}
        dst_plan = Plan(stack, nc, s, "dst")
        zero_table(nc, s, t["S"])
        sort_edges(nc, k, s, a["dst"], a["src"], a["edge_weight"], t["rec_dst"])
        edge_plan(nc, k, s, t["rec_dst"], dst_plan)
        edge_messages(nc, k, s, dst_plan, L1, t["H"], edges, carry)
        scatter_sums(nc, s, dst_plan, t["S"], edges, carry, "scatter1")
        node_update(nc, k, s, L1, t["X"], t["H"], t["S"])
        L3 = {n[7:]: v for n, v in a.items() if n.startswith("L3_gnn_")}
        norms = stack.enter_context(nc.sbuf_tensor("norms", [P, s.T], F32))
        lengths = stack.enter_context(nc.sbuf_tensor("lengths", [P, s.T], F32))
        hyperbolic_messages(nc, k, s, dst_plan, t["H"], edges, norms)
        hyperbolic_fold(nc, k, s, dst_plan, edges, norms, lengths)
        hyperbolic_results(nc, k, s, dst_plan, t["H"], edges, lengths)
        third_norm(nc, k, s, t["X"], t["H"])
        filter_messages(nc, k, s, dst_plan, L3, a["edge_attr_50"], t["H"], edges, carry)
        scatter_sums(nc, s, dst_plan, t["S"], edges, carry, "scatter3")
        last_update(nc, k, s, L3, t["X"], t["S"], t["out"])


def tables(nc, s):
    def dram(name, shape):
        return nc.dram_tensor(name, shape, F32, kind="Internal").ap()
    return {"H": dram("normed", (s.NP, D)), "Y": dram("attended", (s.NP, D)), "U": dram("mlp_out", (s.chunks * P, CH)),
            "X": dram("stream", (s.NP, D)), "S": dram("sums", (s.NP, D)),
            "rec_src": dram("rec_src", (s.EP, REC)), "rec_dst": dram("rec_dst", (s.EP, REC))}


def kernel(**inputs):
    import numpy as np
    from concourse import bacc
    from concourse.bass_utils import run_bass_kernel_spmd

    nc = bacc.Bacc("TRN2", target_bir_lowering=False, num_devices=1)
    arrays, a = {}, {}
    for name, value in inputs.items():
        arrays[f"in_{name}"] = np.ascontiguousarray(value)
        a[name] = nc.dram_tensor(f"in_{name}", arrays[f"in_{name}"].shape, mybir.dt.from_np(arrays[f"in_{name}"].dtype),
                                 kind="ExternalInput").ap()
    a["out"] = nc.dram_tensor("out", inputs["x"].shape, F32, kind="ExternalOutput").ap()
    t = tables(nc, Shapes(inputs["x"].shape[0], inputs["src"].shape[0]))
    t["out"] = a["out"]
    program(nc, a, t)
    r = run_bass_kernel_spmd(nc, [arrays], core_ids=[0])
    return r.results[0]["out"]
```

```python
import math
from contextlib import ExitStack


import concourse.bass as bass
import concourse.mybir as mybir

P = 128
D = 128
J = 4
V = 2
R = 4
CH = P * J
HID = 512
HEADS = 8
DH = D // HEADS
NG = 50
LO_BITS = 9
LO = 1 << LO_BITS
SKIP = 1 << 20
LN_EPS = 1e-5
HYP_EPS = 1e-7
CUTOFF = 6.0

F32 = mybir.dt.float32
F16 = mybir.dt.float16
BF16 = mybir.dt.bfloat16
I32 = mybir.dt.int32
U32 = mybir.dt.uint32
ALU = mybir.AluOpType
ACT = mybir.ActivationFunctionType
AX = mybir.AxisListType

EXP_LN_SET = "natural_log_exp_and_others"

REC_KEY, REC_OTHER, REC_ID, REC_WEIGHT, REC = 0, 1, 2, 3, 4


class Shapes:

    def __init__(self, n_nodes, n_edges):
        self.N, self.E = n_nodes, n_edges
        self.chunks = -(-n_nodes // CH)
        self.chunks += self.chunks % 2
        self.NP = self.chunks * CH
        self.tail = n_nodes - (self.chunks - 1) * CH
        assert 0 < self.tail < CH and self.tail % J == 0
        self.tp = self.tail // J
        self.tiles = -(-n_edges // P)
        self.tiles += self.tiles % 2
        self.echunks = self.tiles * P // CH + 1
        self.echunks += self.echunks % 2
        self.T = self.echunks * J
        self.EP = self.T * P
        assert self.EP > self.tiles * P and n_nodes + 1 <= P * LO


def after(eng, sem, value):
    if isinstance(value, int) and value <= 0:
        return
    eng.wait_ge(sem, value)


def each(eng, n, body, ring=2, peel=1):
    front = min(peel * ring, n)
    loops = max((n - front - 1) // ring, 0)
    for c in range(front):
        body(c, c % ring)
    if loops:
        with eng.Fori(peel, peel + loops) as i:
            for u in range(ring):
                body(i * ring + u, u)
    for c in range(front + loops * ring, n):
        body(c, c % ring)


def each_phases(eng, n, phases, ring=2):
    phases = [f if isinstance(f, tuple) else (i, f) for i, f in enumerate(phases)]
    lags = max(i for i, f in phases) + 1
    peel = -(-(lags + ring - 1) // ring)

    def body(c, u):
        for i, f in phases:
            if f is not None and not (isinstance(c, int) and c < i):
                f(c - i, (u - i) % ring)
    each(eng, n, body, ring, peel)
    for c in range(n, n + lags - 1):
        for i, f in phases:
            if f is not None and c - i < n:
                f(c - i, (c - i) % ring)




class Chain:

    def __init__(self, eng, sem, per):
        self.eng, self.sem, self.per = eng, sem, per
        self.base, self.n = 0, 0

    def step(self, c):
        self.base, self.n = c * self.per, 0

    def link(self, ins):
        ins.then_inc(self.sem, 1)
        self.n += 1
        assert self.n <= self.per
        self.eng.wait_ge(self.sem, self.base + self.n)


class Stage:

    def __init__(self, nc, name):
        self.nc, self.name, self.stack, self.sems = nc, name, ExitStack(), []

    def __enter__(self):
        return self

    def __exit__(self, *e):
        self.stack.close()
        if e[0] is None:
            self.nc.clear_and_free_semaphores([s.num for s in self.sems])
            self.nc.all_engine_barrier()

    def sb(self, name, shape, dt=F32):
        return self.stack.enter_context(self.nc.sbuf_tensor(f"{self.name}_{name}", shape, dt))

    def ps(self, name, shape, dt=F32):
        return self.stack.enter_context(self.nc.psum_tensor(f"{self.name}_{name}", shape, dt))

    def sem(self, name):
        s = self.nc.alloc_semaphore(f"{self.name}_{name}")
        self.sems.append(s)
        return s

    def run(self):
        return self.nc.Block()


def rows(table, c):
    return table[bass.ds(c * CH, CH), :].rearrange("(p j) d -> p j d", j=J)


def make_constants(nc, k):
    with Stage(nc, "consts") as st:
        made = st.sem("made")
        seen = st.sem("seen")
        with st.run() as block:

            @block.gpsimd
            def _(pool):
                n = 0
                for t, v in ((k.ident, 0.0), (k.lower, 1.0), (k.strict, 1.0), (k.shift, 0.0),
                             (k.unshift, 0.0), (k.ones, 1.0), (k.e_first, 0.0),
                             (k.eps_col, LN_EPS), (k.half_col, 0.5)):
                    pool.memset(t[:], v).then_inc(made, 1)
                    n += 1
                pool.wait_ge(made, n)
                pool.affine_select(out=k.ident[:], in_=k.ident[:], compare_op=ALU.not_equal, fill=1.0,
                                   base=0, pattern=[[-1, P]], channel_multiplier=1).then_inc(made, 1)
                pool.affine_select(out=k.lower[:], in_=k.lower[:], compare_op=ALU.is_gt, fill=0.0,
                                   base=0, pattern=[[-1, P]], channel_multiplier=1).then_inc(made, 1)
                pool.affine_select(out=k.strict[:], in_=k.strict[:], compare_op=ALU.is_gt, fill=0.0,
                                   base=0, pattern=[[1, P]], channel_multiplier=-1).then_inc(made, 1)
                pool.affine_select(out=k.shift[:], in_=k.shift[:], compare_op=ALU.not_equal, fill=1.0,
                                   base=1, pattern=[[-1, P]], channel_multiplier=1).then_inc(made, 1)
                pool.affine_select(out=k.unshift[:], in_=k.unshift[:], compare_op=ALU.not_equal, fill=1.0,
                                   base=-1, pattern=[[-1, P]], channel_multiplier=1).then_inc(made, 1)
                pool.affine_select(out=k.e_first[:], in_=k.e_first[:], compare_op=ALU.not_equal, fill=1.0,
                                   base=0, pattern=[[0, 1]], channel_multiplier=1).then_inc(made, 1)
                n += 6
                pool.wait_ge(made, n)

            @block.vector
            def _(dve):
                dve.wait_ge(made, 15)
                nc.vector.tensor_copy(k.ident16[:], k.ident[:]).then_inc(seen, 1)
                dve.wait_ge(seen, 1)


def sort_edges(nc, k, s, key, other, weight, rec, zeroed=None):
    zero_parts = 14 if zeroed is not None else 0
    full = s.E // P
    rem = s.E - full * P
    halves = [(0, min(full, P)), (P, max(full - P, 0))]
    with Stage(nc, f"sort_{key.tensor.name}") as st:
        raw = st.sb("raw", [P, 4, 2, P], I32)
        asf = st.sb("asf", [P, 5, 2, P])
        lanes = st.sb("lanes", [P, 5, 2 * P])
        recs = st.sb("recs", [P, 2 * P, REC])
        iota_i = st.sb("iota_i", [P, LO], I32)
        iota_h = st.sb("iota_h", [P, LO], F16)
        ids = st.sb("ids", [P, 2 * P], I32)
        pad = st.sb("pad", [P, (s.EP // P - s.tiles) * REC])
        hot_hi = st.sb("hot_hi", [P, R, P], BF16)
        hot_lo = st.sb("hot_lo", [P, R, LO], BF16)
        zeros = st.sb("zeros", [P, LO], BF16)
        scan = st.sb("scan", [P, LO])
        onesf = st.sb("onesf", [P, LO])
        rowtot = st.sb("rowtot", [P, 1])
        table = st.sb("table", [P, R, LO])
        hotT = st.sb("hotT", [P, R, P])
        diag = st.sb("diag", [P, R, P])
        junk = st.sb("junk", [P, LO])
        junk2 = st.sb("junk2", [P, P])
        rank = st.sb("rank", [P, R])
        base = st.sb("base", [P, R])
        place = st.sb("place", [P, R], U32)
        outrec = st.sb("outrec", [P, R, REC])
        psT = [st.ps(f"psT{i}", [P, 2 * P]) for i in range(2)]
        count = st.ps("count", [P, LO])
        look = [st.ps(f"look{i}", [P, LO]) for i in range(2)]
        psH = [st.ps(f"psH{i}", [P, P], BF16) for i in range(2)]
        psR = psT[0][:, 0:1]
        psK = [psT[i][:, 0:P] for i in range(2)]

        loaded, cleared, chain = st.sem("loaded"), st.sem("cleared"), st.sem("chain")
        split, turned, taken = st.sem("split"), st.sem("turned"), st.sem("taken")
        iotas, hot, counted = st.sem("iotas"), st.sem("hot"), st.sem("counted")
        totals, offsets, started = st.sem("totals"), st.sem("offsets"), st.sem("started")
        seeded = st.sem("seeded")
        t_hot, t_updated, t_hotT, t_copied, t_hotT_sb = (st.sem("t_hot"), st.sem("t_updated"), st.sem("t_hotT"),
                                                         st.sem("t_copied"), st.sem("t_hotT_sb"))
        t_diag, t_keys, t_rank, t_look, t_place = (st.sem("t_diag"), st.sem("t_keys"), st.sem("t_rank"),
                                                   st.sem("t_look"), st.sem("t_place"))
        t_rec, padded, pad_sent, tick = st.sem("t_rec"), st.sem("padded"), st.sem("pad_sent"), st.sem("tick")
        t_sent = [st.sem(f"t_sent{i}") for i in range(R)]
        n_loads = 3 * ((1 if halves[0][1] else 0) + (1 if halves[1][1] else 0) + (1 if rem else 0))
        rem_half, rem_row = full // P, full % P
        first_pad = s.tiles * P

        if zero_parts:
            width = s.NP * D // P // zero_parts
            flat = zeroed.rearrange("(p r) d -> p (r d)", p=P)
            blank = st.sb("blank", [P, width])
            blanked, zeros_sent = st.sem("blanked"), st.sem("zeros_sent")

        with st.run() as block:

            @block.sync
            def _(sp):
                sp.wait_ge(cleared, 4)
                for a, src in ((0, key), (1, other)):
                    for h, (t0, nt) in enumerate(halves):
                        if nt:
                            sp.dma_start(raw[0:nt, a, h, :], src[t0 * P:(t0 + nt) * P].rearrange("(t e) -> t e", e=P)).then_inc(loaded, 16)
                    if rem:
                        sp.dma_start(raw[rem_row:rem_row + 1, a, rem_half, 0:rem],
                                     src[full * P:s.E].rearrange("(t e) -> t e", t=1)).then_inc(loaded, 16)
                for h, (t0, nt) in enumerate(halves):
                    if nt:
                        sp.dma_start(asf[0:nt, 4, h, :], weight[t0 * P:(t0 + nt) * P].rearrange("(t e) -> t e", e=P)).then_inc(loaded, 16)
                if rem:
                    sp.dma_start(asf[rem_row:rem_row + 1, 4, rem_half, 0:rem],
                                 weight[full * P:s.E].rearrange("(t e) -> t e", t=1)).then_inc(loaded, 16)
                sp.wait_ge(padded, 2)
                sp.dma_start(rec[first_pad:s.EP, :].rearrange("(p t) r -> p (t r)", p=P), pad[:]).then_inc(pad_sent, 16)
                if zero_parts:
                    sp.wait_ge(blanked, 1)
                    for i in range(zero_parts):
                        sp.dma_start(flat[:, i * width:(i + 1) * width], blank[:]).then_inc(zeros_sent, 16)
                    sp.wait_ge(zeros_sent, 16 * zero_parts)
                sp.wait_ge(pad_sent, 16)

            @block.gpsimd
            def _(pool):
                pool.memset(raw[:, 0], s.N).then_inc(cleared, 1)
                pool.memset(raw[:, 1], 0).then_inc(cleared, 1)
                pool.memset(asf[:, 4], 0.0).then_inc(cleared, 1)
                pool.memset(zeros[:], 0.0).then_inc(cleared, 1)
                pool.memset(onesf[:], 1.0).then_inc(iotas, 1)
                pool.iota(iota_i[:], [[1, LO]], base=0, channel_multiplier=0).then_inc(iotas, 1)
                pool.iota(ids[:], [[P, 2 * P]], base=0, channel_multiplier=1).then_inc(iotas, 1)
                pool.memset(pad[:], 0.0).then_inc(padded, 1)
                pool.wait_ge(padded, 1)
                pool.memset(pad[:].rearrange("p (t r) -> p t r", r=REC)[:, :, REC_KEY], float(s.N)).then_inc(padded, 1)

                if zero_parts:
                    pool.memset(blank[:], 0.0).then_inc(blanked, 1)

                bound = pool.to_reg(s.EP - 1)

                def send(t, u):
                    pool.wait_ge(t_place, t + 1)
                    pool.wait_ge(t_rec, t + 1)
                    pool.sem_inc(tick, 1)
                    pool.indirect_dma_start(out=rec, out_offset=bass.IndirectOffsetOnAxis(ap=place[:, u:u + 1], axis=0),
                                            in_=outrec[:, u, :], in_offset=None, bounds_check=bound,
                                            oob_is_err=False).then_inc(t_sent[u], 16)
                each(pool, s.tiles, send, R)
                all_landed(pool, t_sent, s.tiles)

            @block.vector
            def _(dve):
                ch = Chain(dve, chain, 8)
                dve.wait_ge(loaded, 16 * n_loads)
                dve.wait_ge(iotas, 3)
                nc.vector.tensor_scalar(raw[:, 2], raw[:, 0], LO_BITS, None, ALU.logical_shift_right).then_inc(chain, 1)
                nc.vector.tensor_scalar(raw[:, 3], raw[:, 0], LO - 1, None, ALU.bitwise_and).then_inc(chain, 1)
                nc.vector.tensor_copy(iota_h[:], iota_i[:]).then_inc(chain, 1)
                dve.wait_ge(chain, 3)
                nc.vector.tensor_copy(asf[:, 0:4], raw[:]).then_inc(split, 1)
                nc.vector.tensor_copy(recs[:, :, REC_ID], ids[:]).then_inc(chain, 1)
                for a in range(5):
                    dve.wait_ge(turned, a + 1)
                    nc.vector.tensor_copy(lanes[:, a, :], psT[a % 2][:]).then_inc(taken, 1)
                dve.wait_ge(taken, 5)
                nc.vector.tensor_copy(recs[:, :, REC_KEY], lanes[:, 0, :]).then_inc(chain, 1)
                nc.vector.tensor_copy(recs[:, :, REC_OTHER], lanes[:, 1, :]).then_inc(chain, 1)
                nc.vector.tensor_copy(recs[:, :, REC_WEIGHT], lanes[:, 4, :]).then_inc(chain, 1)
                dve.wait_ge(chain, 7)

                def one_hots(t, u):
                    nc.vector.tensor_scalar(hot_hi[:, u, :], iota_h[:, 0:P], lanes[:, 2, bass.ds(t, 1)], None, ALU.is_equal)
                    return nc.vector.tensor_scalar(hot_lo[:, u, :], iota_h[:], lanes[:, 3, bass.ds(t, 1)], None, ALU.is_equal)

                def count_step(t, u):
                    after(dve, counted, t - R + 1)
                    one_hots(t, u).then_inc(hot, 1)
                each(dve, s.tiles, count_step, R)
                dve.wait_ge(counted, s.tiles)
                nc.vector.tensor_tensor_scan(scan[:], onesf[:], count[:], 0.0, ALU.mult, ALU.add).then_inc(chain, 1)
                dve.wait_ge(chain, 8)
                nc.vector.tensor_copy(rowtot[:], scan[:, LO - 1:LO]).then_inc(totals, 1)
                nc.vector.tensor_tensor(junk[:], scan[:], count[:], ALU.subtract).then_inc(chain, 1)
                dve.wait_ge(offsets, 1)
                dve.wait_ge(chain, 9)
                nc.vector.tensor_scalar(table[:, 1, :], junk[:], psR, None, ALU.add).then_inc(started, 1)

                def hot_rows(t, u):
                    after(dve, t_updated, t - R + 1)
                    one_hots(t, u).then_inc(t_hot, 1)

                def look_up(t, u):
                    dve.wait_ge(t_keys, t + 1)
                    after(dve, t_rank, 2 * t)
                    after(dve, t_place, t - R + 1)
                    nc.vector.scalar_tensor_tensor(junk2[:], psK[u % 2], lanes[:, 0, bass.ds(t, 1)], k.lower[:],
                                                   ALU.is_equal, ALU.mult, accum_out=rank[:, u:u + 1]).then_inc(t_rank, 1)
                    dve.wait_ge(t_look, t + 1)
                    nc.vector.scalar_tensor_tensor(junk[:], look[u % 2][:], 1.0, hot_lo[:, u, :],
                                                   ALU.mult, ALU.mult, accum_out=base[:, u:u + 1]).then_inc(t_rank, 1)

                def put(t, u):
                    dve.wait_ge(t_rank, 2 * t + 2)
                    sent(dve, t_sent, t, u)
                    nc.vector.tensor_tensor(place[:, u:u + 1], rank[:, u:u + 1], base[:, u:u + 1], ALU.add).then_inc(t_place, 1)
                    nc.vector.tensor_copy(outrec[:, u, :], recs[:].rearrange("p t r -> p (t r)")[:, bass.ds(t * REC, REC)]).then_inc(t_rec, 1)
                each_phases(dve, s.tiles, [hot_rows, None, look_up, put], R)

            @block.tensor
            def _(pe):
                pe.wait_ge(split, 1)
                for a in range(5):
                    after(pe, taken, a - 1)
                    nc.tensor.transpose(psT[a % 2][:, 0:P], asf[:, a, 0, :], k.ident[:])
                    nc.tensor.transpose(psT[a % 2][:, P:2 * P], asf[:, a, 1, :], k.ident[:]).then_inc(turned, 1)
                pe.wait_ge(cleared, 4)
                nc.tensor.matmul(count[:], zeros[:, 0:P], zeros[:], start=True, stop=False, skip_group_check=True)

                def count_step(t, u):
                    pe.wait_ge(hot, t + 1)
                    nc.tensor.matmul(count[:], hot_hi[:, u, :], hot_lo[:, u, :], start=False, stop=False,
                                     skip_group_check=True).then_inc(counted, 1)
                each(pe, s.tiles, count_step, R)
                pe.wait_ge(totals, 1)
                nc.tensor.matmul(psR, k.strict[:], rowtot[:], start=True, stop=True).then_inc(offsets, 1)
                pe.wait_ge(started, 1)
                nc.tensor.matmul(count[:], k.ident[:], table[:, 1, :], start=True, stop=False,
                                 skip_group_check=True).then_inc(seeded, 1)

                def update(t, u):
                    pe.wait_ge(t_hot, t + 1)
                    after(pe, t_hotT_sb, t - 1)
                    nc.tensor.transpose(psH[u % 2][:], hot_hi[:, u, :], k.ident16[:]).then_inc(t_hotT, 1)
                    pe.wait_ge(t_copied, t + 1)
                    nc.tensor.matmul(count[:], hot_hi[:, u, :], hot_lo[:, u, :], start=False, stop=False,
                                     skip_group_check=True).then_inc(t_updated, 1)

                def look_up(t, u):
                    pe.wait_ge(t_hotT_sb, t + 1)
                    after(pe, t_rank, 2 * t - 2)
                    nc.tensor.matmul(look[u % 2][:], hotT[:, u, :], table[:, u, :], start=True, stop=True).then_inc(t_look, 1)
                    pe.wait_ge(t_diag, t + 1)
                    nc.tensor.matmul(psK[u % 2], k.ones[:], diag[:, u, :], start=True, stop=True).then_inc(t_keys, 1)
                each_phases(pe, s.tiles, [update, look_up], R)

            @block.scalar
            def _(act):
                act.wait_ge(seeded, 1)

                def copies(t, u):
                    after(act, t_updated, t)
                    after(act, t_look, t - R + 1)
                    nc.scalar.copy(table[:, u, :], count[:]).then_inc(t_copied, 1)
                    after(act, t_keys, t - R + 1)
                    nc.scalar.mul(diag[:, u, :], k.ident[:], lanes[:, 0, bass.ds(t, 1)]).then_inc(t_diag, 1)
                    act.wait_ge(t_hotT, t + 1)
                    nc.scalar.copy(hotT[:, u, :], psH[u % 2][:]).then_inc(t_hotT_sb, 1)
                each(act, s.tiles, copies, R)


def edge_plan(nc, k, s, rec, plan):
    T = s.T
    with Stage(nc, f"plan_{plan.name}") as st:
        r = st.sb("r", [P, T, REC])
        keyf = st.sb("keyf", [P, T + 2])
        tmp = st.sb("tmp", [P, T])
        real = st.sb("real", [P, T])
        lastf = st.sb("lastf", [P, T])
        ones = st.sb("ones", [P, T])
        diag = st.sb("diag", [P, P])
        cc = st.sb("cc", [P, 1])
        psE = st.ps("psE", [P, 8])
        psB = st.ps("psB", [P, P])
        loaded, chain = st.sem("loaded"), st.sem("chain")
        keys, ends, first, firsts = st.sem("keys"), st.sem("ends"), st.sem("first"), st.sem("firsts")
        counts, carried = st.sem("counts"), st.sem("carried")
        ones_made = st.sem("ones_made")
        with st.run() as block:

            @block.sync
            def _(sp):
                sp.dma_start(r[:], rec[:, :].rearrange("(p t) r -> p t r", p=P)).then_inc(loaded, 16)
                sp.wait_ge(loaded, 16)

            @block.gpsimd
            def _(pool):
                pool.memset(ones[:], 1.0).then_inc(ones_made, 1)

            @block.vector
            def _(dve):
                ch = Chain(dve, chain, 99)
                key = keyf[:, 1:T + 1]
                dve.wait_ge(loaded, 16)
                nc.vector.tensor_copy(key, r[:, :, REC_KEY]).then_inc(keys, 1)
                nc.vector.tensor_copy(plan.other[:], r[:, :, REC_OTHER])
                nc.vector.tensor_copy(plan.edge[:], r[:, :, REC_ID])
                nc.vector.tensor_copy(plan.weight[:], r[:, :, REC_WEIGHT])
                dve.wait_ge(keys, 1)
                nc.vector.tensor_scalar(diag[:], k.ident[:], keyf[:, 1:2], None, ALU.mult).then_inc(first, 1)
                dve.wait_ge(ends, 1)
                nc.vector.tensor_tensor(keyf[:, 0:1], psE[:, 0:1], k.e_first[:], ALU.subtract)
                ch.link(nc.vector.tensor_copy(keyf[:, T + 1:T + 2], psE[:, 1:2]))
                nc.vector.tensor_tensor(plan.same[:], key, keyf[:, 0:T], ALU.is_equal)
                nc.vector.tensor_tensor(lastf[:], key, keyf[:, 2:T + 2], ALU.not_equal)
                nc.vector.tensor_scalar(real[:], key, float(s.N), None, ALU.is_lt)
                nc.vector.tensor_scalar(plan.first[:], key, keyf[:, 1:2], None, ALU.is_equal)
                ch.link(nc.vector.tensor_tensor(tmp[:], key, key, ALU.bypass))
                ch.link(nc.vector.tensor_tensor(lastf[:], lastf[:], real[:], ALU.mult))
                nc.vector.tensor_copy(plan.cont[:], plan.same[:, 0:1])
                ch.link(nc.vector.tensor_tensor(tmp[:], key, real[:], ALU.mult))
                ch.link(nc.vector.tensor_copy(plan.key[:], tmp[:]))
                ch.link(nc.vector.tensor_scalar(tmp[:], lastf[:], -float(SKIP), float(SKIP), ALU.mult, ALU.add))
                ch.link(nc.vector.tensor_tensor(lastf[:], lastf[:], key, ALU.mult))
                ch.link(nc.vector.tensor_tensor(plan.last[:], tmp[:], lastf[:], ALU.add))
                ch.link(nc.vector.memset(plan.same[:, 0:1], 1.0))
                dve.wait_ge(firsts, 1)
                ch.link(nc.vector.scalar_tensor_tensor(plan.carry[:], psB[:], keyf[:, T:T + 1], k.strict[:],
                                                       ALU.is_equal, ALU.mult))
                dve.wait_ge(ones_made, 1)
                ch.link(nc.vector.tensor_tensor_scan(plan.count[:], plan.same[:], ones[:], 0.0, ALU.mult, ALU.add))
                nc.vector.tensor_copy(tmp[:, 0:1], plan.count[:, T - 1:T]).then_inc(counts, 1)
                dve.wait_ge(carried, 1)
                ch.link(nc.vector.tensor_copy(cc[:], psE[:, 2:3]))
                ch.link(nc.vector.scalar_tensor_tensor(plan.count[:], plan.first[:], cc[:], plan.count[:],
                                                       ALU.mult, ALU.add))
                ch.link(nc.vector.reciprocal(plan.inv[:], plan.count[:]))
                L = T // V
                for v in range(V):
                    goes_on = plan.cont[:] if v == 0 else plan.same[:, v * L:v * L + 1]
                    ch.link(nc.vector.tensor_tensor(tmp[:, 1:2], keyf[:, v * L + 1:v * L + 2], keyf[:, (v + 1) * L:(v + 1) * L + 1], ALU.is_equal))
                    ch.link(nc.vector.tensor_tensor(tmp[:, 1:2], tmp[:, 1:2], goes_on, ALU.mult))
                    into = plan.through[:] if v == 0 else tmp[:, 1:2]
                    ch.link(nc.vector.tensor_tensor(into, tmp[:, 1:2], real[:, v * L:v * L + 1], ALU.mult))
                    if v:
                        ch.link(nc.vector.tensor_tensor(plan.through[:], plan.through[:], tmp[:, 1:2], ALU.add))

            @block.tensor
            def _(pe):
                pe.wait_ge(keys, 1)
                nc.tensor.matmul(psE[:, 0:1], k.shift[:], keyf[:, T:T + 1], start=True, stop=True)
                nc.tensor.matmul(psE[:, 1:2], k.unshift[:], keyf[:, 1:2], start=True, stop=True).then_inc(ends, 1)
                pe.wait_ge(first, 1)
                nc.tensor.matmul(psB[:], k.ones[:], diag[:], start=True, stop=True).then_inc(firsts, 1)
                pe.wait_ge(counts, 1)
                nc.tensor.matmul(psE[:, 2:3], plan.carry[:], tmp[:, 0:1], start=True, stop=True).then_inc(carried, 1)


class Constants:
    def __init__(self, stack, nc):
        def sb(name, shape, dt=F32):
            return stack.enter_context(nc.sbuf_tensor(name, shape, dt))
        self.ident, self.ident16 = sb("ident", [P, P]), sb("ident16", [P, P], BF16)
        self.ones = sb("ones", [P, P])
        self.lower, self.strict = sb("lower", [P, P]), sb("strict", [P, P])
        self.shift, self.unshift = sb("shift", [P, P]), sb("unshift", [P, P])
        self.e_first = sb("e_first", [P, 1])
        self.eps_col, self.half_col = sb("eps_col", [P, 1]), sb("half_col", [P, 1])


class Plan:

    def __init__(self, stack, nc, s, name):
        def sb(n, shape, dt=F32):
            return stack.enter_context(nc.sbuf_tensor(f"{name}_{n}", shape, dt))
        T = s.T
        self.name = name
        self.key, self.other, self.edge = sb("key", [P, T], U32), sb("other", [P, T], U32), sb("edge", [P, T], U32)
        self.last = sb("last", [P, T], U32)
        self.weight = sb("weight", [P, T])
        self.same = sb("same", [P, T])
        self.first = sb("first", [P, T])
        self.count, self.inv = sb("count", [P, T]), sb("inv", [P, T])
        self.carry = sb("carry", [P, P])
        self.cont, self.through = sb("cont", [P, 1]), sb("through", [P, 1])


def sent(eng, sems, c, u, per=1):
    ring = len(sems)
    if isinstance(c, int):
        after(eng, sems[u], 16 * per * ((c - u) // ring))
    else:
        eng.wait_ge(sems[u], (c - u) * (16 * per // ring))


def landed(eng, sems, c, u, per=1):
    eng.wait_ge(sems[u], (c - u) * (16 * per // len(sems)) + 16 * per)


def all_landed(eng, sems, n, per=1):
    for u, sem in enumerate(sems):
        eng.wait_ge(sem, -(-(n - u) // len(sems)) * 16 * per)


class Norm:

    def __init__(self, nc, st, k):
        self.nc, self.k = nc, k
        self.stats = st.sb("ln_stats", [P, R, J, 6])
        self.mv = st.sb("ln_mv", [P, R, J, 2])
        self.std = st.sb("ln_std", [P, R, J])
        self.scale = st.sb("ln_scale", [P, R, J])
        self.bias = st.sb("ln_bias", [P, R, J])
        self.halves, self.moments, self.roots, self.coefs = (st.sem("ln_halves"), st.sem("ln_moments"),
                                                             st.sem("ln_roots"), st.sem("ln_coefs"))
        self.scaled, self.tick = st.sem("ln_scaled"), st.sem("ln_tick")

    def dve_moments(self, dve, x, c, u):
        for j in range(J):
            last = self.nc.vector.bn_stats(self.stats[:, u, j, :], x[:, j, :])
        last.then_inc(self.halves, 1)
        dve.wait_ge(self.halves, c + 1)
        after(dve, self.coefs, c - R + 1)
        dve.sem_inc(self.tick, 1)
        for j in range(J):
            last = self.nc.vector.bn_aggr(self.mv[:, u, j, :], self.stats[:, u, j, :])
        last.then_inc(self.moments, 1)

    def act_root(self, act, c, u):
        act.wait_ge(self.moments, c + 1)
        after(act, self.scaled, c - R + 1)
        self.nc.scalar.activation(self.std[:, u, :], self.mv[:, u, :, 1], ACT.Sqrt,
                                  bias=self.k.eps_col[:]).then_inc(self.roots, 1)

    def dve_coefs(self, dve, c, u, used):
        dve.wait_ge(self.roots, c + 1)
        used()
        self.nc.vector.reciprocal(self.scale[:, u, :], self.std[:, u, :]).then_inc(self.scaled, 1)
        dve.wait_ge(self.scaled, c + 1)
        self.nc.vector.scalar_tensor_tensor(self.bias[:, u, :], self.mv[:, u, :, 0], -1.0, self.scale[:, u, :],
                                            ALU.mult, ALU.mult).then_inc(self.coefs, 1)

    def act_apply(self, act, h, x, c, u):
        act.wait_ge(self.coefs, c + 1)
        for j in range(J):
            last = self.nc.scalar.activation(h[:, j, :], x[:, j, :], ACT.Relu, bias=self.bias[:, u, j:j + 1],
                                             scale=self.scale[:, u, j:j + 1])
        return last


def rows_product(nc, out, lhsT, w, bias, k):
    for j in range(J):
        nc.tensor.matmul(out[:, j * D:(j + 1) * D], lhsT[:, j * P:(j + 1) * P], w[:], start=j == 0, stop=False,
                         skip_group_check=True)
    return nc.tensor.matmul(out[:], k.ones[0:1, :], bias, start=False, stop=True, skip_group_check=True)


def load_x(nc, sp, s, x, dst, c, sem):
    if isinstance(c, int) and c == s.chunks - 1:
        r0 = c * CH
        sp.dma_start(dst[0:s.tp], x[r0:s.N, :].rearrange("(p j) d -> p j d", j=J)).then_inc(sem, 16)
        sp.dma_start(dst[s.tp:P], x[0:(P - s.tp) * J, :].rearrange("(p j) d -> p j d", j=J)).then_inc(sem, 16)
    else:
        sp.dma_start(dst, rows(x, c)).then_inc(sem, 16)


def first_norm(nc, k, s, x, wv, bv, wo, bo, H, Y):
    with Stage(nc, "norm0") as st:
        norm = Norm(nc, st, k)
        xin = st.sb("xin", [P, R, J, D])
        h = st.sb("h", [P, R, J, D])
        hT = st.sb("hT", [P, R, CH])
        y = st.sb("y", [P, R, J, D])
        wv_sb, wo_sb, mean = st.sb("wv", [P, D]), st.sb("wo", [P, D]), st.sb("mean", [P, D])
        wvT, wmean, wc = st.sb("wvT", [P, D]), st.sb("wmean", [P, D]), st.sb("wc", [P, D])
        bv_sb, bo_sb = st.sb("bv", [P, 1]), st.sb("bo", [1, D])
        bias = st.sb("bias", [1, J, D])
        headi = st.sb("headi", [P, D], I32)
        psT = [st.ps(f"psT{i}", [P, CH]) for i in range(2)]
        psY = [st.ps(f"psY{i}", [P, CH]) for i in range(2)]
        psW = st.ps("psW", [P, 4, P])
        weights, prep, mixed, used = st.sem("weights"), st.sem("prep"), st.sem("mixed"), st.sem("used")
        xl = [st.sem(f"xl{i}") for i in range(R)]
        hs = [st.sem(f"hs{i}") for i in range(R)]
        ys = [st.sem(f"ys{i}") for i in range(R)]
        h_done, hT_ps, hT_sb, y_ps, y_sb = (st.sem("h_done"), st.sem("hT_ps"), st.sem("hT_sb"),
                                            st.sem("y_ps"), st.sem("y_sb"))
        n = s.chunks
        with st.run() as block:

            @block.sync
            def _(sp):
                for dst, src in ((wv_sb, wv[:, :]), (wo_sb, wo[:, :]), (bv_sb, column(bv)), (bo_sb, row(bo))):
                    sp.dma_start(dst[:], src).then_inc(weights, 16)

                def load(c, u):
                    after(sp, h_done, c - R + 1)
                    load_x(nc, sp, s, x, xin[:, u], c, xl[u])

                def store(c, u):
                    sp.wait_ge(h_done, c + 1)
                    sp.dma_start(rows(H, c), h[:, u]).then_inc(hs[u], 16)

                def store2(c, u):
                    sp.wait_ge(y_sb, c + 1)
                    sp.dma_start(rows(Y, c), y[:, u]).then_inc(ys[u], 16)
                each_phases(sp, n, [load, (3, store), (6, store2)], R)
                all_landed(sp, hs, n)
                all_landed(sp, ys, n)

            @block.gpsimd
            def _(pool):
                pool.iota(headi[:], [[-1, D]], base=D, channel_multiplier=1).then_inc(prep, 1)

            @block.vector
            def _(dve):
                dve.wait_ge(prep, 1)
                nc.vector.tensor_scalar(headi[:], headi[:], DH - 1, None, ALU.bitwise_and).then_inc(prep, 1)
                dve.wait_ge(prep, 2)
                nc.vector.tensor_copy(mean[:], headi[:]).then_inc(prep, 1)
                dve.wait_ge(prep, 3)
                nc.vector.tensor_scalar(mean[:], mean[:], 0.0, 1.0 / HEADS, ALU.is_equal, ALU.mult).then_inc(prep, 1)
                dve.wait_ge(mixed, 2)
                nc.vector.tensor_copy(wvT[:], psW[:, 0, :])
                nc.vector.tensor_copy(wmean[:], psW[:, 1, :]).then_inc(used, 1)
                dve.wait_ge(mixed, 4)
                nc.vector.tensor_tensor(wc[:], psW[:, 2, :], k.ident[:], ALU.add)
                for j in range(J):
                    last = nc.vector.tensor_tensor(bias[0:1, j, :], psW[0:1, 3, :], bo_sb[:], ALU.add)
                last.then_inc(used, 1)

                def stats(c, u):
                    if isinstance(c, int) and c == n - 1:
                        dve.wait_ge(xl[u], 16 * (c // R + 2))
                    else:
                        landed(dve, xl, c, u)
                    norm.dve_moments(dve, xin[:, u], c, u)

                def coefs(c, u):
                    norm.dve_coefs(dve, c, u, lambda: after(dve, h_done, c - R + 1))

                def take(c, u):
                    dve.wait_ge(hT_ps, c + 1)
                    after(dve, y_ps, c - R + 1)
                    nc.vector.tensor_copy(hT[:, u, :], psT[u % 2][:]).then_inc(hT_sb, 1)
                each_phases(dve, n, [(1, coefs), (0, stats), (3, take)], R)

            @block.scalar
            def _(act):
                def root(c, u):
                    norm.act_root(act, c, u)

                def apply(c, u):
                    sent(act, hs, c, u)
                    after(act, hT_ps, c - R + 1)
                    norm.act_apply(act, h[:, u], xin[:, u], c, u).then_inc(h_done, 1)

                def take(c, u):
                    act.wait_ge(y_ps, c + 1)
                    sent(act, ys, c, u)
                    nc.scalar.copy(y[:, u].rearrange("p j d -> p (j d)"), psY[u % 2][:]).then_inc(y_sb, 1)
                each_phases(act, n, [(1, apply), (0, root), (4, take)], R)

            @block.tensor
            def _(pe):
                pe.wait_ge(weights, 16 * 4)
                pe.wait_ge(prep, 4)
                nc.tensor.transpose(psW[:, 0, :], wv_sb[:], k.ident[:]).then_inc(mixed, 1)
                nc.tensor.matmul(psW[:, 1, :], mean[:], wo_sb[:], start=True, stop=True).then_inc(mixed, 1)
                pe.wait_ge(used, 1)
                nc.tensor.matmul(psW[:, 2, :], wvT[:], wmean[:], start=True, stop=True).then_inc(mixed, 1)
                nc.tensor.matmul(psW[0:1, 3, :], bv_sb[:], wmean[:], start=True, stop=True).then_inc(mixed, 1)
                pe.wait_ge(used, 2)

                def turn(c, u):
                    pe.wait_ge(h_done, c + 1)
                    after(pe, hT_sb, c - 1)
                    for j in range(J):
                        last = nc.tensor.transpose(psT[u % 2][:, j * P:(j + 1) * P], h[:, u, j, :], k.ident[:])
                    last.then_inc(hT_ps, 1)

                def mix(c, u):
                    pe.wait_ge(hT_sb, c + 1)
                    after(pe, y_sb, c - 1)
                    rows_product(nc, psY[u % 2], hT[:, u], wc, bias[:].rearrange("a j d -> a (j d)"), k).then_inc(y_ps, 1)
                each_phases(pe, n, [turn, mix], R)


def column(v):
    return v.rearrange("(p a) -> p a", a=1)


def row(v):
    return v.rearrange("(a p) -> a p", a=1)


def sum_neighbours(nc, k, s, plan, H, edges, carry):
    with Stage(nc, "sum0") as st:
        got_rows = st.sb("rows", [P, 2, J, D])
        idx = st.sb("idx", [P, 2, J], U32)
        psC = st.ps("psC", [P, D])
        idx_ready, chain, tick = st.sem("idx_ready"), st.sem("chain"), st.sem("tick")
        zeroed, carried, taken = st.sem("zeroed"), st.sem("carried"), st.sem("taken")
        got = [st.sem(f"got{i}") for i in range(2)]
        n = s.echunks
        with st.run() as block:

            @block.gpsimd
            def _(pool):
                bound = pool.to_reg(s.NP - 1)

                def gather(c, u):
                    pool.wait_ge(idx_ready, c + 1)
                    after(pool, chain, (c - 1) * J)
                    pool.sem_inc(tick, 1)
                    for q in range(J):
                        pool.indirect_dma_start(out=got_rows[:, u, q, :], out_offset=None, in_=H,
                                                in_offset=bass.IndirectOffsetOnAxis(ap=idx[:, u, q:q + 1], axis=0),
                                                bounds_check=bound, oob_is_err=False).then_inc(got[u], 16)
                each(pool, n, gather)

            @block.scalar
            def _(act):
                def index(c, u):
                    sent(act, got, c, u, J)
                    nc.scalar.copy(idx[:, u, :], plan.other[:, bass.ds(c * J, J)]).then_inc(idx_ready, 1)
                each(act, n, index)

            @block.vector
            def _(dve):
                ch = Chain(dve, chain, J)
                nc.vector.memset(edges[:, 0:D], 0.0).then_inc(zeroed, 1)
                dve.wait_ge(zeroed, 1)

                def add(c, u):
                    landed(dve, got, c, u, J)
                    ch.step(c)
                    for q in range(J):
                        ch.link(nc.vector.scalar_tensor_tensor(
                            edges[:, bass.ds((c * J + q + 1) * D, D)], edges[:, bass.ds((c * J + q) * D, D)],
                            plan.same[:, bass.ds(c * J + q, 1)], got_rows[:, u, q, :], ALU.mult, ALU.add))
                each(dve, n, add)
                dve.wait_ge(carried, 1)
                nc.vector.tensor_copy(carry[:], psC[:]).then_inc(taken, 1)
                dve.wait_ge(taken, 1)

            @block.tensor
            def _(pe):
                pe.wait_ge(chain, n * J)
                nc.tensor.matmul(psC[:], plan.carry[:], edges[:, s.T * D:], start=True, stop=True).then_inc(carried, 1)


def attend(nc, k, s, plan, L0, H, Y, edges, carry):
    A = 2 * R
    with Stage(nc, "attend") as st:
        hs = st.sb("hs", [P, A, D])
        y = st.sb("y", [P, A, D])
        gidx, sidx = st.sb("gidx", [P, A], U32), st.sb("sidx", [P, A], U32)
        kin, kmean = st.sb("kin", [P, A, D]), st.sb("kmean", [P, A, D])
        turned = st.sb("turned", [P, 2, 2 * D])
        qvk = st.sb("qvk", [P, A, 3 * D])
        prod = st.sb("prod", [P, 1024])
        score, shifted, expd, prob = (st.sb("score", [P, 2, 64]), st.sb("shifted", [P, 2, 64]),
                                      st.sb("expd", [P, A, 64]), st.sb("prob", [P, 2, 64]))
        top, total, inv = st.sb("top", [P, 2, HEADS]), st.sb("total", [P, 2, HEADS]), st.sb("inv", [P, 2, HEADS])
        prod2 = st.sb("prod2", [P, 1024])
        mixed, mixedT = st.sb("mixed", [P, A, D]), st.sb("mixedT", [P, 2, D])
        wqv, wk, wo = st.sb("wqv", [P, 2 * D]), st.sb("wk", [P, D]), st.sb("wo", [P, D])
        bias, bo = st.sb("bias", [1, 3 * D]), st.sb("bo", [1, D])
        psT = [st.ps(f"psT{i}", [P, 2 * D]) for i in range(2)]
        psQ = [st.ps(f"psQ{i}", [P, 3 * D]) for i in range(2)]
        psM = [st.ps(f"psM{i}", [P, D]) for i in range(2)]
        psO = [st.ps(f"psO{i}", [P, D]) for i in range(2)]
        weights, tick = st.sem("weights"), st.sem("tick")
        got = [st.sem(f"got{i}") for i in range(A)]
        put = [st.sem(f"put{i}") for i in range(A)]
        (gidx_ready, sidx_ready, kin_done, kmean_done, T_ps, T_sb, q_ps, q_sb) = (
            st.sem(x) for x in ("gidx_ready", "sidx_ready", "kin_done", "kmean_done", "T_ps", "T_sb", "q_ps", "q_sb"))
        chain, score_done, exp_done, mix_done, m_ps, m_sb, o_ps, y_done = (
            st.sem(x) for x in ("chain", "score_done", "exp_done", "mix_done", "m_ps", "m_sb", "o_ps", "y_done"))
        chain2 = st.sem("chain2")
        n = s.T
        with st.run() as block:

            @block.sync
            def _(sp):
                for dst, src in ((wqv[:, 0:D], L0["wq"][:, :]), (wqv[:, D:2 * D], L0["wv"][:, :]), (wk[:], L0["wk"][:, :]),
                                 (wo[:], L0["wo"][:, :]), (bias[:, 0:D], row(L0["bq"])), (bias[:, D:2 * D], row(L0["bv"])),
                                 (bias[:, 2 * D:3 * D], row(L0["bk"])), (bo[:], row(L0["bo"]))):
                    sp.dma_start(dst, src).then_inc(weights, 16)

            @block.gpsimd
            def _(pool):
                bound = pool.to_reg(s.N - 1)

                def gather(t, u):
                    pool.wait_ge(gidx_ready, t + 1)
                    after(pool, y_done, t - A + 1)
                    pool.sem_inc(tick, 1)
                    pool.indirect_dma_start(out=hs[:, u, :], out_offset=None, in_=H,
                                            in_offset=bass.IndirectOffsetOnAxis(ap=gidx[:, u:u + 1], axis=0),
                                            bounds_check=bound, oob_is_err=False).then_inc(got[u], 16)

                def scatter(t, u):
                    pool.wait_ge(y_done, t + 1)
                    pool.wait_ge(sidx_ready, t + 1)
                    pool.sem_inc(tick, 1)
                    pool.indirect_dma_start(out=Y, out_offset=bass.IndirectOffsetOnAxis(ap=sidx[:, u:u + 1], axis=0),
                                            in_=y[:, u, :], in_offset=None, bounds_check=bound,
                                            oob_is_err=False).then_inc(put[u], 16)
                each_phases(pool, n, [gather, None, None, None, None, None, scatter], A)
                all_landed(pool, put, n)

            @block.vector
            def _(dve):
                def keys(t, u):
                    after(dve, kmean_done, t - A + 1)
                    nc.vector.scalar_tensor_tensor(kin[:, u, :], carry[:], plan.first[:, bass.ds(t, 1)],
                                                   edges[:, bass.ds((t + 1) * D, D)], ALU.mult, ALU.add).then_inc(kin_done, 1)

                def s1(t, u):
                    dve.wait_ge(q_sb, t + 1)
                    q4 = qvk[:, u, 0:D].rearrange("p (h a d) -> p h a d", h=HEADS, a=1).broadcast_to([P, HEADS, HEADS, DH])
                    k4 = qvk[:, u, 2 * D:3 * D].rearrange("p (a g d) -> p a g d", a=1, g=HEADS).broadcast_to([P, HEADS, HEADS, DH])
                    nc.vector.tensor_tensor(prod[:].rearrange("p (h g d) -> p h g d", h=HEADS, g=HEADS), q4, k4, ALU.mult).then_inc(chain, 1)

                def s2(t, u):
                    dve.wait_ge(chain, 3 * t + 1)
                    nc.vector.tensor_reduce(score[:, u % 2, :], prod[:].rearrange("p (a d) -> p a d", d=DH), AX.X, ALU.add).then_inc(chain, 1)

                def s3(t, u):
                    dve.wait_ge(chain, 3 * t + 2)
                    nc.vector.tensor_reduce(top[:, u % 2, :], score[:, u % 2, :].rearrange("p (h g) -> p h g", h=HEADS),
                                            AX.X, ALU.max).then_inc(chain, 1)

                def s4(t, u):
                    dve.wait_ge(chain, 3 * t + 3)
                    after(dve, exp_done, t - 1)
                    v = u % 2
                    nc.vector.tensor_tensor(shifted[:, v, :].rearrange("p (h g) -> p h g", h=HEADS),
                                            score[:, v, :].rearrange("p (h g) -> p h g", h=HEADS),
                                            top[:, v, :].rearrange("p (h a) -> p h a", a=1).broadcast_to([P, HEADS, HEADS]),
                                            ALU.subtract).then_inc(score_done, 1)

                def m1(t, u):
                    dve.wait_ge(exp_done, t + 1)
                    nc.vector.tensor_reduce(total[:, u % 2, :], expd[:, u, :].rearrange("p (h g) -> p h g", h=HEADS),
                                            AX.X, ALU.add).then_inc(chain2, 1)

                def m2(t, u):
                    dve.wait_ge(chain2, 4 * t + 1)
                    nc.vector.reciprocal(inv[:, u % 2, :], total[:, u % 2, :]).then_inc(chain2, 1)

                def m3(t, u):
                    dve.wait_ge(chain2, 4 * t + 2)
                    v = u % 2
                    nc.vector.tensor_tensor(prob[:, v, :].rearrange("p (h g) -> p h g", h=HEADS),
                                            expd[:, u, :].rearrange("p (h g) -> p h g", h=HEADS),
                                            inv[:, v, :].rearrange("p (h a) -> p h a", a=1).broadcast_to([P, HEADS, HEADS]),
                                            ALU.mult).then_inc(chain2, 1)

                def m4(t, u):
                    dve.wait_ge(chain2, 4 * t + 3)
                    after(dve, mix_done, t)
                    p4 = prob[:, u % 2, :].rearrange("p (h a g) -> p h a g", h=HEADS, a=1).broadcast_to([P, HEADS, DH, HEADS])
                    v4 = qvk[:, u, D:2 * D].rearrange("p (a g d) -> p a d g", a=1, g=HEADS).broadcast_to([P, HEADS, DH, HEADS])
                    nc.vector.tensor_tensor(prod2[:].rearrange("p (h d g) -> p h d g", h=HEADS, d=DH), p4, v4, ALU.mult).then_inc(chain2, 1)

                def m5(t, u):
                    dve.wait_ge(chain2, 4 * t + 4)
                    after(dve, m_ps, t - A + 1)
                    nc.vector.tensor_reduce(mixed[:, u, :], prod2[:].rearrange("p (a g) -> p a g", g=HEADS), AX.X, ALU.add).then_inc(mix_done, 1)

                def result(t, u):
                    dve.wait_ge(o_ps, t + 1)
                    sent(dve, put, t, u)
                    nc.vector.tensor_tensor(y[:, u, :], psO[u % 2][:], hs[:, u, :], ALU.add).then_inc(y_done, 1)
                each_phases(dve, n, [(3, s1), (4, m1), (3, s2), (4, m2), (3, s3), (4, m3), (3, s4), (4, m4), (0, keys), (4, m5), (6, result)], A)

            @block.scalar
            def _(act):
                def index(t, u):
                    sent(act, got, t, u)
                    nc.scalar.copy(gidx[:, u:u + 1], plan.key[:, bass.ds(t, 1)]).then_inc(gidx_ready, 1)

                def mean(t, u):
                    act.wait_ge(kin_done, t + 1)
                    after(act, T_ps, t - A + 1)
                    nc.scalar.mul(kmean[:, u, :], kin[:, u, :], plan.inv[:, bass.ds(t, 1)]).then_inc(kmean_done, 1)

                def turn(t, u):
                    act.wait_ge(T_ps, t + 1)
                    after(act, q_ps, t - 1)
                    nc.scalar.copy(turned[:, u % 2, :], psT[u % 2][:]).then_inc(T_sb, 1)

                def take(t, u):
                    act.wait_ge(q_ps, t + 1)
                    after(act, mix_done, t - A + 1)
                    nc.scalar.copy(qvk[:, u, :], psQ[u % 2][:]).then_inc(q_sb, 1)
                    exps(t, u)

                def exps(t, u):
                    act.wait_ge(score_done, t + 1)
                    after(act, mix_done, t - A + 1)
                    nc.scalar.activation(expd[:, u, :], shifted[:, u % 2, :], ACT.Exp).then_inc(exp_done, 1)

                def turn_mixed(t, u):
                    act.wait_ge(m_ps, t + 1)
                    after(act, o_ps, t - 1)
                    nc.scalar.copy(mixedT[:, u % 2, :], psM[u % 2][:]).then_inc(m_sb, 1)
                    sent(act, put, t, u)
                    nc.scalar.copy(sidx[:, u:u + 1], plan.last[:, bass.ds(t, 1)]).then_inc(sidx_ready, 1)
                each_phases(act, n, [index, mean, turn, take, None, turn_mixed], A)

            @block.tensor
            def _(pe):
                pe.wait_ge(weights, 16 * 8)

                def turn(t, u):
                    v = u % 2
                    pe.wait_ge(kmean_done, t + 1)
                    landed(pe, got, t, u)
                    after(pe, T_sb, t - 1)
                    nc.tensor.transpose(psT[v][:, 0:D], kmean[:, u, :], k.ident[:])
                    nc.tensor.transpose(psT[v][:, D:2 * D], hs[:, u, :], k.ident[:]).then_inc(T_ps, 1)

                def project(t, u):
                    v = u % 2
                    pe.wait_ge(T_sb, t + 1)
                    after(pe, q_sb, t - 1)
                    nc.tensor.matmul(psQ[v][:, 0:2 * D], turned[:, v, D:2 * D], wqv[:], start=True, stop=False, skip_group_check=True)
                    nc.tensor.matmul(psQ[v][:, 2 * D:3 * D], turned[:, v, 0:D], wk[:], start=False, stop=False, skip_group_check=True)
                    nc.tensor.matmul(psQ[v][:], k.ones[0:1, :], bias[:], start=False, stop=True, skip_group_check=True).then_inc(q_ps, 1)

                def turn_mixed(t, u):
                    pe.wait_ge(mix_done, t + 1)
                    after(pe, m_sb, t - 1)
                    nc.tensor.transpose(psM[u % 2][:], mixed[:, u, :], k.ident[:]).then_inc(m_ps, 1)

                def out(t, u):
                    v = u % 2
                    pe.wait_ge(m_sb, t + 1)
                    after(pe, y_done, t - 1)
                    nc.tensor.matmul(psO[v][:], mixedT[:, v, :], wo[:], start=True, stop=False)
                    nc.tensor.matmul(psO[v][:], k.ones[0:1, :], bo[:], start=False, stop=True).then_inc(o_ps, 1)
                each_phases(pe, n, [None, turn, project, None, None, turn_mixed, out], A)


def batch_coefs(nc, dve, act_ready, ch, k, gain, shift, mean, var, std, scale, offset):
    dve.wait_ge(act_ready, 1)
    ch.link(nc.vector.reciprocal(scale[:], std[:]))
    ch.link(nc.vector.tensor_tensor(scale[:], scale[:], gain[:], ALU.mult))
    ch.link(nc.vector.tensor_tensor(offset[:], mean, scale[:], ALU.mult))
    ch.link(nc.vector.tensor_tensor(offset[:], shift[:], offset[:], ALU.subtract))


def node_moments(nc, k, s, Y, g1, be1, scale, offset):
    with Stage(nc, "moments") as st:
        y = st.sb("y", [P, R, J, D])
        sq = st.sb("sq", [P, R, J, D])
        acc = st.sb("acc", [P, J, D])
        acc2 = st.sb("acc2", [P, J, D])
        gain, shift = st.sb("gain", [P, 1]), st.sb("shift", [P, 1])
        mean, second, var, std = (st.sb(x, [P, 1]) for x in ("mean", "second", "var", "std"))
        psS = st.ps("psS", [P, 2])
        weights, zeroed, zeroed2 = st.sem("weights"), st.sem("zeroed"), st.sem("zeroed2")
        yl = [st.sem(f"yl{i}") for i in range(R)]
        added, squared, added2, folded, chain, root, var_done = (
            st.sem(x) for x in ("added", "squared", "added2", "folded", "chain", "root", "var_done"))
        n = s.chunks
        with st.run() as block:

            def live(buf, c, u):
                last = isinstance(c, int) and c == n - 1
                return buf[0:s.tp if last else P, u] if u is not None else buf[0:s.tp if last else P]

            @block.sync
            def _(sp):
                sp.dma_start(gain[:], column(g1)).then_inc(weights, 16)
                sp.dma_start(shift[:], column(be1)).then_inc(weights, 16)

                def load(c, u):
                    after(sp, added, c - R + 1)
                    after(sp, squared, c - R + 1)
                    sp.dma_start(y[:, u], rows(Y, c)).then_inc(yl[u], 16)
                each(sp, n, load, R)

            @block.vector
            def _(dve):
                nc.vector.memset(acc[:], 0.0).then_inc(zeroed, 1)
                dve.wait_ge(zeroed, 1)

                def add(c, u):
                    landed(dve, yl, c, u)
                    nc.vector.tensor_tensor(live(acc, c, None), live(acc, c, None), live(y, c, u), ALU.add).then_inc(added, 1)
                    dve.wait_ge(added, c + 1)
                each(dve, n, add, R)
                ch = Chain(dve, chain, 99)
                dve.wait_ge(folded, 1)
                ch.link(nc.vector.tensor_scalar(mean[:], psS[:, 0:1], 1.0 / s.N, None, ALU.mult))
                ch.link(nc.vector.tensor_scalar(second[:], psS[:, 1:2], 1.0 / s.N, None, ALU.mult))
                ch.link(nc.vector.tensor_tensor(var[:], mean[:], mean[:], ALU.mult))
                nc.vector.tensor_tensor(var[:], second[:], var[:], ALU.subtract).then_inc(var_done, 1)
                dve.wait_ge(weights, 32)
                batch_coefs(nc, dve, root, ch, k, gain, shift, mean[:], var, std, scale, offset)

            @block.scalar
            def _(act):
                def square(c, u):
                    landed(act, yl, c, u)
                    after(act, added2, c - R + 1)
                    nc.scalar.activation(sq[:, u], y[:, u], ACT.Square).then_inc(squared, 1)
                each(act, n, square, R)
                act.wait_ge(var_done, 1)
                nc.scalar.activation(std[:], var[:], ACT.Sqrt, bias=k.eps_col[:]).then_inc(root, 1)

            @block.gpsimd
            def _(pool):
                pool.memset(acc2[:], 0.0).then_inc(zeroed2, 1)
                pool.wait_ge(zeroed2, 1)

                def add(c, u):
                    pool.wait_ge(squared, c + 1)
                    nc.gpsimd.tensor_tensor(live(acc2, c, None), live(acc2, c, None), live(sq, c, u), ALU.add).then_inc(added2, 1)
                    pool.wait_ge(added2, c + 1)
                each(pool, n, add, R)

            @block.tensor
            def _(pe):
                for a, (src, done) in enumerate(((acc, added), (acc2, added2))):
                    pe.wait_ge(done, n)
                    for j in range(J):
                        last = nc.tensor.matmul(psS[:, a:a + 1], src[:, j, :], k.ones[:, 0:1], start=j == 0, stop=j == J - 1)
                last.then_inc(folded, 1)


def node_mlp(nc, k, s, L0, Y, U, scale, offset, scale2, offset2):
    M = HID // P
    with Stage(nc, "mlp") as st:
        y = st.sb("y", [P, R, J, D])
        t = st.sb("t", [P, R, CH])
        g = st.sb("g", [P, 2, M, CH])
        u_sb = st.sb("u", [P, R, CH])
        w1, w2 = st.sb("w1", [P, HID]), st.sb("w2", [P, M, D])
        b1, b2 = st.sb("b1", [P, M]), st.sb("b2", [P, 1])
        gain, shift, std = st.sb("gain", [P, 1]), st.sb("shift", [P, 1]), st.sb("std", [P, 1])
        stats, mv = st.sb("stats", [P, s.chunks, 6]), st.sb("mv", [P, 2])
        psT = [st.ps("psT0", [P, CH])]
        psG = [st.ps(f"psG{i}", [P, CH]) for i in range(M)]
        psU = [st.ps(f"psU{i}", [P, CH]) for i in range(2)]
        weights = st.sem("weights")
        yl = [st.sem(f"yl{i}") for i in range(R)]
        us = [st.sem(f"us{i}") for i in range(R)]
        T_ps, T_sb, G_ps, G_sb, U_ps, U_sb, stat, moments, root, chain = (
            st.sem(x) for x in ("T_ps", "T_sb", "G_ps", "G_sb", "U_ps", "U_sb", "stat", "moments", "root", "chain"))
        n = s.chunks
        with st.run() as block:

            @block.sync
            def _(sp):
                with nc.allow_non_contiguous_dma("biases as columns"):
                    for dst, src in ((w1[:], L0["w1"][:, :]), (w2[:], L0["w2"].rearrange("(m p) d -> p m d", p=P)),
                                     (b1[:], L0["b1"].rearrange("(m p) -> p m", p=P)), (b2[:], column(L0["b2"])),
                                     (gain[:], column(L0["g2"])), (shift[:], column(L0["be2"]))):
                        sp.dma_start(dst, src).then_inc(weights, 16)

                def load(c, u):
                    after(sp, T_ps, c - R + 1)
                    sp.dma_start(y[:, u], rows(Y, c)).then_inc(yl[u], 16)

                def store(c, u):
                    sp.wait_ge(U_sb, c + 1)
                    sp.dma_start(U[bass.ds(c * P, P), :], u_sb[:, u, :]).then_inc(us[u], 16)
                each_phases(sp, n, [load, None, None, store], R)
                all_landed(sp, us, n)

            @block.tensor
            def _(pe):
                pe.wait_ge(weights, 16 * 6)

                def turn(c, u):
                    landed(pe, yl, c, u)
                    after(pe, T_sb, c)
                    for j in range(J):
                        last = nc.tensor.transpose(psT[0][:, j * P:(j + 1) * P], y[:, u, j, :], k.ident[:])
                    last.then_inc(T_ps, 1)

                def up(c, u):
                    pe.wait_ge(T_sb, c + 1)
                    for m in range(M):
                        after(pe, G_sb, M * (c - 1) + m + 1)
                        nc.tensor.matmul(psG[m][:], w1[:, m * P:(m + 1) * P], t[:, u, :], start=True, stop=True).then_inc(G_ps, 1)

                def down(c, u):
                    after(pe, U_sb, c - 1)
                    for m in range(M):
                        pe.wait_ge(G_sb, M * c + m + 1)
                        last = nc.tensor.matmul(psU[u % 2][:], w2[:, m, :], g[:, u % 2, m, :], start=m == 0, stop=m == M - 1)
                    last.then_inc(U_ps, 1)

                def step(c, u):
                    up(c, u)
                    if not (isinstance(c, int) and c == n - 1):
                        turn(c + 1, (u + 1) % R)
                turn(0, 0)
                each_phases(pe, n, [step, down], R)

            @block.scalar
            def _(act):
                act.wait_ge(weights, 16 * 6)

                def turn(c, u):
                    act.wait_ge(T_ps, c + 1)
                    after(act, U_sb, c - R + 1)
                    nc.scalar.activation(t[:, u, :], psT[0][:], ACT.Identity, bias=offset[:], scale=scale[:]).then_inc(T_sb, 1)

                def step(c, u):
                    after(act, U_ps, c - 1)
                    for m in range(M):
                        act.wait_ge(G_ps, M * c + m + 1)
                        nc.scalar.activation(g[:, u % 2, m, :], psG[m][:], ACT.Gelu, bias=b1[:, m:m + 1]).then_inc(G_sb, 1)
                    if not (isinstance(c, int) and c == n - 1):
                        turn(c + 1, (u + 1) % R)
                turn(0, 0)
                each(act, n, step, R)
                act.wait_ge(moments, 1)
                nc.scalar.activation(std[:], mv[:, 1:2], ACT.Sqrt, bias=k.eps_col[:]).then_inc(root, 1)

            @block.vector
            def _(dve):
                dve.wait_ge(weights, 16 * 6)

                def finish(c, u):
                    dve.wait_ge(U_ps, c + 1)
                    sent(dve, us, c, u)
                    nc.vector.scalar_tensor_tensor(u_sb[:, u, :], psU[u % 2][:], b2[:], t[:, u, :], ALU.add, ALU.add).then_inc(U_sb, 1)
                    dve.wait_ge(U_sb, c + 1)
                    out = stats[:].rearrange("p c x -> p (c x)")[:, bass.ds(c * 6, 6)]
                    real = u_sb[:, u, :]
                    if isinstance(c, int) and c == n - 1:
                        real = real.rearrange("f (j p) -> f j p", j=J)[:, :, 0:s.tp]
                    nc.vector.bn_stats(out, real).then_inc(stat, 1)
                each(dve, n, finish, R)
                dve.wait_ge(stat, n)
                nc.vector.bn_aggr(mv[:], stats[:].rearrange("p c x -> p (c x)")).then_inc(moments, 1)
                ch = Chain(dve, chain, 99)
                batch_coefs(nc, dve, root, ch, k, gain, shift, mv[:, 0:1], None, std, scale2, offset2)


def second_norm(nc, k, s, x, U, X, H, scale2, offset2):
    with Stage(nc, "norm1") as st:
        norm = Norm(nc, st, k)
        uin, z = st.sb("uin", [P, R, CH]), st.sb("z", [P, R, CH])
        xin, x1, h = (st.sb(v, [P, R, J, D]) for v in ("xin", "x1", "h"))
        psZ = [st.ps(f"psZ{i}", [P, CH]) for i in range(2)]
        ul, xl, xs, hs = ([st.sem(f"{v}{i}") for i in range(R)] for v in ("ul", "xl", "xs", "hs"))
        z_done, z_ps, x_done, h_done = (st.sem(v) for v in ("z_done", "z_ps", "x_done", "h_done"))
        n = s.chunks
        with st.run() as block:

            @block.sync
            def _(sp):
                def load(c, u):
                    after(sp, z_done, c - R + 1)
                    sp.dma_start(uin[:, u, :], U[bass.ds(c * P, P), :]).then_inc(ul[u], 16)
                    after(sp, x_done, c - R + 1)
                    load_x(nc, sp, s, x, xin[:, u], c, xl[u])

                def store(c, u):
                    sp.wait_ge(x_done, c + 1)
                    sp.dma_start(rows(X, c), x1[:, u]).then_inc(xs[u], 16)
                    sp.wait_ge(h_done, c + 1)
                    sp.dma_start(rows(H, c), h[:, u]).then_inc(hs[u], 16)
                each_phases(sp, n, [load, None, None, store], R)
                all_landed(sp, xs, n)
                all_landed(sp, hs, n)

            @block.scalar
            def _(act):
                def scaled(c, u):
                    landed(act, ul, c, u)
                    after(act, z_ps, c - R + 1)
                    nc.scalar.activation(z[:, u, :], uin[:, u, :], ACT.Identity, bias=offset2[:], scale=scale2[:]).then_inc(z_done, 1)

                def normed(c, u):
                    norm.act_root(act, c, u)
                    sent(act, hs, c, u)
                    norm.act_apply(act, h[:, u], x1[:, u], c, u).then_inc(h_done, 1)
                each_phases(act, n, [scaled, None, normed], R)

            @block.tensor
            def _(pe):
                def turn(c, u):
                    pe.wait_ge(z_done, c + 1)
                    after(pe, x_done, c - 1)
                    for j in range(J):
                        last = nc.tensor.transpose(psZ[u % 2][:, j * D:(j + 1) * D], z[:, u, j * P:(j + 1) * P], k.ident[:])
                    last.then_inc(z_ps, 1)
                each_phases(pe, n, [None, turn], R)

            @block.vector
            def _(dve):
                def add(c, u):
                    if isinstance(c, int) and c == n - 1:
                        dve.wait_ge(xl[u], 16 * (c // R + 2))
                    else:
                        landed(dve, xl, c, u)
                    dve.wait_ge(z_ps, c + 1)
                    sent(dve, xs, c, u)
                    after(dve, h_done, c - R + 1)
                    flat = x1[:, u].rearrange("p j d -> p (j d)")
                    nc.vector.tensor_tensor(flat, psZ[u % 2][:], xin[:, u].rearrange("p j d -> p (j d)"), ALU.add).then_inc(x_done, 1)
                    dve.wait_ge(x_done, c + 1)
                    norm.dve_moments(dve, x1[:, u], c, u)
                    norm.dve_coefs(dve, c, u, lambda: after(dve, h_done, c - R + 1))
                each_phases(dve, n, [None, add], R)


def gather_rows(pool, dst, table, idx, bound, sem):
    pool.indirect_dma_start(out=dst, out_offset=None, in_=table,
                            in_offset=bass.IndirectOffsetOnAxis(ap=idx, axis=0),
                            bounds_check=bound, oob_is_err=False).then_inc(sem, 16)


def scatter_rows(pool, table, src, idx, bound, sem):
    pool.indirect_dma_start(out=table, out_offset=bass.IndirectOffsetOnAxis(ap=idx, axis=0),
                            in_=src, in_offset=None, bounds_check=bound, oob_is_err=False).then_inc(sem, 16)


def edge_messages(nc, k, s, plan, L1, H, edges, carry):
    with Stage(nc, "edge1") as st:
        got_rows = st.sb("rows", [P, 2, 2, J, D])
        idx = st.sb("idx", [P, 2, 2, J], U32)
        turned = st.sb("turned", [P, 2, 2, CH])
        m = st.sb("m", [P, 2, CH])
        ws, wd, b = st.sb("ws", [P, D]), st.sb("wd", [P, D]), st.sb("b", [P, 1])
        psS = [st.ps(f"psS{i}", [P, CH]) for i in range(2)]
        psD = [st.ps(f"psD{i}", [P, CH]) for i in range(2)]
        psM = [st.ps(f"psM{i}", [P, CH]) for i in range(2)]
        psR = [st.ps(f"psR{i}", [P, CH]) for i in range(2)]
        got = [st.sem(f"got{i}") for i in range(2)]
        weights, idx_ready, tick, T_ps, S_sb, D_sb, M_ps, M_sb, R_ps, chain, zeroed, carried, taken = (
            st.sem(v) for v in ("weights", "idx_ready", "tick", "T_ps", "S_sb", "D_sb", "M_ps", "M_sb", "R_ps",
                                "chain", "zeroed", "carried", "taken"))
        n = s.echunks
        with st.run() as block:

            @block.sync
            def _(sp):
                sp.dma_start(ws[:], L1["W_edge"][0:D, :]).then_inc(weights, 16)
                sp.dma_start(wd[:], L1["W_edge"][D:2 * D, :]).then_inc(weights, 16)
                sp.dma_start(b[:], column(L1["b_edge"])).then_inc(weights, 16)

            @block.gpsimd
            def _(pool):
                bound = pool.to_reg(s.N - 1)

                def gather(c, u):
                    pool.wait_ge(idx_ready, c + 1)
                    after(pool, T_ps, c - 1)
                    pool.sem_inc(tick, 1)
                    for side in range(2):
                        for q in range(J):
                            gather_rows(pool, got_rows[:, u, side, q, :], H, idx[:, u, side, q:q + 1], bound, got[u])
                each(pool, n, gather)

            @block.scalar
            def _(act):
                act.wait_ge(weights, 48)

                def index(c, u):
                    sent(act, got, c, u, 2 * J)
                    nc.scalar.copy(idx[:, u, 0, :], plan.other[:, bass.ds(c * J, J)])
                    nc.scalar.copy(idx[:, u, 1, :], plan.key[:, bass.ds(c * J, J)]).then_inc(idx_ready, 1)

                def take(c, u):
                    act.wait_ge(T_ps, c + 1)
                    after(act, M_ps, c - 1)
                    nc.scalar.copy(turned[:, u, 0, :], psS[u][:]).then_inc(S_sb, 1)

                def relu(c, u):
                    act.wait_ge(M_ps, c + 1)
                    after(act, R_ps, c - 1)
                    nc.scalar.activation(m[:, u, :], psM[u][:], ACT.Relu, bias=b[:]).then_inc(M_sb, 1)
                each_phases(act, n, [index, take, relu])

            @block.vector
            def _(dve):
                ch = Chain(dve, chain, J)
                nc.vector.memset(edges[:, 0:D], 0.0).then_inc(zeroed, 1)
                dve.wait_ge(zeroed, 1)

                def take(c, u):
                    dve.wait_ge(T_ps, c + 1)
                    after(dve, M_ps, c - 1)
                    nc.vector.tensor_copy(turned[:, u, 1, :], psD[u][:]).then_inc(D_sb, 1)

                def add(c, u):
                    dve.wait_ge(R_ps, c + 1)
                    ch.step(c)
                    for q in range(J):
                        ch.link(nc.vector.scalar_tensor_tensor(
                            edges[:, bass.ds((c * J + q + 1) * D, D)], edges[:, bass.ds((c * J + q) * D, D)],
                            plan.same[:, bass.ds(c * J + q, 1)], psR[u][:, q * D:(q + 1) * D], ALU.mult, ALU.add))
                each_phases(dve, n, [None, take, None, add])
                dve.wait_ge(carried, 1)
                nc.vector.tensor_copy(carry[:], psM[0][:, 0:D]).then_inc(taken, 1)
                dve.wait_ge(taken, 1)

            @block.tensor
            def _(pe):
                pe.wait_ge(weights, 48)

                def turn(c, u):
                    landed(pe, got, c, u, 2 * J)
                    after(pe, S_sb, c - 1)
                    after(pe, D_sb, c - 1)
                    for side, ps in ((0, psS), (1, psD)):
                        for q in range(J):
                            last = nc.tensor.transpose(ps[u][:, q * P:(q + 1) * P], got_rows[:, u, side, q, :], k.ident[:])
                    last.then_inc(T_ps, 1)

                def mix(c, u):
                    pe.wait_ge(S_sb, c + 1)
                    pe.wait_ge(D_sb, c + 1)
                    after(pe, M_sb, c - 1)
                    nc.tensor.matmul(psM[u][:], ws[:], turned[:, u, 0, :], start=True, stop=False)
                    nc.tensor.matmul(psM[u][:], wd[:], turned[:, u, 1, :], start=False, stop=True).then_inc(M_ps, 1)

                def back(c, u):
                    pe.wait_ge(M_sb, c + 1)
                    after(pe, chain, (c - 1) * J)
                    for q in range(J):
                        last = nc.tensor.transpose(psR[u][:, q * D:(q + 1) * D], m[:, u, q * P:(q + 1) * P], k.ident[:])
                    last.then_inc(R_ps, 1)
                each_phases(pe, n, [None, turn, mix, back])
                pe.wait_ge(chain, n * J)
                nc.tensor.matmul(psM[0][:, 0:D], plan.carry[:], edges[:, s.T * D:], start=True, stop=True).then_inc(carried, 1)


def scatter_sums(nc, s, plan, S, edges, carry, name):
    with Stage(nc, name) as st:
        y, idx = st.sb("y", [P, R, D]), st.sb("idx", [P, R], U32)
        put = [st.sem(f"put{i}") for i in range(R)]
        y_done, idx_ready, tick = st.sem("y_done"), st.sem("idx_ready"), st.sem("tick")
        n = s.T
        with st.run() as block:

            @block.vector
            def _(dve):
                def total(t, u):
                    sent(dve, put, t, u)
                    nc.vector.scalar_tensor_tensor(y[:, u, :], carry[:], plan.first[:, bass.ds(t, 1)],
                                                   edges[:, bass.ds((t + 1) * D, D)], ALU.mult, ALU.add).then_inc(y_done, 1)
                each(dve, n, total, R)

            @block.scalar
            def _(act):
                def index(t, u):
                    sent(act, put, t, u)
                    nc.scalar.copy(idx[:, u:u + 1], plan.last[:, bass.ds(t, 1)]).then_inc(idx_ready, 1)
                each(act, n, index, R)

            @block.gpsimd
            def _(pool):
                bound = pool.to_reg(s.N - 1)

                def scatter(t, u):
                    pool.wait_ge(idx_ready, t + 1)
                    pool.wait_ge(y_done, t + 1)
                    pool.sem_inc(tick, 1)
                    scatter_rows(pool, S, y[:, u, :], idx[:, u:u + 1], bound, put[u])
                each(pool, n, scatter, R)
                all_landed(pool, put, n)


def node_update(nc, k, s, L1, X, H, S):
    with Stage(nc, "node1") as st:
        norm = Norm(nc, st, k)
        xin, hin, sin, rst, x2, h2 = (st.sb(v, [P, R, J, D]) for v in ("xin", "hin", "sin", "rst", "x2", "h2"))
        rT, a_sb = st.sb("rT", [P, R, CH]), st.sb("a", [P, R, CH])
        w1, w2, b1 = st.sb("w1", [P, D]), st.sb("w2", [P, D]), st.sb("b1", [P, 1])
        bias, eps1 = st.sb("bias", [1, J, D]), st.sb("eps1", [P, 1])
        psT = [st.ps(f"psT{i}", [P, CH]) for i in range(2)]
        psA = [st.ps(f"psA{i}", [P, CH]) for i in range(2)]
        psB = [st.ps(f"psB{i}", [P, CH]) for i in range(2)]
        xl, hl, xs, hs = ([st.sem(f"{v}{i}") for i in range(R)] for v in ("xl", "hl", "xs", "hs"))
        weights, eps_done, r_done, T_ps, T_sb, A_ps, A_sb, B_ps, x_done, h_done = (
            st.sem(v) for v in ("weights", "eps_done", "r_done", "T_ps", "T_sb", "A_ps", "A_sb", "B_ps", "x_done", "h_done"))
        n = s.chunks
        with st.run() as block:

            @block.sync
            def _(sp):
                for j in range(J):
                    sp.dma_start(bias[:, j, :], row(L1["b2"])).then_inc(weights, 16)
                sp.dma_start(w1[:], L1["W1"][:, :]).then_inc(weights, 16)
                sp.dma_start(w2[:], L1["W2"][:, :]).then_inc(weights, 16)
                sp.dma_start(b1[:], column(L1["b1"])).then_inc(weights, 16)
                sp.dma_start(eps1[:], L1["eps"].rearrange("(a b) -> a b", a=1).broadcast_to([P, 1])).then_inc(weights, 16)

                def load(c, u):
                    after(sp, r_done, c - R + 1)
                    sp.dma_start(hin[:, u], rows(H, c)).then_inc(hl[u], 16)
                    sp.dma_start(sin[:, u], rows(S, c)).then_inc(hl[u], 16)

                def load2(c, u):
                    after(sp, x_done, c - R + 1)
                    sp.dma_start(xin[:, u], rows(X, c)).then_inc(xl[u], 16)

                def store(c, u):
                    sp.wait_ge(x_done, c + 1)
                    sp.dma_start(rows(X, c), x2[:, u]).then_inc(xs[u], 16)
                    sp.wait_ge(h_done, c + 1)
                    sp.dma_start(rows(H, c), h2[:, u]).then_inc(hs[u], 16)
                each_phases(sp, n, [load, load2, (6, store)], R)
                all_landed(sp, xs, n)
                all_landed(sp, hs, n)

            @block.vector
            def _(dve):
                dve.wait_ge(weights, 16 * (J + 4))
                nc.vector.tensor_scalar(eps1[:], eps1[:], 1.0, None, ALU.add).then_inc(eps_done, 1)
                dve.wait_ge(eps_done, 1)

                def rest(c, u):
                    landed(dve, hl, c, u, 2)
                    after(dve, T_ps, c - R + 1)
                    nc.vector.scalar_tensor_tensor(rst[:, u], hin[:, u], eps1[:], sin[:, u], ALU.mult, ALU.add).then_inc(r_done, 1)

                def finish(c, u):
                    dve.wait_ge(B_ps, c + 1)
                    landed(dve, xl, c, u)
                    sent(dve, xs, c, u)
                    after(dve, h_done, c - R + 1)
                    nc.vector.tensor_tensor(x2[:, u].rearrange("p j d -> p (j d)"), psB[u % 2][:],
                                            xin[:, u].rearrange("p j d -> p (j d)"), ALU.add).then_inc(x_done, 1)
                    dve.wait_ge(x_done, c + 1)
                    norm.dve_moments(dve, x2[:, u], c, u)

                def coefs(c, u):
                    norm.dve_coefs(dve, c, u, lambda: after(dve, h_done, c - R + 1))
                each_phases(dve, n, [rest, (4, coefs), (3, finish)], R)

            @block.scalar
            def _(act):
                act.wait_ge(weights, 16 * (J + 4))

                def take(c, u):
                    act.wait_ge(T_ps, c + 1)
                    after(act, A_ps, c - R + 1)
                    nc.scalar.copy(rT[:, u, :], psT[u % 2][:]).then_inc(T_sb, 1)

                def relu(c, u):
                    act.wait_ge(A_ps, c + 1)
                    after(act, B_ps, c - R + 1)
                    nc.scalar.activation(a_sb[:, u, :], psA[u % 2][:], ACT.Relu, bias=b1[:]).then_inc(A_sb, 1)

                def root(c, u):
                    norm.act_root(act, c, u)

                def apply(c, u):
                    sent(act, hs, c, u)
                    norm.act_apply(act, h2[:, u], x2[:, u], c, u).then_inc(h_done, 1)
                each_phases(act, n, [take, relu, (4, apply), (3, root)], R)

            @block.tensor
            def _(pe):
                pe.wait_ge(weights, 16 * (J + 4))

                def turn(c, u):
                    pe.wait_ge(r_done, c + 1)
                    after(pe, T_sb, c - 1)
                    for j in range(J):
                        last = nc.tensor.transpose(psT[u % 2][:, j * P:(j + 1) * P], rst[:, u, j, :], k.ident[:])
                    last.then_inc(T_ps, 1)

                def up(c, u):
                    pe.wait_ge(T_sb, c + 1)
                    after(pe, A_sb, c - 1)
                    nc.tensor.matmul(psA[u % 2][:], w1[:], rT[:, u, :], start=True, stop=True).then_inc(A_ps, 1)

                def down(c, u):
                    pe.wait_ge(A_sb, c + 1)
                    after(pe, x_done, c - 1)
                    rows_product(nc, psB[u % 2], a_sb[:, u], w2, bias[:].rearrange("a j d -> a (j d)"), k).then_inc(B_ps, 1)
                each_phases(pe, n, [turn, up, down], R)


def hyperbolic_messages(nc, k, s, plan, H, edges, norms, own):
    with Stage(nc, "mobius") as st:
        got_rows = st.sb("rows", [P, R, 2, J, D])
        idx = st.sb("idx", [P, R, 2, J], U32)
        sq, dot = st.sb("sq", [P, R, 2, J]), st.sb("dot", [P, R, J])
        c1, al, den, be = (st.sb(v, [P, R, J]) for v in ("c1", "al", "den", "be"))
        scaled = st.sb("scaled", [P, R, J, D])
        junk, junk2, junk3 = st.sb("junk", [P, J, D]), st.sb("junk2", [P, 2, J, D]), st.sb("junk3", [P, J, D])
        got = [st.sem(f"got{i}") for i in range(R)]
        idx_ready, tick, sq_done, dot_done, chain, coef, tmp_done, m_done, norm_done = (
            st.sem(v) for v in ("idx_ready", "tick", "sq_done", "dot_done", "chain", "coef", "tmp_done", "m_done", "norm_done"))
        kept = [st.sem(f"kept{i}") for i in range(R)]
        n = s.echunks
        with st.run() as block:

            @block.sync
            def _(sp):
                def keep(c, u):
                    landed(sp, got, c, u, 2 * J)
                    sp.dma_start(rows(own, c), got_rows[:, u, 1]).then_inc(kept[u], 16)
                each(sp, n, keep, R)
                all_landed(sp, kept, n)

            @block.gpsimd
            def _(pool):
                bound = pool.to_reg(s.N - 1)

                def gather(c, u):
                    pool.wait_ge(idx_ready, c + 1)
                    after(pool, m_done, c - R + 1)
                    sent(pool, kept, c, u)
                    pool.sem_inc(tick, 1)
                    for side in range(2):
                        for q in range(J):
                            gather_rows(pool, got_rows[:, u, side, q, :], H, idx[:, u, side, q:q + 1], bound, got[u])
                each(pool, n, gather, R)

            @block.scalar
            def _(act):
                def index(c, u):
                    sent(act, got, c, u, 2 * J)
                    nc.scalar.copy(idx[:, u, 0, :], plan.other[:, bass.ds(c * J, J)])
                    nc.scalar.copy(idx[:, u, 1, :], plan.key[:, bass.ds(c * J, J)]).then_inc(idx_ready, 1)

                def squares(c, u):
                    landed(act, got, c, u, 2 * J)
                    after(act, coef, c - R + 1)
                    after(act, sq_done, c)
                    for side in range(2):
                        for q in range(J):
                            last = nc.scalar.activation(junk2[:, side, q, :], got_rows[:, u, side, q, :], ACT.Square,
                                                        accum_out=sq[:, u, side, q:q + 1])
                    last.then_inc(sq_done, 1)

                def scale(c, u):
                    act.wait_ge(coef, c + 1)
                    after(act, m_done, c - R + 1)
                    for q in range(J):
                        last = nc.scalar.mul(scaled[:, u, q, :], got_rows[:, u, 1, q, :], be[:, u, q:q + 1])
                    last.then_inc(tmp_done, 1)

                def norm(c, u):
                    act.wait_ge(m_done, c + 1)
                    after(act, norm_done, c)
                    for q in range(J):
                        last = nc.scalar.activation(junk3[:, q, :], edges[:, bass.ds((c * J + q + 1) * D, D)], ACT.Square,
                                                    accum_out=norms[:, bass.ds(c * J + q, 1)])
                    last.then_inc(norm_done, 1)

                def late(c, u):
                    scale(c, u)
                    norm(c, u)
                each_phases(act, n, [index, None, None, squares, late], R)

            @block.vector
            def _(dve):
                ch = Chain(dve, chain, 6)

                def coefs(c, u):
                    landed(dve, got, c, u, 2 * J)
                    after(dve, dot_done, c)
                    for q in range(J):
                        last = nc.vector.scalar_tensor_tensor(junk[:, q, :], got_rows[:, u, 0, q, :], 1.0, got_rows[:, u, 1, q, :],
                                                              ALU.mult, ALU.mult, accum_out=dot[:, u, q:q + 1])
                    last.then_inc(dot_done, 1)
                    dve.wait_ge(dot_done, c + 1)
                    dve.wait_ge(sq_done, c + 1)
                    after(dve, tmp_done, c - R + 1)
                    after(dve, m_done, c - R + 1)
                    x2, y2 = sq[:, u, 0, :], sq[:, u, 1, :]
                    ch.step(c)
                    nc.vector.tensor_scalar(c1[:, u], dot[:, u], -2.0, 1.0, ALU.mult, ALU.add)
                    ch.link(nc.vector.tensor_tensor(den[:, u], x2, y2, ALU.mult))
                    nc.vector.tensor_tensor(al[:, u], c1[:, u], y2, ALU.add)
                    ch.link(nc.vector.tensor_tensor(den[:, u], den[:, u], c1[:, u], ALU.add))
                    ch.link(nc.vector.tensor_scalar(den[:, u], den[:, u], HYP_EPS, None, ALU.max))
                    ch.link(nc.vector.reciprocal(den[:, u], den[:, u]))
                    ch.link(nc.vector.tensor_tensor(al[:, u], al[:, u], den[:, u], ALU.mult))
                    nc.vector.scalar_tensor_tensor(be[:, u], x2, -1.0, den[:, u], ALU.add, ALU.mult).then_inc(coef, 1)
                    ch.link(nc.vector.tensor_copy(c1[:, u], c1[:, u]))

                def finish(c, u):
                    dve.wait_ge(tmp_done, c + 1)
                    for q in range(J):
                        last = nc.vector.scalar_tensor_tensor(edges[:, bass.ds((c * J + q + 1) * D, D)], got_rows[:, u, 0, q, :],
                                                              al[:, u, q:q + 1], scaled[:, u, q, :], ALU.mult, ALU.add)
                    last.then_inc(m_done, 1)
                each_phases(dve, n, [coefs, finish], R)


class FoldScratch:
    def __init__(self, st):
        self.junk, self.scaled = st.sb("junk", [P, V, D]), st.sb("scaled", [P, V, D])
        self.dot, self.a1, self.x2, self.sum, self.al, self.be, self.prod = (
            st.sb(v, [P, V]) for v in ("dot", "a1", "x2", "sum", "al", "be", "prod"))
        self.den, self.cut, self.inv, self.al2, self.be2 = (st.sb(v, [P, V]) for v in ("den", "cut", "inv", "al2", "be2"))


def fold_step(nc, b, plan, norms, t, state, m, out, q, link, q_ready):
    def lanes(x):
        return x[:].rearrange("p (v t) -> p v t", v=V)[:, :, bass.ds(t, 1)].rearrange("p v t -> p (v t)")
    same, m2 = lanes(plan.same), lanes(norms)
    steps = plan.same.shape[1] // V
    for v in range(V):
        last = nc.vector.scalar_tensor_tensor(b.junk[:, v, :], m(v), plan.same[:, bass.ds(v * steps + t, 1)], state(v),
                                              ALU.mult, ALU.mult, accum_out=b.dot[:, v:v + 1])
    q_ready()
    link(nc.vector.tensor_tensor(b.x2[:], q, same, ALU.mult))
    nc.vector.tensor_scalar(b.a1[:], b.dot[:], 2.0, 1.0, ALU.mult, ALU.add)
    nc.vector.tensor_scalar(b.be[:], b.x2[:], -1.0, 1.0, ALU.mult, ALU.add)
    link(nc.vector.tensor_tensor(b.prod[:], b.x2[:], m2, ALU.mult))
    nc.vector.tensor_tensor(b.sum[:], b.a1[:], m2, ALU.add)
    link(nc.vector.tensor_tensor(b.den[:], b.prod[:], b.a1[:], ALU.add))
    nc.vector.tensor_tensor(b.al[:], b.sum[:], same, ALU.mult)
    link(nc.vector.tensor_scalar(b.cut[:], b.den[:], HYP_EPS, None, ALU.max))
    link(nc.vector.reciprocal(b.inv[:], b.cut[:]))
    nc.vector.tensor_tensor(b.al2[:], b.al[:], b.inv[:], ALU.mult)
    link(nc.vector.tensor_tensor(b.be2[:], b.be[:], b.inv[:], ALU.mult))
    for v in range(V):
        last = nc.vector.tensor_scalar(b.scaled[:, v, :], m(v), b.be2[:, v:v + 1], None, ALU.mult)
    link(last)
    for v in range(V):
        last = nc.vector.scalar_tensor_tensor(out(v), state(v), b.al2[:, v:v + 1], b.scaled[:, v, :], ALU.mult, ALU.add)
    return last


FOLD_LINKS = 7


def hyperbolic_fold(nc, k, s, plan, edges, norms, lengths, attr, attr_sorted):
    with Stage(nc, "fold") as st:
        state = st.sb("state", [P, 2, V, D])
        final, start = st.sb("final", [P, V, D]), st.sb("start", [P, V, D])
        flag = st.sb("flag", [P, 1], I32)
        q = st.sb("q", [P, 2, V])
        qjunk = st.sb("qjunk", [P, V, D])
        b = FoldScratch(st)
        attr_rows, attr_idx = st.sb("attr_rows", [P, 2, V, NG]), st.sb("attr_idx", [P, 2, V], U32)
        attr_got, attr_kept = ([st.sem(f"{x}{i}") for i in range(2)] for x in ("attr_got", "attr_kept"))
        attr_cleared, attr_indexed = st.sem("attr_cleared"), st.sem("attr_indexed")
        psC, psF = st.ps("psC", [P, D]), st.ps("psF", [P, 1])
        tick = st.sem("tick")
        (zeroed, flagged, flag_done, s1_chain, s1_state, s1_q, slow_chain, slow_state, slow_moved, state_done, moved,
         start_done, s2_chain, s2_state, s2_q) = (
            st.sem(v) for v in ("zeroed", "flagged", "flag_done", "s1_chain", "s1_state", "s1_q", "slow_chain", "slow_state",
                                "slow_moved", "state_done", "moved", "start_done", "s2_chain", "s2_state", "s2_q"))
        n = s.T // V
        rounds = V * P - 2
        per = FOLD_LINKS
        assert n % 2 == 0

        def column_at(v, t):
            return edges[:, bass.ds((v * n + t) * D, D)]

        def lengths_at(t):
            return lengths[:].rearrange("p (v t) -> p v t", v=V)[:, :, bass.ds(t - 1, 1)].rearrange("p v t -> p (v t)")

        def message(t):
            return lambda v: column_at(v, t + 1)

        def state_in(u):
            return lambda v: state[:, u, v, :]

        def hand_on(to, done):
            nc.vector.tensor_copy(to[:, 1:V, :], final[:, 0:V - 1, :])
            nc.vector.tensor_scalar(to[:, 0, :], psC[:], plan.cont[:], None, ALU.mult).then_inc(done, 1)

        with st.run() as block:

            @block.gpsimd
            def _(pool):
                bound = pool.to_reg(s.E - 1)
                pool.memset(attr_rows[:], 0.0).then_inc(attr_cleared, 1)
                pool.wait_ge(attr_cleared, 1)

                def gather(t, u):
                    pool.wait_ge(attr_indexed, t + 1)
                    sent(pool, attr_kept, t, u)
                    pool.sem_inc(tick, 1)
                    for v in range(V):
                        gather_rows(pool, attr_rows[:, u, v, :], attr, attr_idx[:, u, v:v + 1], bound, attr_got[u])
                each(pool, n, gather)

            @block.sync
            def _(sp):
                def keep(t, u):
                    landed(sp, attr_got, t, u, V)
                    sp.dma_start(attr_sorted[bass.ds(t * P, P), :].rearrange("p (v g) -> p v g", v=V),
                                 attr_rows[:, u]).then_inc(attr_kept[u], 16)
                each(sp, n, keep)
                all_landed(sp, attr_kept, n)

            @block.vector
            def _(dve):
                dve.wait_ge(flagged, 1)
                nc.vector.tensor_copy(flag[:], psF[:]).then_inc(flag_done, 1)
                nc.vector.memset(state[:], 0.0).then_inc(zeroed, 1)
                dve.wait_ge(zeroed, 1)
                dve.wait_ge(flag_done, 1)
                ch = Chain(dve, s1_chain, per)

                def first_sweep(t, u):
                    ch.step(t)
                    last = fold_step(nc, b, plan, norms, t, state_in(u), message(t), state_in(1 - u), q[:, u, :],
                                     ch.link, lambda: dve.wait_ge(s1_q, t + 1))
                    last.then_inc(s1_state, 1)
                    dve.wait_ge(s1_state, t + 1)
                each(dve, n, first_sweep)

                crossing = dve.value_load(flag[0:1, 0:1], min_val=0, max_val=P * V)
                nc.vector.tensor_copy(final[:], state[:, 0]).then_inc(state_done, 1)
                dve.wait_ge(state_done, 1)
                with dve.If(crossing > 0):
                    dve.sem_inc(slow_state, 1)
                    with dve.Fori(0, rounds) as r:
                        dve.wait_ge(slow_moved, r + 1)
                        hand_on(state[:, 0], slow_chain)
                        dve.wait_ge(slow_chain, r * ((per + 2) * n + 1) + 1)
                        dve.sem_inc(tick, 1)
                        with dve.Fori(0, n // 2) as i:
                            for u in range(2):
                                count = [0]

                                def link(ins, u=u):
                                    ins.then_inc(slow_chain, 1)
                                    count[0] += 1
                                    dve.wait_ge(slow_chain, r * ((per + 2) * n + 1) + 1 + (i * 2 + u) * (per + 2) + count[0])
                                for v in range(V):
                                    last = nc.vector.scalar_tensor_tensor(b.junk[:, v, :], state[:, u, v, :], 1.0, state[:, u, v, :],
                                                                          ALU.mult, ALU.mult, accum_out=q[:, u, v:v + 1])
                                link(last)
                                link(fold_step(nc, b, plan, norms, i * 2 + u, state_in(u), message(i * 2 + u), state_in(1 - u),
                                               q[:, u, :], link, lambda: None))
                                assert count[0] == per + 2
                        nc.vector.tensor_copy(final[:], state[:, 0]).then_inc(slow_state, 1)
                        dve.wait_ge(slow_state, r + 2)
                dve.sem_inc(state_done, 1)

                dve.wait_ge(moved, 1)
                hand_on(start, start_done)
                dve.wait_ge(start_done, 1)
                ch2 = Chain(dve, s2_chain, per)

                def last_sweep(t, u):
                    ch2.step(t)
                    before = (lambda v: start[:, v, :]) if isinstance(t, int) and t == 0 else (lambda v: column_at(v, t))
                    last = fold_step(nc, b, plan, norms, t, before, message(t), message(t),
                                     q[:, 0, :] if isinstance(t, int) and t == 0 else lengths_at(t),
                                     ch2.link, lambda: dve.wait_ge(s2_q, t + 1))
                    last.then_inc(s2_state, 1)
                    dve.wait_ge(s2_state, t + 1)
                each(dve, n, last_sweep)

            @block.scalar
            def _(act):
                def first_sweep(t, u):
                    if isinstance(t, int) and t == 0:
                        act.wait_ge(zeroed, 1)
                    else:
                        act.wait_ge(s1_state, t)
                    after(act, s1_q, t)
                    for v in range(V):
                        last = nc.scalar.activation(qjunk[:, v, :], state[:, u, v, :], ACT.Square, accum_out=q[:, u, v:v + 1])
                    last.then_inc(s1_q, 1)
                    sent(act, attr_got, t, u, V)
                    nc.scalar.copy(attr_idx[:, u, :], plan.edge[:, bass.ds(t * V, V)]).then_inc(attr_indexed, 1)
                each(act, n, first_sweep)
                act.wait_ge(start_done, 1)

                def last_sweep(t, u):
                    first = isinstance(t, int) and t == 0
                    if not first:
                        act.wait_ge(s2_state, t)
                        act.wait_ge(s2_q, t)
                    for v in range(V):
                        last = nc.scalar.activation(qjunk[:, v, :], start[:, v, :] if first else column_at(v, t), ACT.Square,
                                                    accum_out=q[:, 0, v:v + 1] if first else lengths[:, bass.ds(v * n + t - 1, 1)])
                    last.then_inc(s2_q, 1)
                each(act, n + 1, last_sweep)
                act.wait_ge(s2_q, n + 1)

            @block.tensor
            def _(pe):
                nc.tensor.matmul(psF[:], k.ones[:], plan.through[:], start=True, stop=True).then_inc(flagged, 1)
                pe.wait_ge(flag_done, 1)
                crossing = pe.value_load(flag[0:1, 0:1], min_val=0, max_val=P * V)
                pe.wait_ge(s1_state, n)
                with pe.If(crossing > 0):
                    with pe.Fori(0, rounds) as r:
                        pe.wait_ge(slow_state, r + 1)
                        nc.tensor.matmul(psC[:], k.shift[:], final[:, V - 1, :], start=True, stop=True).then_inc(slow_moved, 1)
                pe.wait_ge(state_done, 2)
                nc.tensor.matmul(psC[:], k.shift[:], final[:, V - 1, :], start=True, stop=True).then_inc(moved, 1)


def hyperbolic_results(nc, k, s, plan, H, edges, lengths, own):
    T = s.T
    with Stage(nc, "aggregate") as st:
        rows_in = st.sb("rows", [P, R, J, D])
        res = st.sb("res", [P, R, J, D])
        scaled = st.sb("scaled", [P, R, J, D])
        junk2, junk3 = st.sb("junk2", [P, J, D]), st.sb("junk3", [P, J, D])
        idx = st.sb("idx", [P, R, J], U32)
        nrm, cut, low, lg, th, factor, alive, y2 = (
            st.sb(v, [P, T]) for v in ("nrm", "cut", "low", "lg", "th", "factor", "alive", "y2"))
        x2, dot = st.sb("x2", [P, R, J]), st.sb("dot", [P, R, J])
        c1, al, den, be, xy = (st.sb(v, [P, R, J]) for v in ("c1", "al", "den", "be", "xy"))
        got = [st.sem(f"got{i}") for i in range(R)]
        put = [st.sem(f"put{i}") for i in range(R)]
        root, ratio, logged, argd, thd, prep, batch = (
            st.sem(v) for v in ("root", "ratio", "logged", "argd", "thd", "prep", "batch"))
        idx_ready, tick, sq_done, dot_done, chain, coef, tmp_done, res_done = (
            st.sem(v) for v in ("idx_ready", "tick", "sq_done", "dot_done", "chain", "coef", "tmp_done", "res_done"))
        n = s.echunks
        with st.run() as block:

            @block.sync
            def _(sp):
                def load(c, u):
                    after(sp, res_done, c - R + 1)
                    sp.dma_start(rows_in[:, u], rows(own, c)).then_inc(got[u], 16)
                each(sp, n, load, R)

            @block.gpsimd
            def _(pool):
                bound = pool.to_reg(s.N - 1)
                def scatter(c, u):
                    pool.wait_ge(idx_ready, c + 1)
                    pool.wait_ge(res_done, c + 1)
                    pool.sem_inc(tick, 1)
                    for q in range(J):
                        scatter_rows(pool, H, res[:, u, q, :], idx[:, u, q:q + 1], bound, put[u])
                each(pool, n, scatter, R)
                all_landed(pool, put, n, J)

            @block.scalar
            def _(act):
                act.wait_ge(prep, 1)
                nc.scalar.activation(nrm[:], cut[:], ACT.Sqrt).then_inc(root, 1)
                act.wait_ge(ratio, 1)
                nc.scalar.activation(lg[:], low[:], ACT.Ln).then_inc(logged, 1)
                act.wait_ge(argd, 1)
                nc.scalar.activation(th[:], lg[:], ACT.Tanh).then_inc(thd, 1)

                def index(c, u):
                    sent(act, put, c, u, J)
                    nc.scalar.copy(idx[:, u, :], plan.last[:, bass.ds(c * J, J)]).then_inc(idx_ready, 1)

                def squares(c, u):
                    landed(act, got, c, u)
                    after(act, coef, c - R + 1)
                    after(act, sq_done, c)
                    for q in range(J):
                        last = nc.scalar.activation(junk2[:, q, :], rows_in[:, u, q, :], ACT.Square, accum_out=x2[:, u, q:q + 1])
                    last.then_inc(sq_done, 1)

                def scale(c, u):
                    act.wait_ge(coef, c + 1)
                    after(act, res_done, c - R + 1)
                    for q in range(J):
                        last = nc.scalar.mul(scaled[:, u, q, :], rows_in[:, u, q, :], al[:, u, q:q + 1])
                    last.then_inc(tmp_done, 1)
                each_phases(act, n, [squares, scale, index], R)

            @block.vector
            def _(dve):
                ch = Chain(dve, batch, 99)
                nc.vector.tensor_scalar(cut[:], lengths[:], 1e-30, None, ALU.max).then_inc(prep, 1)
                dve.wait_ge(root, 1)
                ch.link(nc.vector.tensor_scalar(alive[:], nrm[:], HYP_EPS, None, ALU.is_gt))
                ch.link(nc.vector.tensor_scalar(cut[:], nrm[:], HYP_EPS, 1.0 - HYP_EPS, ALU.max, ALU.min))
                ch.link(nc.vector.tensor_scalar(low[:], cut[:], -1.0, 1.0, ALU.mult, ALU.add))
                ch.link(nc.vector.reciprocal(low[:], low[:]))
                ch.link(nc.vector.tensor_scalar(nrm[:], cut[:], 1.0, None, ALU.add))
                nc.vector.tensor_tensor(low[:], low[:], nrm[:], ALU.mult).then_inc(ratio, 1)
                dve.wait_ge(logged, 1)
                nc.vector.scalar_tensor_tensor(lg[:], lg[:], 0.5, plan.inv[:], ALU.mult, ALU.mult).then_inc(argd, 1)
                ch.link(nc.vector.reciprocal(factor[:], cut[:]))
                ch.link(nc.vector.tensor_tensor(factor[:], factor[:], alive[:], ALU.mult))
                dve.wait_ge(thd, 1)
                ch.link(nc.vector.tensor_tensor(factor[:], factor[:], th[:], ALU.mult))
                ch.link(nc.vector.tensor_tensor(y2[:], factor[:], factor[:], ALU.mult))
                ch.link(nc.vector.tensor_tensor(y2[:], y2[:], lengths[:], ALU.mult))
                ch2 = Chain(dve, chain, 10)

                def coefs(c, u):
                    landed(dve, got, c, u)
                    after(dve, dot_done, c)
                    for q in range(J):
                        last = nc.vector.scalar_tensor_tensor(junk3[:, q, :], rows_in[:, u, q, :], 1.0, edges[:, bass.ds((c * J + q + 1) * D, D)],
                                                              ALU.mult, ALU.mult, accum_out=dot[:, u, q:q + 1])
                    last.then_inc(dot_done, 1)
                    dve.wait_ge(dot_done, c + 1)
                    dve.wait_ge(sq_done, c + 1)
                    f, y = factor[:, bass.ds(c * J, J)], y2[:, bass.ds(c * J, J)]
                    ch2.step(c)
                    ch2.link(nc.vector.tensor_tensor(xy[:, u], dot[:, u], f, ALU.mult))
                    ch2.link(nc.vector.tensor_scalar(c1[:, u], xy[:, u], 2.0, 1.0, ALU.mult, ALU.add))
                    ch2.link(nc.vector.tensor_tensor(den[:, u], x2[:, u], y, ALU.mult))
                    ch2.link(nc.vector.tensor_tensor(den[:, u], den[:, u], c1[:, u], ALU.add))
                    ch2.link(nc.vector.tensor_scalar(den[:, u], den[:, u], HYP_EPS, None, ALU.max))
                    ch2.link(nc.vector.reciprocal(den[:, u], den[:, u]))
                    ch2.link(nc.vector.tensor_scalar(be[:, u], x2[:, u], -1.0, 1.0, ALU.mult, ALU.add))
                    ch2.link(nc.vector.tensor_tensor(be[:, u], be[:, u], f, ALU.mult))
                    ch2.link(nc.vector.tensor_tensor(c1[:, u], c1[:, u], y, ALU.add))
                    after(dve, tmp_done, c - R + 1)
                    ch2.link(nc.vector.tensor_tensor(be[:, u], be[:, u], den[:, u], ALU.mult))
                    nc.vector.tensor_tensor(al[:, u], c1[:, u], den[:, u], ALU.mult).then_inc(coef, 1)

                def finish(c, u):
                    dve.wait_ge(tmp_done, c + 1)
                    sent(dve, put, c, u, J)
                    for q in range(J):
                        last = nc.vector.scalar_tensor_tensor(res[:, u, q, :], edges[:, bass.ds((c * J + q + 1) * D, D)], be[:, u, q:q + 1],
                                                              scaled[:, u, q, :], ALU.mult, ALU.add)
                    last.then_inc(res_done, 1)
                each_phases(dve, n, [coefs, finish], R)


def third_norm(nc, k, s, X, H):
    with Stage(nc, "norm3") as st:
        norm = Norm(nc, st, k)
        xin, hin, x3, h3 = (st.sb(v, [P, R, J, D]) for v in ("xin", "hin", "x3", "h3"))
        ld, xs, hs = ([st.sem(f"{v}{i}") for i in range(R)] for v in ("ld", "xs", "hs"))
        x_done, h_done = st.sem("x_done"), st.sem("h_done")
        n = s.chunks
        with st.run() as block:

            @block.sync
            def _(sp):
                def load(c, u):
                    after(sp, x_done, c - R + 1)
                    sp.dma_start(xin[:, u], rows(X, c)).then_inc(ld[u], 16)
                    sp.dma_start(hin[:, u], rows(H, c)).then_inc(ld[u], 16)

                def store(c, u):
                    sp.wait_ge(x_done, c + 1)
                    sp.dma_start(rows(X, c), x3[:, u]).then_inc(xs[u], 16)
                    sp.wait_ge(h_done, c + 1)
                    sp.dma_start(rows(H, c), h3[:, u]).then_inc(hs[u], 16)
                each_phases(sp, n, [load, None, store], R)
                all_landed(sp, xs, n)
                all_landed(sp, hs, n)

            @block.vector
            def _(dve):
                def add(c, u):
                    landed(dve, ld, c, u, 2)
                    sent(dve, xs, c, u)
                    after(dve, h_done, c - R + 1)
                    nc.vector.tensor_tensor(x3[:, u], xin[:, u], hin[:, u], ALU.add).then_inc(x_done, 1)
                    dve.wait_ge(x_done, c + 1)
                    norm.dve_moments(dve, x3[:, u], c, u)
                    norm.dve_coefs(dve, c, u, lambda: after(dve, h_done, c - R + 1))
                each(dve, n, add, R)

            @block.scalar
            def _(act):
                def normed(c, u):
                    norm.act_root(act, c, u)
                    sent(act, hs, c, u)
                    norm.act_apply(act, h3[:, u], x3[:, u], c, u).then_inc(h_done, 1)
                each(act, n, normed, R)


class Ssp:

    def __init__(self, nc, st, k, b, ring):
        self.nc, self.b, self.k, self.ring = nc, b, k, ring
        self.v, self.mag, self.dec, self.log = (st.sb(x, [P, ring, CH]) for x in ("ssp_v", "ssp_mag", "ssp_dec", "ssp_log"))
        self.taken, self.a, self.e, self.logged, self.used = (
            st.sem(x) for x in ("ssp_taken", "ssp_a", "ssp_e", "ssp_logged", "ssp_used"))

    def dve_take(self, dve, psum, c, u):
        after(dve, self.used, c - self.ring + 1)
        after(dve, self.a, c - self.ring + 1)
        self.nc.vector.tensor_scalar(self.v[:, u], psum, self.b[:], None, ALU.add).then_inc(self.taken, 1)

    def act_log(self, act, c, u):
        nc = self.nc
        act.wait_ge(self.taken, c + 1)
        nc.scalar.activation(self.mag[:, u], self.v[:, u], ACT.Abs).then_inc(self.a, 1)
        act.wait_ge(self.a, c + 1)
        nc.scalar.activation(self.dec[:, u], self.mag[:, u], ACT.Exp, scale=-1.0).then_inc(self.e, 1)
        act.wait_ge(self.e, c + 1)
        after(act, self.used, c - self.ring + 1)
        nc.scalar.activation(self.log[:, u], self.dec[:, u], ACT.Ln, bias=self.k.half_col[:], scale=0.5).then_inc(self.logged, 1)

    def dve_result(self, dve, out, c, u):
        dve.wait_ge(self.logged, c + 1)
        self.nc.vector.scalar_tensor_tensor(out, self.v[:, u], 0.0, self.log[:, u], ALU.max, ALU.add).then_inc(self.used, 1)


def filter_messages(nc, k, s, plan, L3, attr_sorted, H, edges, carry):
    T = s.T
    with Stage(nc, "edge3") as st:
        rows_in = st.sb("rows", [P, R, J, D])
        attr_in = st.sb("attr", [P, R, J, D])
        idx = st.sb("idx", [P, R, J], U32)
        aT, hT, msg = (st.sb(v, [P, 2, CH]) for v in ("aT", "hT", "msg"))
        hl = st.sb("hl", [P, R, CH])
        sp_out = st.sb("sp_out", [P, 2, CH])
        cut_rows = st.sb("cut_rows", [P, 2, J, D])
        phase, whole, cosine = st.sb("phase", [P, T]), st.sb("whole", [P, T]), st.sb("cosine", [P, T])
        w1, w2, lin1 = st.sb("w1", [P, D]), st.sb("w2", [P, D]), st.sb("lin1", [P, D])
        b1, b2 = st.sb("b1", [P, 1]), st.sb("b2", [P, 1])
        ssp = Ssp(nc, st, k, b1, R)
        psA = st.ps("psA", [P, CH])
        psH = st.ps("psH", [P, CH])
        psV = st.ps("psV", [P, CH])
        psL = st.ps("psL", [P, CH])
        psW = [st.ps(f"psW{i}", [P, CH]) for i in range(2)]
        psR = [st.ps(f"psR{i}", [P, CH]) for i in range(2)]
        got, attr_got = ([st.sem(f"{x}{i}") for i in range(R)] for x in ("got", "attr_got"))
        weights, padded, idx_ready, tick, A_ps, A_sb, H_sb, V_ps, L_ps, L_sb, W_ps, msg_done, R_ps, R_sb = (
            st.sem(v) for v in ("weights", "padded", "idx_ready", "tick", "A_ps", "A_sb", "H_sb", "V_ps", "L_ps", "L_sb",
                                "W_ps", "msg_done", "R_ps", "R_sb"))
        chain, zeroed, carried, taken, turns, cos_done, sin_done = (
            st.sem(v) for v in ("chain", "zeroed", "carried", "taken", "turns", "cos_done", "sin_done"))
        n = s.echunks
        big = 1.5 * 2.0 ** 23
        with st.run() as block:

            @block.sync
            def _(sp):
                sp.wait_ge(padded, 2)
                for dst, src in ((w1[0:NG, :], L3["mlp_w1"][:, :]), (w2[:], L3["mlp_w2"][:, :]), (lin1[:], L3["lin1_w"][:, :]),
                                 (b1[:], column(L3["mlp_b1"])), (b2[:], column(L3["mlp_b2"]))):
                    sp.dma_start(dst, src).then_inc(weights, 16)

                def load(c, u):
                    after(sp, A_ps, c - R + 1)
                    steps = J // V
                    for i in range(steps):
                        sp.dma_start(attr_in[:, u, i * V:(i + 1) * V, 0:NG],
                                     attr_sorted[bass.ds((c * steps + i) * P, P), :].rearrange("p (v g) -> p v g", v=V)
                                     ).then_inc(attr_got[u], 16)
                each(sp, n, load, R)

            @block.gpsimd
            def _(pool):
                bound = pool.to_reg(s.N - 1)
                pool.memset(w1[:], 0.0).then_inc(padded, 1)
                pool.memset(attr_in[:], 0.0).then_inc(padded, 1)

                def gather(c, u):
                    pool.wait_ge(idx_ready, c + 1)
                    after(pool, A_ps, c - R + 1)
                    pool.sem_inc(tick, 1)
                    for q in range(J):
                        gather_rows(pool, rows_in[:, u, q, :], H, idx[:, u, q:q + 1], bound, got[u])
                each(pool, n, gather, R)

            @block.scalar
            def _(act):
                act.wait_ge(weights, 80)
                act.wait_ge(turns, 1)
                nc.scalar.activation(cosine[:], phase[:], ACT.Sin, scale=2.0 * math.pi).then_inc(sin_done, 1)
                act.preload_act_table_set(EXP_LN_SET)

                def index(c, u):
                    sent(act, got, c, u, J)
                    nc.scalar.copy(idx[:, u, :], plan.other[:, bass.ds(c * J, J)]).then_inc(idx_ready, 1)

                def take_attr(c, u):
                    act.wait_ge(A_ps, c + 1)
                    after(act, V_ps, c - 1)
                    nc.scalar.copy(aT[:, u % 2, :], psA[:]).then_inc(A_sb, 1)

                def take_rows(c, u):
                    act.wait_ge(L_ps, c + 1)
                    after(act, msg_done, c - R + 1)
                    nc.scalar.copy(hl[:, u, :], psL[:]).then_inc(L_sb, 1)
                    ssp.act_log(act, c, u)

                def cutoff(c, u):
                    act.wait_ge(R_ps, c + 1)
                    act.wait_ge(cos_done, 1)
                    after(act, chain, (c - 1) * J)
                    for q in range(J):
                        last = nc.scalar.mul(cut_rows[:, u % 2, q, :], psR[u % 2][:, q * D:(q + 1) * D], cosine[:, bass.ds(c * J + q, 1)])
                    last.then_inc(R_sb, 1)
                each_phases(act, n, [index, None, None, take_attr, take_rows, None, None, cutoff], R)

            @block.vector
            def _(dve):
                ch = Chain(dve, chain, J)
                nc.vector.memset(edges[:, 0:D], 0.0).then_inc(zeroed, 1)
                dve.wait_ge(zeroed, 1)
                nc.vector.tensor_scalar(phase[:], plan.weight[:], 0.5 / CUTOFF, 0.25, ALU.mult, ALU.add).then_inc(zeroed, 1)
                dve.wait_ge(zeroed, 2)
                nc.vector.tensor_scalar(whole[:], phase[:], big, None, ALU.add).then_inc(zeroed, 1)
                dve.wait_ge(zeroed, 3)
                nc.vector.tensor_scalar(whole[:], whole[:], -big, None, ALU.add).then_inc(zeroed, 1)
                dve.wait_ge(zeroed, 4)
                nc.vector.tensor_tensor(phase[:], phase[:], whole[:], ALU.subtract).then_inc(zeroed, 1)
                dve.wait_ge(zeroed, 5)
                nc.vector.tensor_scalar(phase[:], phase[:], 0.4999999, -0.4999999, ALU.min, ALU.max).then_inc(turns, 1)
                dve.wait_ge(sin_done, 1)
                nc.vector.tensor_scalar(cosine[:], cosine[:], 0.5, 0.5, ALU.mult, ALU.add).then_inc(cos_done, 1)
                dve.wait_ge(weights, 80)

                def take(c, u):
                    dve.wait_ge(A_ps, c + 1)
                    after(dve, L_ps, c - 1)
                    nc.vector.tensor_copy(hT[:, u % 2, :], psH[:]).then_inc(H_sb, 1)

                def soft_in(c, u):
                    dve.wait_ge(V_ps, c + 1)
                    ssp.dve_take(dve, psV[:], c, u)

                def soft_out(c, u):
                    after(dve, W_ps, c - 1)
                    ssp.dve_result(dve, sp_out[:, u % 2, :], c, u)

                def product(c, u):
                    dve.wait_ge(W_ps, c + 1)
                    dve.wait_ge(L_sb, c + 1)
                    after(dve, R_ps, c - 1)
                    nc.vector.scalar_tensor_tensor(msg[:, u % 2, :], psW[u % 2][:], b2[:], hl[:, u, :], ALU.add, ALU.mult).then_inc(msg_done, 1)

                def add(c, u):
                    dve.wait_ge(R_sb, c + 1)
                    ch.step(c)
                    for q in range(J):
                        ch.link(nc.vector.scalar_tensor_tensor(
                            edges[:, bass.ds((c * J + q + 1) * D, D)], edges[:, bass.ds((c * J + q) * D, D)],
                            plan.same[:, bass.ds(c * J + q, 1)], cut_rows[:, u % 2, q, :], ALU.mult, ALU.add))
                each_phases(dve, n, [take, soft_in, soft_out, product, None, add], R)
                dve.wait_ge(carried, 1)
                nc.vector.tensor_copy(carry[:], psA[:, 0:D]).then_inc(taken, 1)
                dve.wait_ge(taken, 1)

            @block.tensor
            def _(pe):
                pe.wait_ge(weights, 80)

                def turn(c, u):
                    landed(pe, got, c, u, J)
                    landed(pe, attr_got, c, u, J // V)
                    after(pe, A_sb, c)
                    after(pe, H_sb, c)
                    for q in range(J):
                        nc.tensor.transpose(psA[:, q * P:(q + 1) * P], attr_in[:, u, q, :], k.ident[:])
                    for q in range(J):
                        last = nc.tensor.transpose(psH[:, q * P:(q + 1) * P], rows_in[:, u, q, :], k.ident[:])
                    last.then_inc(A_ps, 1)

                def project(c, u):
                    pe.wait_ge(A_sb, c + 1)
                    after(pe, ssp.taken, c)
                    nc.tensor.matmul(psV[:], w1[:], aT[:, u % 2, :], start=True, stop=True).then_inc(V_ps, 1)
                    pe.wait_ge(H_sb, c + 1)
                    after(pe, L_sb, c)
                    nc.tensor.matmul(psL[:], lin1[:], hT[:, u % 2, :], start=True, stop=True).then_inc(L_ps, 1)

                def filt(c, u):
                    pe.wait_ge(ssp.used, c + 1)
                    after(pe, msg_done, c - 1)
                    nc.tensor.matmul(psW[u % 2][:], w2[:], sp_out[:, u % 2, :], start=True, stop=True).then_inc(W_ps, 1)

                def back(c, u):
                    pe.wait_ge(msg_done, c + 1)
                    after(pe, R_sb, c - 1)
                    for q in range(J):
                        last = nc.tensor.transpose(psR[u % 2][:, q * D:(q + 1) * D], msg[:, u % 2, q * P:(q + 1) * P], k.ident[:])
                    last.then_inc(R_ps, 1)
                each_phases(pe, n, [turn, project, filt, back], R)
                pe.wait_ge(chain, n * J)
                nc.tensor.matmul(psA[:, 0:D], plan.carry[:], edges[:, s.T * D:], start=True, stop=True).then_inc(carried, 1)


def last_update(nc, k, s, L3, X, S, out):
    with Stage(nc, "node3") as st:
        xin, sin, y = (st.sb(v, [P, R, J, D]) for v in ("xin", "sin", "y"))
        sT, a_sb = st.sb("sT", [P, R, CH]), st.sb("a", [P, R, CH])
        w1, w2, b1 = st.sb("w1", [P, D]), st.sb("w2", [P, D]), st.sb("b1", [P, 1])
        bias = st.sb("bias", [1, J, D])
        ssp = Ssp(nc, st, k, b1, R)
        psT = [st.ps(f"psT{i}", [P, CH]) for i in range(2)]
        psA = [st.ps(f"psA{i}", [P, CH]) for i in range(2)]
        psB = [st.ps(f"psB{i}", [P, CH]) for i in range(2)]
        xl, sl, ys = ([st.sem(f"{v}{i}") for i in range(R)] for v in ("xl", "sl", "ys"))
        weights, T_ps, T_sb, A_ps, B_ps, y_done = (
            st.sem(v) for v in ("weights", "T_ps", "T_sb", "A_ps", "B_ps", "y_done"))
        n = s.chunks
        with st.run() as block:

            @block.sync
            def _(sp):
                for j in range(J):
                    sp.dma_start(bias[:, j, :], row(L3["lin_b"])).then_inc(weights, 16)
                sp.dma_start(w1[:], L3["lin2_w"][:, :]).then_inc(weights, 16)
                sp.dma_start(w2[:], L3["lin_w"][:, :]).then_inc(weights, 16)
                sp.dma_start(b1[:], column(L3["lin2_b"])).then_inc(weights, 16)

                def load(c, u):
                    after(sp, T_ps, c - R + 1)
                    sp.dma_start(sin[:, u], rows(S, c)).then_inc(sl[u], 16)

                def load2(c, u):
                    after(sp, y_done, c - R + 1)
                    sp.dma_start(xin[:, u], rows(X, c)).then_inc(xl[u], 16)

                def store(c, u):
                    sp.wait_ge(y_done, c + 1)
                    if isinstance(c, int) and c == n - 1:
                        sp.dma_start(out[c * CH:s.N, :].rearrange("(p j) d -> p j d", j=J), y[0:s.tp, u]).then_inc(ys[u], 16)
                    else:
                        sp.dma_start(rows(out, c), y[:, u]).then_inc(ys[u], 16)
                each_phases(sp, n, [load, (3, load2), (7, store)], R)
                all_landed(sp, ys, n)

            @block.tensor
            def _(pe):
                pe.wait_ge(weights, 16 * (J + 3))

                def turn(c, u):
                    landed(pe, sl, c, u)
                    after(pe, T_sb, c - 1)
                    for j in range(J):
                        last = nc.tensor.transpose(psT[u % 2][:, j * P:(j + 1) * P], sin[:, u, j, :], k.ident[:])
                    last.then_inc(T_ps, 1)

                def up(c, u):
                    pe.wait_ge(T_sb, c + 1)
                    after(pe, ssp.taken, c - 1)
                    nc.tensor.matmul(psA[u % 2][:], w1[:], sT[:, u, :], start=True, stop=True).then_inc(A_ps, 1)

                def down(c, u):
                    pe.wait_ge(ssp.used, c + 1)
                    after(pe, y_done, c - 1)
                    rows_product(nc, psB[u % 2], a_sb[:, u], w2, bias[:].rearrange("a j d -> a (j d)"), k).then_inc(B_ps, 1)
                each_phases(pe, n, [turn, up, (4, down)], R)

            @block.scalar
            def _(act):
                act.preload_act_table_set(EXP_LN_SET)
                act.wait_ge(weights, 16 * (J + 3))

                def take(c, u):
                    act.wait_ge(T_ps, c + 1)
                    after(act, A_ps, c - R + 1)
                    nc.scalar.copy(sT[:, u, :], psT[u % 2][:]).then_inc(T_sb, 1)

                def soft(c, u):
                    ssp.act_log(act, c, u)
                each_phases(act, n, [take, (3, soft)], R)

            @block.vector
            def _(dve):
                dve.wait_ge(weights, 16 * (J + 3))

                def take(c, u):
                    dve.wait_ge(A_ps, c + 1)
                    ssp.dve_take(dve, psA[u % 2][:], c, u)

                def result(c, u):
                    after(dve, B_ps, c - R + 1)
                    ssp.dve_result(dve, a_sb[:, u, :], c, u)

                def finish(c, u):
                    dve.wait_ge(B_ps, c + 1)
                    landed(dve, xl, c, u)
                    sent(dve, ys, c, u)
                    nc.vector.tensor_tensor(y[:, u].rearrange("p j d -> p (j d)"), psB[u % 2][:],
                                            xin[:, u].rearrange("p j d -> p (j d)"), ALU.add).then_inc(y_done, 1)
                each_phases(dve, n, [(4, result), (2, take), (5, finish)], R)


def program(nc, a, t):
    s = Shapes(a["x"].shape[0], a["src"].shape[0])
    L0 = {n[7:]: v for n, v in a.items() if n.startswith("L0_gnn_")}
    with ExitStack() as stack:
        k = Constants(stack, nc)
        make_constants(nc, k)
        first_norm(nc, k, s, a["x"], L0["wv"], L0["bv"], L0["wo"], L0["bo"], t["H"], t["Y"])
        src_plan = Plan(stack, nc, s, "src")
        edges = stack.enter_context(nc.sbuf_tensor("edges", [P, (s.T + 1) * D], F32))
        carry = stack.enter_context(nc.sbuf_tensor("carry", [P, D], F32))
        sort_edges(nc, k, s, a["src"], a["dst"], a["edge_weight"], t["rec_src"])
        edge_plan(nc, k, s, t["rec_src"], src_plan)
        sum_neighbours(nc, k, s, src_plan, t["H"], edges, carry)
        attend(nc, k, s, src_plan, L0, t["H"], t["Y"], edges, carry)
        coefs = [stack.enter_context(nc.sbuf_tensor(f"bn_{x}", [P, 1], F32)) for x in ("scale1", "offset1", "scale2", "offset2")]
        node_moments(nc, k, s, t["Y"], L0["g1"], L0["be1"], coefs[0], coefs[1])
        node_mlp(nc, k, s, L0, t["Y"], t["U"], *coefs)
        second_norm(nc, k, s, a["x"], t["U"], t["X"], t["H"], coefs[2], coefs[3])
        L1 = {n[7:]: v for n, v in a.items() if n.startswith("L1_gnn_")}
        dst_plan = Plan(stack, nc, s, "dst")
        sort_edges(nc, k, s, a["dst"], a["src"], a["edge_weight"], t["rec_dst"], t["S"])
        edge_plan(nc, k, s, t["rec_dst"], dst_plan)
        edge_messages(nc, k, s, dst_plan, L1, t["H"], edges, carry)
        scatter_sums(nc, s, dst_plan, t["S"], edges, carry, "scatter1")
        node_update(nc, k, s, L1, t["X"], t["H"], t["S"])
        L3 = {n[7:]: v for n, v in a.items() if n.startswith("L3_gnn_")}
        norms = stack.enter_context(nc.sbuf_tensor("norms", [P, s.T], F32))
        lengths = stack.enter_context(nc.sbuf_tensor("lengths", [P, s.T], F32))
        hyperbolic_messages(nc, k, s, dst_plan, t["H"], edges, norms, t["Y"])
        hyperbolic_fold(nc, k, s, dst_plan, edges, norms, lengths, a["edge_attr_50"], t["attr"])
        hyperbolic_results(nc, k, s, dst_plan, t["H"], edges, lengths, t["Y"])
        third_norm(nc, k, s, t["X"], t["H"])
        filter_messages(nc, k, s, dst_plan, L3, t["attr"], t["H"], edges, carry)
        scatter_sums(nc, s, dst_plan, t["S"], edges, carry, "scatter3")
        last_update(nc, k, s, L3, t["X"], t["S"], t["out"])


def tables(nc, s):
    def dram(name, shape):
        return nc.dram_tensor(name, shape, F32, kind="Internal").ap()
    return {"H": dram("normed", (s.NP, D)), "Y": dram("attended", (s.NP, D)), "U": dram("mlp_out", (s.chunks * P, CH)),
            "X": dram("stream", (s.NP, D)), "S": dram("sums", (s.NP, D)),
            "attr": dram("attr_sorted", (s.EP // V, V * NG)),
            "rec_src": dram("rec_src", (s.EP, REC)), "rec_dst": dram("rec_dst", (s.EP, REC))}


def kernel(**inputs):
    import numpy as np
    from concourse import bacc
    from concourse.bass_utils import run_bass_kernel_spmd

    nc = bacc.Bacc("TRN2", target_bir_lowering=False, num_devices=1)
    arrays, a = {}, {}
    for name, value in inputs.items():
        arrays[f"in_{name}"] = np.ascontiguousarray(value)
        a[name] = nc.dram_tensor(f"in_{name}", arrays[f"in_{name}"].shape, mybir.dt.from_np(arrays[f"in_{name}"].dtype),
                                 kind="ExternalInput").ap()
    a["out"] = nc.dram_tensor("out", inputs["x"].shape, F32, kind="ExternalOutput").ap()
    t = tables(nc, Shapes(inputs["x"].shape[0], inputs["src"].shape[0]))
    t["out"] = a["out"]
    program(nc, a, t)
    r = run_bass_kernel_spmd(nc, [arrays], core_ids=[0])
    return r.results[0]["out"]
```
